# Optimizing a Trainium2 kernel written in Bass

```python
import numpy as np
import jax
import jax.numpy as jnp

def _softmax(x, axis=-1):
    return jax.nn.softmax(x, axis=axis)

def _gelu(x):
    return jax.nn.gelu(x, approximate=True)

def _silu(x):
    return jax.nn.silu(x)

def _sigmoid(x):
    return jax.nn.sigmoid(x)

def _layernorm(x, axis=-1, eps=1e-05):
    m = jnp.mean(x, axis=axis, keepdims=True)
    v = jnp.var(x, axis=axis, keepdims=True)
    return (x - m) / jnp.sqrt(v + eps)

def _scatter_add(tgt, idx, src, axis=0):
    return tgt.at[idx].add(src)

def _segment_sum(src, seg, n):
    return jax.ops.segment_sum(src, seg, n)
kernel_name = 'mk_xattn_ffn_d4_seqx_r8_284a3c'

def setup_inputs(seed: int=0):
    np.random.seed(seed)
    _w = jnp.asarray

    def _rec_inputs():
        import jax
        import jax.numpy as jnp
        _rk = jax.random.key(seed)
        x = -0.0002928 + 1 * jax.random.normal(jax.random.fold_in(_rk, 1), (16, 256, 128), jnp.float32)
        _lenS = 256 - jax.random.randint(jax.random.fold_in(_rk, 7), (16,), 0, max(1, 256 // 4) + 1, jnp.int32)
        _lenS2 = 64 - jax.random.randint(jax.random.fold_in(_rk, 8), (16,), 0, max(1, 64 // 4) + 1, jnp.int32)
        _ctx_512P = jax.random.normal(jax.random.fold_in(_rk, 11), (16, 16, 64), jnp.float32)
        _ctx_512c = jax.random.dirichlet(jax.random.fold_in(_rk, 511), 0.3 * jnp.ones((16,), jnp.float32), (16, 64))
        _ctx_512t = jnp.einsum('bsk,bkd->bsd', _ctx_512c, _ctx_512P)
        _ctx_512t = _ctx_512t * jax.lax.rsqrt(jnp.mean(jnp.square(_ctx_512t)) + 1e-12) * 0.953939
        ctx_512 = 0.00222621 + 0.99962 * (_ctx_512t + 0.3 * jax.random.normal(jax.random.fold_in(_rk, 611), (16, 64, 64), jnp.float32))
        return (x, ctx_512)
    x, ctx_512 = _rec_inputs()

    def _L0_xattn_setup():
        import jax, jax.numpy as jnp
        import numpy as np
        B, T, TC, C, CC, H = (2, 256, 64, 128, 64, 16)
        D = C // H

        def _heads(t):
            b, l, _ = t.shape
            return t.reshape(b, l, H, D).transpose(0, 2, 1, 3)
        key = jax.random.key(seed)
        ks = jax.random.split(key, 18)
        w = lambda k, i, o: jax.random.normal(k, (i, o), jnp.float32) / np.sqrt(i).astype(np.float32)
        return {'x': jax.random.normal(ks[0], (B, T, C), jnp.float32), 'cross_input': jax.random.normal(ks[1], (B, TC, CC), jnp.float32), 'Wk': w(ks[2], C, C), 'bk': jnp.zeros((C,), jnp.float32), 'Wq': w(ks[3], C, C), 'bq': jnp.zeros((C,), jnp.float32), 'Wv': w(ks[4], C, C), 'bv': jnp.zeros((C,), jnp.float32), 'Wck': w(ks[5], CC, C), 'bck': jnp.zeros((C,), jnp.float32), 'Wcq': w(ks[6], C, C), 'bcq': jnp.zeros((C,), jnp.float32), 'Wcv': w(ks[7], CC, C), 'bcv': jnp.zeros((C,), jnp.float32), 'Wp': w(ks[8], C, C), 'bp': jnp.zeros((C,), jnp.float32)}
    _L0_xattn_all = _L0_xattn_setup()
    _L0_xattn_in = {k: v for k, v in _L0_xattn_all.items() if k in ('Wk', 'bk', 'Wq', 'bq', 'Wv', 'bv', 'Wck', 'bck', 'Wcq', 'bcq', 'Wcv', 'bcv', 'Wp', 'bp')}
    del _L0_xattn_all

    def _L0_ffn_setup():
        import jax, jax.numpy as jnp
        import numpy as np
        DIM = 128
        HID = 64
        N_EXPERTS = 16
        TOP_K = 4
        key = jax.random.key(seed)
        ks = jax.random.split(key, 8)
        s = 0.02
        x = jax.random.normal(ks[0], (2, 128, DIM), dtype=jnp.float32)
        gate_w = jax.random.normal(ks[1], (N_EXPERTS, DIM), dtype=jnp.float32) * s
        w1 = jax.random.normal(ks[2], (N_EXPERTS, HID, DIM), dtype=jnp.float32) * s
        w3 = jax.random.normal(ks[3], (N_EXPERTS, HID, DIM), dtype=jnp.float32) * s
        w2 = jax.random.normal(ks[4], (N_EXPERTS, DIM, HID), dtype=jnp.float32) * s
        sw1 = jax.random.normal(ks[5], (HID, DIM), dtype=jnp.float32) * s
        sw3 = jax.random.normal(ks[6], (HID, DIM), dtype=jnp.float32) * s
        sw2 = jax.random.normal(ks[7], (DIM, HID), dtype=jnp.float32) * s
        return {'x': x, 'gate_w': gate_w, 'w1': w1, 'w3': w3, 'w2': w2, 'sw1': sw1, 'sw3': sw3, 'sw2': sw2}
    _L0_ffn_all = _L0_ffn_setup()
    _L0_ffn_in = {k: v for k, v in _L0_ffn_all.items() if k in ('gate_w', 'w1', 'w3', 'w2', 'sw1', 'sw3', 'sw2')}
    del _L0_ffn_all

    def _L1_xattn_setup():
        import jax, jax.numpy as jnp
        import numpy as np
        H, D, C1, C2, S, M, B, W = (16, 32, 128, 64, 256, 64, 2, 4)

        def _ln(x, g, b):
            m = jnp.mean(x, -1, keepdims=True)
            v = jnp.var(x, -1, keepdims=True)
            return (x - m) * jax.lax.rsqrt(v + 1e-05) * g + b

        def _mha(x, y, wq, wk, wv, li1_w, li1_b, lnx_g, lnx_b, lny_g, lny_b, ln3_g, ln3_b, li2_w, li2_b, li3_w, li3_b, causal):
            xn = _ln(x, lnx_g, lnx_b)
            yn = _ln(y, lny_g, lny_b)
            q = jnp.einsum('bsc,hcd->bhsd', xn, wq)
            k = jnp.einsum('btc,hcd->bhtd', yn, wk)
            v = jnp.einsum('btc,hcd->bhtd', yn, wv)
            a = jax.nn.softmax(jnp.einsum('bhsd,bhtd->bhst', q, k) * D ** (-0.5), axis=-1)
            if causal:
                s, t = (a.shape[-2], a.shape[-1])
                mask = (jnp.arange(t)[None, :] > jnp.arange(s)[:, None]).astype(a.dtype)
                a = a * mask
            o = jnp.einsum('bhst,bhtd->bhsd', a, v)
            o = o.transpose(0, 2, 1, 3).reshape(x.shape[0], x.shape[1], H * D)
            x_out = x + o @ li1_w + li1_b
            h = jax.nn.gelu(_ln(x_out, ln3_g, ln3_b) @ li2_w + li2_b, approximate=False)
            return x_out + h @ li3_w + li3_b
        key = jax.random.key(seed)
        ks = iter(jax.random.split(key, 64))

        def w(shape, scale=0.02):
            return jax.random.normal(next(ks), shape, jnp.float32) * scale
        inp = {'xx': jax.random.normal(next(ks), (B, S, C1), jnp.float32), 'ee': jax.random.normal(next(ks), (B, M, C2), jnp.float32), 'ln1_g': jnp.ones(C1, jnp.float32), 'ln1_b': jnp.zeros(C1, jnp.float32), 'ln2_g': jnp.ones(C1, jnp.float32), 'ln2_b': jnp.zeros(C1, jnp.float32)}
        for pfx, cy in (('a1', C1), ('a2', C2)):
            inp[pfx + '_wq'] = w((H, C1, D))
            inp[pfx + '_wk'] = w((H, cy, D))
            inp[pfx + '_wv'] = w((H, cy, D))
            inp[pfx + '_li1_w'] = w((H * D, C1))
            inp[pfx + '_li1_b'] = jnp.zeros(C1, jnp.float32)
            inp[pfx + '_lnx_g'] = jnp.ones(C1, jnp.float32)
            inp[pfx + '_lnx_b'] = jnp.zeros(C1, jnp.float32)
            inp[pfx + '_lny_g'] = jnp.ones(cy, jnp.float32)
            inp[pfx + '_lny_b'] = jnp.zeros(cy, jnp.float32)
            inp[pfx + '_ln3_g'] = jnp.ones(C1, jnp.float32)
            inp[pfx + '_ln3_b'] = jnp.zeros(C1, jnp.float32)
            inp[pfx + '_li2_w'] = w((C1, C1 * W))
            inp[pfx + '_li2_b'] = jnp.zeros(C1 * W, jnp.float32)
            inp[pfx + '_li3_w'] = w((C1 * W, C1))
            inp[pfx + '_li3_b'] = jnp.zeros(C1, jnp.float32)
        inp['training'] = 0
        return inp
    _L1_xattn_all = _L1_xattn_setup()
    _L1_xattn_in = {k: v for k, v in _L1_xattn_all.items() if k in ('ln1_g', 'ln1_b', 'ln2_g', 'ln2_b', 'a1_wq', 'a1_wk', 'a1_wv', 'a1_li1_w', 'a1_li1_b', 'a1_lnx_g', 'a1_lnx_b', 'a1_lny_g', 'a1_lny_b', 'a1_ln3_g', 'a1_ln3_b', 'a1_li2_w', 'a1_li2_b', 'a1_li3_w', 'a1_li3_b', 'a2_wq', 'a2_wk', 'a2_wv', 'a2_li1_w', 'a2_li1_b', 'a2_lnx_g', 'a2_lnx_b', 'a2_lny_g', 'a2_lny_b', 'a2_ln3_g', 'a2_ln3_b', 'a2_li2_w', 'a2_li2_b', 'a2_li3_w', 'a2_li3_b')}
    del _L1_xattn_all

    def _L1_ffn_setup():
        import jax, jax.numpy as jnp
        import numpy as np
        EPS = 1e-05

        def _quantize(W):
            gamma = jnp.mean(jnp.abs(W))
            return jnp.clip(jnp.round(W / (gamma + EPS)), -1.0, 1.0)
        key = jax.random.key(seed)
        k_x, k_w1, k_b1, k_w2, k_b2 = jax.random.split(key, 5)
        n_embd = 128
        d_ff = 4 * n_embd
        B, S = (4, 512)
        bound1 = 1.0 / np.sqrt(n_embd)
        bound2 = 1.0 / np.sqrt(d_ff)
        x = jax.random.normal(k_x, (B, S, n_embd), dtype=jnp.float32)
        W1 = jax.random.uniform(k_w1, (d_ff, n_embd), jnp.float32, -bound1, bound1)
        b1 = jax.random.uniform(k_b1, (d_ff,), jnp.float32, -bound1, bound1)
        W2 = jax.random.uniform(k_w2, (n_embd, d_ff), jnp.float32, -bound2, bound2)
        b2 = jax.random.uniform(k_b2, (n_embd,), jnp.float32, -bound2, bound2)
        return {'x': x, 'W1': W1, 'b1': b1, 'W2': W2, 'b2': b2}
    _L1_ffn_all = _L1_ffn_setup()
    _L1_ffn_in = {k: v for k, v in _L1_ffn_all.items() if k in ('W1', 'b1', 'W2', 'b2')}
    del _L1_ffn_all

    def _L2_xattn_setup():
        import jax, jax.numpy as jnp
        import numpy as np
        DIM = 128
        LATENT_DIM = 64
        NUM_HEADS = 16
        HEAD_DIM = DIM // NUM_HEADS
        SCALE = HEAD_DIM ** (-0.5)
        key = jax.random.key(seed)
        k1, k2, k3, k4, k5 = jax.random.split(key, 5)
        B, xN, zN = (2, 256, 256)
        x = jax.random.normal(k1, (B, xN, DIM), dtype=jnp.float32)
        z = jax.random.normal(k2, (B, zN, LATENT_DIM), dtype=jnp.float32)
        Wq = jax.random.normal(k3, (DIM, DIM), dtype=jnp.float32) * DIM ** (-0.5)
        Wkv = jax.random.normal(k4, (2 * DIM, LATENT_DIM), dtype=jnp.float32) * LATENT_DIM ** (-0.5)
        Wo = jax.random.normal(k5, (DIM, DIM), dtype=jnp.float32) * DIM ** (-0.5)
        return {'x': x, 'z': z, 'Wq': Wq, 'Wkv': Wkv, 'Wo': Wo}
    _L2_xattn_all = _L2_xattn_setup()
    _L2_xattn_in = {k: v for k, v in _L2_xattn_all.items() if k in ('Wq', 'Wkv', 'Wo')}
    del _L2_xattn_all

    def _L2_ffn_setup():
        import jax, jax.numpy as jnp
        import numpy as np
        LN_EPS = 1e-05

        def layernorm(x, g, b):
            mu = jnp.mean(x, axis=-1, keepdims=True)
            var = jnp.mean((x - mu) ** 2, axis=-1, keepdims=True)
            return (x - mu) * jax.lax.rsqrt(var + LN_EPS) * g + b

        def act_quant_fake(x):
            scale = 127.0 / jnp.clip(jnp.max(jnp.abs(x), axis=-1, keepdims=True), 1e-05)
            return jnp.clip(jnp.round(x * scale), -128.0, 127.0) / scale

        def weight_quant_fake(w):
            scale = 1.0 / jnp.clip(jnp.mean(jnp.abs(w)), 1e-05)
            return jnp.clip(jnp.round(w * scale), -1.0, 1.0) / scale

        def bitlinear(x, w, b):
            dqx = act_quant_fake(x)
            dqw = weight_quant_fake(w)
            return jnp.einsum('btd,hd->bth', dqx, dqw) + b
        key = jax.random.key(seed)
        ks = jax.random.split(key, 5)
        B, T, D, H = (8, 512, 128, 512)
        return {'x': jax.random.normal(ks[0], (B, T, D), dtype=jnp.float32), 'ln1_g': jnp.ones((D,), jnp.float32), 'ln1_b': jnp.zeros((D,), jnp.float32), 'w1': jax.random.normal(ks[1], (H, D), dtype=jnp.float32) * (1.0 / np.sqrt(D)), 'b1': jax.random.normal(ks[2], (H,), dtype=jnp.float32) * 0.02, 'ln2_g': jnp.ones((H,), jnp.float32), 'ln2_b': jnp.zeros((H,), jnp.float32), 'w2': jax.random.normal(ks[3], (D, H), dtype=jnp.float32) * (1.0 / np.sqrt(H)), 'b2': jax.random.normal(ks[4], (D,), jnp.float32) * 0.02}
    _L2_ffn_all = _L2_ffn_setup()
    _L2_ffn_in = {k: v for k, v in _L2_ffn_all.items() if k in ('ln1_g', 'ln1_b', 'w1', 'b1', 'ln2_g', 'ln2_b', 'w2', 'b2')}
    del _L2_ffn_all

    def _L3_xattn_setup():
        import jax, jax.numpy as jnp
        import numpy as np
        NUM_HEADS = 16
        HEAD_DIM = 64
        Q_DIM = 128
        KV_DIM = 64
        INNER = NUM_HEADS * HEAD_DIM
        key = jax.random.key(seed)
        ks = jax.random.split(key, 7)
        B, N, M = (32, 128, 256)
        q = jax.random.normal(ks[0], (B, N, Q_DIM), dtype=jnp.float32)
        kv = jax.random.normal(ks[1], (B, M, KV_DIM), dtype=jnp.float32)
        Wq = jax.random.normal(ks[2], (Q_DIM, INNER), dtype=jnp.float32) / np.sqrt(Q_DIM)
        Wk = jax.random.normal(ks[3], (KV_DIM, INNER), dtype=jnp.float32) / np.sqrt(KV_DIM)
        Wv = jax.random.normal(ks[4], (KV_DIM, INNER), dtype=jnp.float32) / np.sqrt(KV_DIM)
        Wo = jax.random.normal(ks[5], (INNER, Q_DIM), dtype=jnp.float32) / np.sqrt(INNER)
        bo = jax.random.normal(ks[6], (Q_DIM,), dtype=jnp.float32) * 0.01
        return {'q': q, 'kv': kv, 'Wq': Wq, 'Wk': Wk, 'Wv': Wv, 'Wo': Wo, 'bo': bo}
    _L3_xattn_all = _L3_xattn_setup()
    _L3_xattn_in = {k: v for k, v in _L3_xattn_all.items() if k in ('Wq', 'Wk', 'Wv', 'Wo', 'bo')}
    del _L3_xattn_all

    def _L3_ffn_setup():
        import jax, jax.numpy as jnp
        import numpy as np
        K_TOP = 2
        key = jax.random.key(seed)
        k1, k2, k3 = jax.random.split(key, 3)
        B, S, H, E = (4, 256, 128, 8)
        hidden_states = jax.random.normal(k1, (B, S, H), dtype=jnp.float32)
        router_w = jax.random.normal(k2, (E, H), dtype=jnp.float32) * 0.02
        expert_weights = jax.random.normal(k3, (E, H, H), dtype=jnp.float32) * 0.02
        return {'hidden_states': hidden_states, 'router_w': router_w, 'expert_weights': expert_weights}
    _L3_ffn_all = _L3_ffn_setup()
    _L3_ffn_in = {k: v for k, v in _L3_ffn_all.items() if k in ('router_w', 'expert_weights')}
    del _L3_ffn_all
    return {'x': x, 'ctx_512': ctx_512, 'L0_xattn_Wk': _L0_xattn_in['Wk'], 'L0_xattn_bk': _L0_xattn_in['bk'], 'L0_xattn_Wq': _L0_xattn_in['Wq'], 'L0_xattn_bq': _L0_xattn_in['bq'], 'L0_xattn_Wv': _L0_xattn_in['Wv'], 'L0_xattn_bv': _L0_xattn_in['bv'], 'L0_xattn_Wck': _L0_xattn_in['Wck'], 'L0_xattn_bck': _L0_xattn_in['bck'], 'L0_xattn_Wcq': _L0_xattn_in['Wcq'], 'L0_xattn_bcq': _L0_xattn_in['bcq'], 'L0_xattn_Wcv': _L0_xattn_in['Wcv'], 'L0_xattn_bcv': _L0_xattn_in['bcv'], 'L0_xattn_Wp': _L0_xattn_in['Wp'], 'L0_xattn_bp': _L0_xattn_in['bp'], 'L0_ffn_gate_w': _L0_ffn_in['gate_w'], 'L0_ffn_w1': _L0_ffn_in['w1'], 'L0_ffn_w3': _L0_ffn_in['w3'], 'L0_ffn_w2': _L0_ffn_in['w2'], 'L0_ffn_sw1': _L0_ffn_in['sw1'], 'L0_ffn_sw3': _L0_ffn_in['sw3'], 'L0_ffn_sw2': _L0_ffn_in['sw2'], 'L1_xattn_ln1_g': _L1_xattn_in['ln1_g'], 'L1_xattn_ln1_b': _L1_xattn_in['ln1_b'], 'L1_xattn_ln2_g': _L1_xattn_in['ln2_g'], 'L1_xattn_ln2_b': _L1_xattn_in['ln2_b'], 'L1_xattn_a1_wq': _L1_xattn_in['a1_wq'], 'L1_xattn_a1_wk': _L1_xattn_in['a1_wk'], 'L1_xattn_a1_wv': _L1_xattn_in['a1_wv'], 'L1_xattn_a1_li1_w': _L1_xattn_in['a1_li1_w'], 'L1_xattn_a1_li1_b': _L1_xattn_in['a1_li1_b'], 'L1_xattn_a1_lnx_g': _L1_xattn_in['a1_lnx_g'], 'L1_xattn_a1_lnx_b': _L1_xattn_in['a1_lnx_b'], 'L1_xattn_a1_lny_g': _L1_xattn_in['a1_lny_g'], 'L1_xattn_a1_lny_b': _L1_xattn_in['a1_lny_b'], 'L1_xattn_a1_ln3_g': _L1_xattn_in['a1_ln3_g'], 'L1_xattn_a1_ln3_b': _L1_xattn_in['a1_ln3_b'], 'L1_xattn_a1_li2_w': _L1_xattn_in['a1_li2_w'], 'L1_xattn_a1_li2_b': _L1_xattn_in['a1_li2_b'], 'L1_xattn_a1_li3_w': _L1_xattn_in['a1_li3_w'], 'L1_xattn_a1_li3_b': _L1_xattn_in['a1_li3_b'], 'L1_xattn_a2_wq': _L1_xattn_in['a2_wq'], 'L1_xattn_a2_wk': _L1_xattn_in['a2_wk'], 'L1_xattn_a2_wv': _L1_xattn_in['a2_wv'], 'L1_xattn_a2_li1_w': _L1_xattn_in['a2_li1_w'], 'L1_xattn_a2_li1_b': _L1_xattn_in['a2_li1_b'], 'L1_xattn_a2_lnx_g': _L1_xattn_in['a2_lnx_g'], 'L1_xattn_a2_lnx_b': _L1_xattn_in['a2_lnx_b'], 'L1_xattn_a2_lny_g': _L1_xattn_in['a2_lny_g'], 'L1_xattn_a2_lny_b': _L1_xattn_in['a2_lny_b'], 'L1_xattn_a2_ln3_g': _L1_xattn_in['a2_ln3_g'], 'L1_xattn_a2_ln3_b': _L1_xattn_in['a2_ln3_b'], 'L1_xattn_a2_li2_w': _L1_xattn_in['a2_li2_w'], 'L1_xattn_a2_li2_b': _L1_xattn_in['a2_li2_b'], 'L1_xattn_a2_li3_w': _L1_xattn_in['a2_li3_w'], 'L1_xattn_a2_li3_b': _L1_xattn_in['a2_li3_b'], 'L1_ffn_W1': _L1_ffn_in['W1'], 'L1_ffn_b1': _L1_ffn_in['b1'], 'L1_ffn_W2': _L1_ffn_in['W2'], 'L1_ffn_b2': _L1_ffn_in['b2'], 'L2_xattn_Wq': _L2_xattn_in['Wq'], 'L2_xattn_Wkv': _L2_xattn_in['Wkv'], 'L2_xattn_Wo': _L2_xattn_in['Wo'], 'L2_ffn_ln1_g': _L2_ffn_in['ln1_g'], 'L2_ffn_ln1_b': _L2_ffn_in['ln1_b'], 'L2_ffn_w1': _L2_ffn_in['w1'], 'L2_ffn_b1': _L2_ffn_in['b1'], 'L2_ffn_ln2_g': _L2_ffn_in['ln2_g'], 'L2_ffn_ln2_b': _L2_ffn_in['ln2_b'], 'L2_ffn_w2': _L2_ffn_in['w2'], 'L2_ffn_b2': _L2_ffn_in['b2'], 'L3_xattn_Wq': _L3_xattn_in['Wq'], 'L3_xattn_Wk': _L3_xattn_in['Wk'], 'L3_xattn_Wv': _L3_xattn_in['Wv'], 'L3_xattn_Wo': _L3_xattn_in['Wo'], 'L3_xattn_bo': _L3_xattn_in['bo'], 'L3_ffn_router_w': _L3_ffn_in['router_w'], 'L3_ffn_expert_weights': _L3_ffn_in['expert_weights']}

def reference(x, ctx_512, L0_xattn_Wk, L0_xattn_bk, L0_xattn_Wq, L0_xattn_bq, L0_xattn_Wv, L0_xattn_bv, L0_xattn_Wck, L0_xattn_bck, L0_xattn_Wcq, L0_xattn_bcq, L0_xattn_Wcv, L0_xattn_bcv, L0_xattn_Wp, L0_xattn_bp, L0_ffn_gate_w, L0_ffn_w1, L0_ffn_w3, L0_ffn_w2, L0_ffn_sw1, L0_ffn_sw3, L0_ffn_sw2, L1_xattn_ln1_g, L1_xattn_ln1_b, L1_xattn_ln2_g, L1_xattn_ln2_b, L1_xattn_a1_wq, L1_xattn_a1_wk, L1_xattn_a1_wv, L1_xattn_a1_li1_w, L1_xattn_a1_li1_b, L1_xattn_a1_lnx_g, L1_xattn_a1_lnx_b, L1_xattn_a1_lny_g, L1_xattn_a1_lny_b, L1_xattn_a1_ln3_g, L1_xattn_a1_ln3_b, L1_xattn_a1_li2_w, L1_xattn_a1_li2_b, L1_xattn_a1_li3_w, L1_xattn_a1_li3_b, L1_xattn_a2_wq, L1_xattn_a2_wk, L1_xattn_a2_wv, L1_xattn_a2_li1_w, L1_xattn_a2_li1_b, L1_xattn_a2_lnx_g, L1_xattn_a2_lnx_b, L1_xattn_a2_lny_g, L1_xattn_a2_lny_b, L1_xattn_a2_ln3_g, L1_xattn_a2_ln3_b, L1_xattn_a2_li2_w, L1_xattn_a2_li2_b, L1_xattn_a2_li3_w, L1_xattn_a2_li3_b, L1_ffn_W1, L1_ffn_b1, L1_ffn_W2, L1_ffn_b2, L2_xattn_Wq, L2_xattn_Wkv, L2_xattn_Wo, L2_ffn_ln1_g, L2_ffn_ln1_b, L2_ffn_w1, L2_ffn_b1, L2_ffn_ln2_g, L2_ffn_ln2_b, L2_ffn_w2, L2_ffn_b2, L3_xattn_Wq, L3_xattn_Wk, L3_xattn_Wv, L3_xattn_Wo, L3_xattn_bo, L3_ffn_router_w, L3_ffn_expert_weights):
    import jax
    import jax.numpy as jnp

    def _L0_xattn_ref(x, cross_input, Wk, bk, Wq, bq, Wv, bv, Wck, bck, Wcq, bcq, Wcv, bcv, Wp, bp):
        import jax, jax.numpy as jnp
        import numpy as np
        B, T, TC, C, CC, H = (2, 256, 64, 128, 64, 16)
        D = C // H

        def _heads(t):
            b, l, _ = t.shape
            return t.reshape(b, l, H, D).transpose(0, 2, 1, 3)
        scale = np.float32(1.0 / np.sqrt(D))
        q = _heads(x @ Wq + bq)
        k = _heads(x @ Wk + bk)
        v = _heads(x @ Wv + bv)
        att = jnp.einsum('bhqd,bhkd->bhqk', q, k) * scale
        causal = jnp.tril(jnp.ones((T, T), bool))
        att = jnp.where(causal[None, None], att, -jnp.inf)
        y = jnp.einsum('bhqk,bhkd->bhqd', jax.nn.softmax(att, axis=-1), v)
        qc = _heads(x @ Wcq + bcq)
        kc = _heads(cross_input @ Wck + bck)
        vc = _heads(cross_input @ Wcv + bcv)
        attc = jnp.einsum('bhqd,bhkd->bhqk', qc, kc) * scale
        y = y + jnp.einsum('bhqk,bhkd->bhqd', jax.nn.softmax(attc, axis=-1), vc)
        y = y.transpose(0, 2, 1, 3).reshape(x.shape[0], T, C)
        return y @ Wp + bp

    def _L0_ffn_ref(x, gate_w, w1, w3, w2, sw1, sw3, sw2):
        import jax, jax.numpy as jnp
        import numpy as np
        DIM = 128
        HID = 64
        N_EXPERTS = 16
        TOP_K = 4
        bsz, seq_len, dim = x.shape
        xf = x.reshape(-1, dim)
        T = xf.shape[0]
        probs = jax.nn.softmax(xf @ gate_w.T, axis=-1)
        top_w, top_idx = jax.lax.top_k(probs, TOP_K)
        top_w = top_w / jnp.sum(top_w, axis=-1, keepdims=True)
        rows = jnp.arange(T)[:, None]
        combine = jnp.zeros((T, N_EXPERTS), dtype=xf.dtype).at[rows, top_idx].set(top_w)
        h1 = jnp.einsum('td,ehd->teh', xf, w1)
        h3 = jnp.einsum('td,ehd->teh', xf, w3)
        act = jax.nn.silu(h1) * h3
        eout = jnp.einsum('teh,edh->ted', act, w2)
        moe_out = jnp.einsum('ted,te->td', eout, combine)
        shared = jax.nn.silu(xf @ sw1.T) * (xf @ sw3.T) @ sw2.T
        return (moe_out + shared).reshape(bsz, seq_len, dim)

    def _L1_xattn_ref(xx, ee, ln1_g, ln1_b, ln2_g, ln2_b, a1_wq, a1_wk, a1_wv, a1_li1_w, a1_li1_b, a1_lnx_g, a1_lnx_b, a1_lny_g, a1_lny_b, a1_ln3_g, a1_ln3_b, a1_li2_w, a1_li2_b, a1_li3_w, a1_li3_b, a2_wq, a2_wk, a2_wv, a2_li1_w, a2_li1_b, a2_lnx_g, a2_lnx_b, a2_lny_g, a2_lny_b, a2_ln3_g, a2_ln3_b, a2_li2_w, a2_li2_b, a2_li3_w, a2_li3_b, training):
        import jax, jax.numpy as jnp
        import numpy as np
        H, D, C1, C2, S, M, B, W = (16, 32, 128, 64, 256, 64, 2, 4)

        def _ln(x, g, b):
            m = jnp.mean(x, -1, keepdims=True)
            v = jnp.var(x, -1, keepdims=True)
            return (x - m) * jax.lax.rsqrt(v + 1e-05) * g + b

        def _mha(x, y, wq, wk, wv, li1_w, li1_b, lnx_g, lnx_b, lny_g, lny_b, ln3_g, ln3_b, li2_w, li2_b, li3_w, li3_b, causal):
            xn = _ln(x, lnx_g, lnx_b)
            yn = _ln(y, lny_g, lny_b)
            q = jnp.einsum('bsc,hcd->bhsd', xn, wq)
            k = jnp.einsum('btc,hcd->bhtd', yn, wk)
            v = jnp.einsum('btc,hcd->bhtd', yn, wv)
            a = jax.nn.softmax(jnp.einsum('bhsd,bhtd->bhst', q, k) * D ** (-0.5), axis=-1)
            if causal:
                s, t = (a.shape[-2], a.shape[-1])
                mask = (jnp.arange(t)[None, :] > jnp.arange(s)[:, None]).astype(a.dtype)
                a = a * mask
            o = jnp.einsum('bhst,bhtd->bhsd', a, v)
            o = o.transpose(0, 2, 1, 3).reshape(x.shape[0], x.shape[1], H * D)
            x_out = x + o @ li1_w + li1_b
            h = jax.nn.gelu(_ln(x_out, ln3_g, ln3_b) @ li2_w + li2_b, approximate=False)
            return x_out + h @ li3_w + li3_b
        x = _ln(xx, ln1_g, ln1_b)
        x = x + _mha(x, x, a1_wq, a1_wk, a1_wv, a1_li1_w, a1_li1_b, a1_lnx_g, a1_lnx_b, a1_lny_g, a1_lny_b, a1_ln3_g, a1_ln3_b, a1_li2_w, a1_li2_b, a1_li3_w, a1_li3_b, causal=True)
        x = _ln(x, ln2_g, ln2_b)
        return x + _mha(x, ee, a2_wq, a2_wk, a2_wv, a2_li1_w, a2_li1_b, a2_lnx_g, a2_lnx_b, a2_lny_g, a2_lny_b, a2_ln3_g, a2_ln3_b, a2_li2_w, a2_li2_b, a2_li3_w, a2_li3_b, causal=False)

    def _L1_ffn_ref(x, W1, b1, W2, b2):
        import jax, jax.numpy as jnp
        import numpy as np
        EPS = 1e-05

        def _quantize(W):
            gamma = jnp.mean(jnp.abs(W))
            return jnp.clip(jnp.round(W / (gamma + EPS)), -1.0, 1.0)
        Wq1 = _quantize(W1)
        Wq2 = _quantize(W2)
        h = jax.nn.relu(jnp.einsum('bsd,fd->bsf', x, Wq1) + b1)
        out = jnp.einsum('bsf,df->bsd', h, Wq2) + b2
        return out

    def _L2_xattn_ref(x, z, Wq, Wkv, Wo):
        import jax, jax.numpy as jnp
        import numpy as np
        DIM = 128
        LATENT_DIM = 64
        NUM_HEADS = 16
        HEAD_DIM = DIM // NUM_HEADS
        SCALE = HEAD_DIM ** (-0.5)
        B, xN, _ = x.shape
        _, zN, _ = z.shape
        Q = (x @ Wq.T).reshape(B, xN, NUM_HEADS, HEAD_DIM)
        KV = (z @ Wkv.T).reshape(B, zN, 2, NUM_HEADS, HEAD_DIM)
        K = KV[:, :, 0]
        V = KV[:, :, 1]
        attn = jnp.einsum('bqhd,bkhd->bhqk', Q, K) * SCALE
        attn = jax.nn.softmax(attn, axis=-1)
        O = jnp.einsum('bhqk,bkhd->bqhd', attn, V).reshape(B, xN, DIM)
        return O @ Wo.T

    def _L2_ffn_ref(x, ln1_g, ln1_b, w1, b1, ln2_g, ln2_b, w2, b2):
        import jax, jax.numpy as jnp
        import numpy as np
        LN_EPS = 1e-05

        def layernorm(x, g, b):
            mu = jnp.mean(x, axis=-1, keepdims=True)
            var = jnp.mean((x - mu) ** 2, axis=-1, keepdims=True)
            return (x - mu) * jax.lax.rsqrt(var + LN_EPS) * g + b

        def act_quant_fake(x):
            scale = 127.0 / jnp.clip(jnp.max(jnp.abs(x), axis=-1, keepdims=True), 1e-05)
            return jnp.clip(jnp.round(x * scale), -128.0, 127.0) / scale

        def weight_quant_fake(w):
            scale = 1.0 / jnp.clip(jnp.mean(jnp.abs(w)), 1e-05)
            return jnp.clip(jnp.round(w * scale), -1.0, 1.0) / scale

        def bitlinear(x, w, b):
            dqx = act_quant_fake(x)
            dqw = weight_quant_fake(w)
            return jnp.einsum('btd,hd->bth', dqx, dqw) + b
        h = layernorm(x, ln1_g, ln1_b)
        h = bitlinear(h, w1, b1)
        h = jax.nn.gelu(h, approximate=False)
        h = layernorm(h, ln2_g, ln2_b)
        h = bitlinear(h, w2, b2)
        return h

    def _L3_xattn_ref(q, kv, Wq, Wk, Wv, Wo, bo):
        import jax, jax.numpy as jnp
        import numpy as np
        NUM_HEADS = 16
        HEAD_DIM = 64
        Q_DIM = 128
        KV_DIM = 64
        INNER = NUM_HEADS * HEAD_DIM
        B, N, _ = q.shape
        M = kv.shape[1]
        scale = HEAD_DIM ** (-0.5)
        qh = (q @ Wq).reshape(B, N, NUM_HEADS, HEAD_DIM).transpose(0, 2, 1, 3)
        kh = (kv @ Wk).reshape(B, M, NUM_HEADS, HEAD_DIM).transpose(0, 2, 1, 3)
        vh = (kv @ Wv).reshape(B, M, NUM_HEADS, HEAD_DIM).transpose(0, 2, 1, 3)
        scores = jnp.einsum('bhnd,bhmd->bhnm', qh, kh) * scale
        attn = jax.nn.softmax(scores, axis=-1)
        out = jnp.einsum('bhnm,bhmd->bhnd', attn, vh)
        out = out.transpose(0, 2, 1, 3).reshape(B, N, INNER)
        return out @ Wo + bo

    def _L3_ffn_ref(hidden_states, router_w, expert_weights):
        import jax, jax.numpy as jnp
        import numpy as np
        K_TOP = 2
        B, S, H = hidden_states.shape
        x = hidden_states.reshape(-1, H)
        logits = x @ router_w.T
        probs = jax.nn.softmax(logits, axis=-1)
        topk_vals, topk_idx = jax.lax.top_k(probs, K_TOP)
        topk_w = topk_vals / (topk_vals.sum(-1, keepdims=True) + 1e-06)
        expert_out = jnp.einsum('nh,eho->eno', x, expert_weights)
        combined = jnp.take_along_axis(expert_out.transpose(1, 0, 2), topk_idx[:, :, None], axis=1)
        combined = combined.transpose(1, 0, 2)
        remap_bias = jnp.take_along_axis(probs, topk_idx, axis=1).T[:, :, None]
        weights = topk_w.T[:, :, None]
        out = ((combined + remap_bias) * weights).sum(axis=0)
        return out.reshape(B, S, H)
    x = x + _L0_xattn_ref(_layernorm(x, axis=-1), ctx_512, L0_xattn_Wk, L0_xattn_bk, L0_xattn_Wq, L0_xattn_bq, L0_xattn_Wv, L0_xattn_bv, L0_xattn_Wck, L0_xattn_bck, L0_xattn_Wcq, L0_xattn_bcq, L0_xattn_Wcv, L0_xattn_bcv, L0_xattn_Wp, L0_xattn_bp)
    x = x + _L0_ffn_ref(_layernorm(x, axis=-1), L0_ffn_gate_w, L0_ffn_w1, L0_ffn_w3, L0_ffn_w2, L0_ffn_sw1, L0_ffn_sw3, L0_ffn_sw2)
    x = x + _L1_xattn_ref(_layernorm(x, axis=-1), ctx_512, L1_xattn_ln1_g, L1_xattn_ln1_b, L1_xattn_ln2_g, L1_xattn_ln2_b, L1_xattn_a1_wq, L1_xattn_a1_wk, L1_xattn_a1_wv, L1_xattn_a1_li1_w, L1_xattn_a1_li1_b, L1_xattn_a1_lnx_g, L1_xattn_a1_lnx_b, L1_xattn_a1_lny_g, L1_xattn_a1_lny_b, L1_xattn_a1_ln3_g, L1_xattn_a1_ln3_b, L1_xattn_a1_li2_w, L1_xattn_a1_li2_b, L1_xattn_a1_li3_w, L1_xattn_a1_li3_b, L1_xattn_a2_wq, L1_xattn_a2_wk, L1_xattn_a2_wv, L1_xattn_a2_li1_w, L1_xattn_a2_li1_b, L1_xattn_a2_lnx_g, L1_xattn_a2_lnx_b, L1_xattn_a2_lny_g, L1_xattn_a2_lny_b, L1_xattn_a2_ln3_g, L1_xattn_a2_ln3_b, L1_xattn_a2_li2_w, L1_xattn_a2_li2_b, L1_xattn_a2_li3_w, L1_xattn_a2_li3_b, 0)
    x = x + _L1_ffn_ref(_layernorm(x, axis=-1), L1_ffn_W1, L1_ffn_b1, L1_ffn_W2, L1_ffn_b2)
    x = x + _L2_xattn_ref(_layernorm(x, axis=-1), ctx_512, L2_xattn_Wq, L2_xattn_Wkv, L2_xattn_Wo)
    x = x + _L2_ffn_ref(_layernorm(x, axis=-1), L2_ffn_ln1_g, L2_ffn_ln1_b, L2_ffn_w1, L2_ffn_b1, L2_ffn_ln2_g, L2_ffn_ln2_b, L2_ffn_w2, L2_ffn_b2)
    x = x + _L3_xattn_ref(_layernorm(x, axis=-1), ctx_512, L3_xattn_Wq, L3_xattn_Wk, L3_xattn_Wv, L3_xattn_Wo, L3_xattn_bo)
    x = x + _L3_ffn_ref(_layernorm(x, axis=-1), L3_ffn_router_w, L3_ffn_expert_weights)
    return x

_drawn_inputs = setup_inputs


def setup_inputs(seed=0):
    import zlib

    import numpy as np

    out = dict(_drawn_inputs(seed))
    spreads = {'L0_xattn_bk': (0.0, 2.0),
     'L0_xattn_bq': (0.0, 0.472),
     'L0_xattn_bv': (0.0, 0.1),
     'L0_xattn_bck': (0.0, 2.0),
     'L0_xattn_bcq': (0.0, 0.378),
     'L0_xattn_bcv': (0.0, 0.1),
     'L0_xattn_bp': (0.0, 0.1),
     'L1_xattn_ln1_g': (1.0, 0.2),
     'L1_xattn_ln1_b': (0.0, 0.1),
     'L1_xattn_ln2_g': (1.0, 0.2),
     'L1_xattn_ln2_b': (0.0, 0.1),
     'L1_xattn_a1_li1_b': (0.0, 0.1),
     'L1_xattn_a1_lnx_g': (1.0, 0.6),
     'L1_xattn_a1_lnx_b': (0.0, 0.8),
     'L1_xattn_a1_lny_g': (1.0, 0.6),
     'L1_xattn_a1_lny_b': (0.0, 0.8),
     'L1_xattn_a1_ln3_g': (1.0, 0.6),
     'L1_xattn_a1_ln3_b': (0.0, 0.8),
     'L1_xattn_a1_li2_b': (0.0, 0.8),
     'L1_xattn_a1_li3_b': (0.0, 0.1),
     'L1_xattn_a2_li1_b': (0.0, 0.1),
     'L1_xattn_a2_lnx_g': (1.0, 0.6),
     'L1_xattn_a2_lnx_b': (0.0, 0.8),
     'L1_xattn_a2_lny_g': (1.0, 0.6),
     'L1_xattn_a2_lny_b': (0.0, 0.8),
     'L1_xattn_a2_ln3_g': (1.0, 0.6),
     'L1_xattn_a2_ln3_b': (0.0, 0.8),
     'L1_xattn_a2_li2_b': (0.0, 0.8),
     'L1_xattn_a2_li3_b': (0.0, 0.1),
     'L2_ffn_ln1_g': (1.0, 0.6),
     'L2_ffn_ln1_b': (0.0, 0.8),
     'L2_ffn_ln2_g': (1.0, 0.6),
     'L2_ffn_ln2_b': (0.0, 0.8)}
    factors = {'L0_ffn_gate_w': 8.0,
     'L0_ffn_w1': 8.0,
     'L0_ffn_w3': 8.0,
     'L0_ffn_w2': 8.0,
     'L0_ffn_sw1': 8.0,
     'L0_ffn_sw3': 8.0,
     'L0_ffn_sw2': 8.0,
     'L1_xattn_a1_wq': 8.0,
     'L1_xattn_a1_wk': 8.0,
     'L1_xattn_a1_wv': 6.517,
     'L1_xattn_a1_li1_w': 6.236,
     'L1_xattn_a1_li2_w': 3.473,
     'L1_xattn_a1_li3_w': 3.18,
     'L1_xattn_a2_wq': 8.0,
     'L1_xattn_a2_wk': 8.0,
     'L1_xattn_a2_wv': 4.388,
     'L1_xattn_a2_li1_w': 4.333,
     'L1_xattn_a2_li2_w': 3.244,
     'L1_xattn_a2_li3_w': 2.886,
     'L1_ffn_b1': 8.0,
     'L1_ffn_b2': 49.322,
     'L2_xattn_Wq': 8.0,
     'L2_xattn_Wkv': 8.0,
     'L2_xattn_Wo': 8.0,
     'L2_ffn_w1': 8.0,
     'L2_ffn_b1': 64.0,
     'L2_ffn_w2': 8.0,
     'L2_ffn_b2': 171.798,
     'L3_xattn_Wq': 8.0,
     'L3_xattn_Wk': 8.0,
     'L3_xattn_Wv': 8.0,
     'L3_xattn_Wo': 8.0,
     'L3_xattn_bo': 200.0,
     'L3_ffn_router_w': 58.37,
     'L3_ffn_expert_weights': 53.853}
    for name, (base, spread) in spreads.items():
        noise = np.random.default_rng([zlib.crc32(name.encode()), seed]).standard_normal(out[name].shape)
        drawn = base * np.exp(spread * noise) if base else spread * noise
        out[name] = jnp.asarray(drawn.astype(out[name].dtype))
    for name, factor in factors.items():
        out[name] = (out[name] * factor).astype(out[name].dtype)
    return out
```

```python
from collections import namedtuple
from contextlib import ExitStack, contextmanager

import numpy as np

import concourse.bass as bass
from concourse import mybir

F32 = mybir.dt.float32
BF16 = mybir.dt.bfloat16
ALU = mybir.AluOpType
ACT = mybir.ActivationFunctionType
AX_X = mybir.AxisListType.X

P = 128
B, T, C = 16, 256, 128
NT = T // P
TC, CC = 64, 64
H = 16
SLOT = 32
HG = P // SLOT
G = H // HG
PAIRS = H // 2
EPS = 1e-5
MASKED = -1e30
ROUND = 1.5 * 2.0 ** 23


class Store:
    pass


def record(**fields):
    return namedtuple("record", fields)(**fields)


def per_batch(eng, prologue, body):
    prologue()
    with eng.Fori(0, B // 2 - 1) as pair:
        body(2 * pair, 0, True)
        body(2 * pair + 1, 1, True)
    body(B - 2, 0, True)
    body(B - 1, 1, False)


def wait(eng, sem, value):
    if not isinstance(value, int) or value > 0:
        eng.wait_ge(sem, value)


def wait_apart(eng, sem, value):
    eng.wait_ge(sem, value)
    eng.nop(nofuse=True)


def bank_uses(front, middle, tail):
    def before(step, m, k):
        if step == "tail":
            done = m + 1 if isinstance(m, int) and m == B - 1 else m + 2
            return (front + middle) * done + tail * m + k
        ahead = front if step == "middle" else 0
        if isinstance(m, int) and m == 0:
            return ahead + k
        return (front + middle) * m + tail * (m - 1) + ahead + k
    return before


def tokens(array, n):
    return array[:, bass.ds(NT * n, NT), :] if not isinstance(n, int) else array[:, NT * n:NT * n + NT, :]


def tile_of(array, n, t):
    at = NT * n + t
    return array[:, bass.ds(at, 1), :] if not isinstance(at, int) else array[:, at:at + 1, :]


@contextmanager
def stage_semaphores(nc, prefix, names):
    sems = {s: nc.alloc_semaphore(f"{prefix}_{s}") for s in names.split()}
    yield record(**sems)
    nc.clear_and_free_semaphores(list(sems.values()))
    nc.all_engine_barrier()


def sem_space(nc, ctx, prefix, names):
    return ctx.enter_context(stage_semaphores(nc, prefix, names))



LN_SEMS = " ".join(f"{s}{k}" for k in range(3) for s in ("stats", "mean", "veps", "rstd", "norm", "gain", "shift"))


def ln_vector(dve, s, buf, k, source, target, n):
    stats, mean, rstd, norm = ln_sems(s, k)
    for t in range(NT):
        dve.bn_stats(buf.stats[k][:, t, :], source[t]).then_inc(stats, 1)
    wait_apart(dve, stats, NT * (n + 1))
    for t in range(NT):
        dve.bn_aggr(buf.mv[k][:, t, :], buf.stats[k][:, t, :]).then_inc(mean, 1)
    dve.wait_ge(mean, NT * (n + 1))
    dve.wait_ge(rstd, n + 1)
    for t in range(NT):
        dve.tensor_scalar(target[t], source[t], buf.mv[k][:, t, 0:1], buf.rstd[k][:, t:t + 1],
                          ALU.subtract, ALU.mult).then_inc(norm, 1)


def ln_sems(s, k):
    return [(s.stats0, s.mean0, s.rstd0, s.norm0), (s.stats1, s.mean1, s.rstd1, s.norm1),
            (s.stats2, s.mean2, s.rstd2, s.norm2)][k]


def ln_pool(pool, s, buf, k, n):
    _, mean, rstd, _ = ln_sems(s, k)
    veps = (s.veps0, s.veps1, s.veps2)[k]
    wait_apart(pool, mean, NT * (n + 1))
    pool.tensor_scalar(buf.veps[k][:, :], buf.mv[k][:, :, 1], EPS, None, ALU.add).then_inc(veps, 1)
    pool.wait_ge(veps, n + 1)
    pool.tensor_tensor(out=buf.rstd[k][:, :], in0=buf.veps[k][:, :], in1=buf.minus_half[:, :],
                       op=ALU.pow).then_inc(rstd, 1)


def ln_chain(s, g, cfg, n, p):
    src = [tile_of(cfg.source, n, t)[:, 0, :] for t in range(NT)]
    out = []
    for k, (gain, shift, keep) in enumerate(cfg.norms):
        last = k == len(cfg.norms) - 1
        dst = ([g.xn[p][:, t, :] for t in range(NT)] if last or keep is None
               else [tile_of(keep, n, t)[:, 0, :] for t in range(NT)])
        out.append((src, dst, gain, shift))
        src = dst
    return out


def front_vector(dve, s, g, cfg, n, p):
    for k, (src, dst, gain, shift) in enumerate(ln_chain(s, g, cfg, n, p)):
        ln_vector(dve, s, g, k, src, dst, n)
        norm = ln_sems(s, k)[3]
        if gain is not None:
            gs, ss = [(s.gain0, s.shift0), (s.gain1, s.shift1), (s.gain2, s.shift2)][k]
            dve.wait_ge(norm, NT * (n + 1))
            for t in range(NT):
                dve.tensor_tensor(out=dst[t], in0=dst[t], in1=gain, op=ALU.mult).then_inc(gs, 1)
            dve.wait_ge(gs, NT * (n + 1))
            for t in range(NT):
                dve.tensor_tensor(out=dst[t], in0=dst[t], in1=shift, op=ALU.add).then_inc(ss, 1)
            wait_apart(dve, ss, NT * (n + 1))
        elif k < len(cfg.norms) - 1:
            wait_apart(dve, norm, NT * (n + 1))


def front_pool(pool, s, g, cfg, n):
    for k in range(len(cfg.norms)):
        ln_pool(pool, s, g, k, n)


def wait_normed(eng, s, cfg, n):
    k = len(cfg.norms) - 1
    if cfg.norms[k][0] is not None:
        eng.wait_ge((s.shift0, s.shift1, s.shift2)[k], NT * (n + 1))
    else:
        eng.wait_ge(ln_sems(s, k)[3], NT * (n + 1))



def self_attention(nc, g, name, cfg):
    D = cfg.D
    NO = H * D // P
    banks_a = 3 + (cfg.wide_v)
    fa = bank_uses(banks_a, 1, 1)
    fb = bank_uses(3, 0, 1 + (NO > 1))
    pieces = [(0, j, 0, 4, P) for j in range(HG)] if cfg.causal else []
    pieces += [(qt, j, i, 2, T) for qt in range(1 if cfg.causal else 0, 2) for j in range(HG) for i in (0, 2)]
    NPC = len(pieces)
    piece_at = [[i for i in range(NPC) if i * H // NPC == h] for h in range(H)]
    SW = 384 if cfg.causal else 512
    K1 = 256
    K1Q = P if cfg.causal else 0
    with ExitStack() as ctx:
        s = sem_space(nc, ctx, name, LN_SEMS + " a_full a_free b_full b_free low max_full max_free "
                      "negmax_ready scores_ready exp_done masked pv_done recip_done "
                      "heads_normed ones_ready bias_added")
        qT = [g.qT[p][:, 0:G * T].rearrange("p (g q) -> p g q", g=G) for p in range(2)]
        kT = [g.kT[p][:, 0:G * T].rearrange("p (g q) -> p g q", g=G) for p in range(2)]
        qh = [g.qh[p][:, 0:G * T].rearrange("p (g q) -> p g q", g=G) for p in range(2)]
        kh = [g.kh[p][:, 0:G * T].rearrange("p (g q) -> p g q", g=G) for p in range(2)]
        V = [g.V[p][:, 0:NT * H * (D + 1)].rearrange("p (t h d) -> p t h d", t=NT, h=H) for p in range(2)]
        yT = g.yT if cfg.kv_gain is not None else g.xT
        osb = g.osb[:, 0:NT * H * D].rearrange("p (t f) -> p t f", t=NT)
        oT = g.oT[:, 0:NO * T].rearrange("p (n q) -> p n q", n=NO)
        FA, FB, MX, SC, O = g.bank[0], g.bank[1], g.bank[2:4], g.bank[4:6], g.bank[6:8]
        block = ctx.enter_context(nc.Block())
        load_later(block, cfg)

        @block.vector
        def _(dve):
            for p in range(2):
                last = dve.memset(V[p][:, :, :, D:D + 1], 1.0)
            last.then_inc(s.ones_ready, 1)

            def front(m, p):
                front_vector(dve, s, g, cfg, m, p)
                for i, (dst, bias) in enumerate(((qT[p], cfg.bq), (kT[p], cfg.bk))):
                    use = fb("front", m, i)
                    dve.wait_ge(s.b_full, use + 1)
                    src = FB[:, 0:512].rearrange("p (g q) -> p g q", g=2)
                    if bias is None:
                        dve.tensor_copy(dst[:, 0:2, :], src).then_inc(s.b_free, 1)
                    else:
                        dve.tensor_tensor(out=dst[:, 0:2, :], in0=src,
                                          in1=bias[:, 0:2].unsqueeze(2).to_broadcast([P, 2, T]),
                                          op=ALU.add).then_inc(s.b_free, 1)
                use = fb("front", m, 2)
                dve.wait_ge(s.b_full, use + 1)
                nt = 1 if cfg.wide_v else NT
                for t in range(nt):
                    src = FB[:, t * H * D:(t + 1) * H * D].rearrange("p (h d) -> p h d", h=H)
                    if cfg.bv is None:
                        last = dve.tensor_copy(V[p][:, t, :, 0:D], src)
                    else:
                        last = dve.tensor_tensor(out=V[p][:, t, :, 0:D], in0=src,
                                                 in1=cfg.bv.rearrange("p (h d) -> p h d", h=H), op=ALU.add)
                last.then_inc(s.b_free, 1)

            def piece(m, i):
                qt, j, g0, nh, keys = pieces[i]
                dve.wait_ge(s.max_full, NPC * m + i + 1)
                dve.tensor_reduce(g.negmax[:, qt, :].rearrange("p (g j) -> p g j", g=G)[:, g0:g0 + nh, j],
                                  MX[i % 2][:, 0:512].rearrange("p (h k) -> p h k", h=nh),
                                  AX_X, ALU.max, negate=True).then_inc(s.max_free, 1)

            def spread(m):
                dve.wait_ge(s.max_free, NPC * (m + 1))
                dve.tensor_copy(g.negmax4[:, :, :, 0:H],
                                g.negmax[:, :, :].unsqueeze(2).to_broadcast([P, NT, 4, H])
                                ).then_inc(s.negmax_ready, 1)

            def normalise(n, half):
                dve.wait_ge(s.pv_done, H * n + 8 * (half + 1))
                for qt in range(NT):
                    o = O[qt][:, 0:8 * (D + 1)].rearrange("p (h d) -> p h d", h=8)
                    dve.reciprocal(g.recip[:, qt, :], o[:, :, D]).then_inc(s.recip_done, 1)
                dve.wait_ge(s.recip_done, NT * (2 * n + half + 1))
                for qt in range(NT):
                    o = O[qt][:, 0:8 * (D + 1)].rearrange("p (h d) -> p h d", h=8)
                    last = dve.tensor_tensor(
                        out=osb[:, qt, half * 8 * D:(half + 1) * 8 * D].rearrange("p (h d) -> p h d", h=8),
                        in0=o[:, :, 0:D], in1=g.recip[:, qt, :].unsqueeze(2).to_broadcast([P, 8, D]),
                        op=ALU.mult)
                last.then_inc(s.heads_normed, 1)

            def tail(n, p):
                if NO > 1:
                    dve.wait_ge(s.b_full, fb("tail", n, 0) + 1)
                    dve.tensor_copy(oT[:, 2:4, :], FB[:, 0:512].rearrange("p (n q) -> p n q", n=2)
                                    ).then_inc(s.b_free, 1)
                dve.wait_ge(s.b_full, fb("tail", n, NO > 1) + 1)
                dve.wait_ge(s.bias_added, n + 1)
                dve.tensor_tensor(out=tokens(cfg.target, n), in0=FB[:, 0:T].rearrange("p (t c) -> p t c", t=NT),
                                  in1=g.resb[p][:, :, :], op=ALU.add).then_inc(s.b_free, 1)

            def prologue():
                front(0, 0)
                for i in range(NPC):
                    piece(0, i)
                spread(0)

            def body(n, p, has_next):
                if has_next:
                    front(n + 1, 1 - p)
                for h in range(H):
                    if has_next:
                        for i in piece_at[h]:
                            piece(n + 1, i)
                    if h == 8:
                        normalise(n, 0)
                if has_next:
                    spread(n + 1)
                normalise(n, 1)
                tail(n, p)

            per_batch(dve, prologue, body)

        @block.gpsimd
        def _(pool):
            def front(m, p):
                front_pool(pool, s, g, cfg, m)
                wait_normed(pool, s, cfg, m)
                pool.tensor_tensor(out=g.resb[p][:, :, :], in0=tokens(cfg.residual, m),
                                   in1=cfg.bias.unsqueeze(1).to_broadcast([P, NT, C]),
                                   op=ALU.add).then_inc(s.bias_added, 1)
                wait_apart(pool, s.b_free, fb("front", m, 1) + 1)
                pool.tensor_copy(qh[p][:, 0:2, :], qT[p][:, 0:2, :])
                pool.tensor_copy(kh[p][:, 0:2, :], kT[p][:, 0:2, :])
                wait_apart(pool, s.a_free, fa("front", m, 2) + 1)
                pool.tensor_copy(qh[p][:, 2:4, :], qT[p][:, 2:4, :])
                pool.tensor_copy(kh[p][:, 2:4, :], kT[p][:, 2:4, :]).then_inc(s.low, 1)

            def mask(n, h):
                wait_apart(pool, s.exp_done, H * n + h + 1)
                if cfg.causal:
                    diag = g.prob[h % 3][:, 0:512].rearrange("p (b q) -> p b q", b=2)[:, :, 0:P]
                    pool.affine_select(out=diag, in_=diag, compare_op=ALU.is_ge, fill=0.0, base=0,
                                       pattern=[[0, 2], [1, P]], channel_multiplier=-1).then_inc(s.masked, 1)
                else:
                    for t in range(NT):
                        last = pool.affine_select(out=g.probm[h % 3][:, t, :],
                                                  in_=g.prob[h % 3][:, t * (K1 + P):t * (K1 + P) + P],
                                                  compare_op=ALU.is_gt, fill=0.0, base=0,
                                                  pattern=[[-1, P]], channel_multiplier=1)
                    last.then_inc(s.masked, 1)

            def body(n, p, has_next):
                if has_next:
                    front(n + 1, 1 - p)
                for h in range(H):
                    mask(n, h)

            per_batch(pool, lambda: front(0, 0), body)

        @block.scalar
        def _(act):
            def front(m, p):
                act.wait_ge(s.a_full, fa("front", m, 0) + 1)
                if cfg.q_gain is None:
                    act.activation(g.xT[p][:, :], FA[:, 0:T], ACT.Copy).then_inc(s.a_free, 1)
                else:
                    act.activation(g.yT[p][:, :], FA[:, 0:T], ACT.Identity, scale=cfg.kv_gain, bias=cfg.kv_shift)
                    act.activation(g.xT[p][:, :], FA[:, 0:T], ACT.Identity, scale=cfg.q_gain,
                                   bias=cfg.q_shift).then_inc(s.a_free, 1)
                for i, (dst, bias) in enumerate(((qT[p], cfg.bq), (kT[p], cfg.bk))):
                    act.wait_ge(s.a_full, fa("front", m, 1 + i) + 1)
                    if bias is None:
                        act.activation(dst[:, 2:4, :], FA[:, 0:512].rearrange("p (g q) -> p g q", g=2),
                                       ACT.Copy).then_inc(s.a_free, 1)
                    else:
                        act.activation(dst[:, 2, :], FA[:, 0:T], ACT.Identity, bias=bias[:, 2:3])
                        act.activation(dst[:, 3, :], FA[:, T:2 * T], ACT.Identity,
                                       bias=bias[:, 3:4]).then_inc(s.a_free, 1)
                if cfg.wide_v:
                    act.wait_ge(s.a_full, fa("front", m, 3) + 1)
                    act.activation(V[p][:, 1, :, 0:D], FA[:, 0:512].rearrange("p (h d) -> p h d", h=H),
                                   ACT.Copy).then_inc(s.a_free, 1)

            def shift(m, p):
                act.wait_ge(s.a_full, fa("middle", m, 0) + 1)
                act.activation(g.negmaxT[p][:, :], FA[:, 0:P].bitcast(BF16), ACT.Copy).then_inc(s.a_free, 1)

            def exponent(n, h):
                act.wait_ge(s.scores_ready, H * n + h + 1)
                if h >= 3:
                    act.wait_ge(s.pv_done, H * n + h - 2)
                act.activation(g.prob[h % 3][:, 0:SW], SC[h % 2][:, 0:SW], ACT.Exp,
                               scale=cfg.scale).then_inc(s.exp_done, 1)

            def tail(n):
                act.wait_ge(s.a_full, fa("tail", n, 0) + 1)
                k = min(NO, 2)
                act.activation(oT[:, 0:k, :], FA[:, 0:k * T].rearrange("p (n q) -> p n q", n=k),
                               ACT.Copy).then_inc(s.a_free, 1)

            def prologue():
                front(0, 0)
                shift(0, 0)

            def body(n, p, has_next):
                if has_next:
                    front(n + 1, 1 - p)
                for h in range(H):
                    exponent(n, h)
                if has_next:
                    shift(n + 1, 1 - p)
                tail(n)

            per_batch(act, prologue, body)

        @block.tensor
        def _(pe):
            cfg.loaded(pe)
            pe.wait_ge(s.ones_ready, 1)

            def use_a(step, m, k):
                wait(pe, s.a_free, fa(step, m, k))

            def use_b(step, m, k):
                wait(pe, s.b_free, fb(step, m, k))

            def front(m, p):
                wait_normed(pe, s, cfg, m)
                use_a("front", m, 0)
                for t in range(NT):
                    last = pe.transpose(FA[:, t * P:(t + 1) * P], g.xn[p][:, t, :], g.ident[:, :])
                last.then_inc(s.a_full, 1)
                pe.wait_ge(s.a_free, fa("front", m, 0) + 1)
                for i, (w, x) in enumerate(((cfg.wq, g.xT[p]), (cfg.wk, yT[p]))):
                    for j, (bank, use, full) in enumerate(((FB, use_b, s.b_full), (FA, use_a, s.a_full))):
                        use("front", m, i + j)
                        for k in range(2):
                            last = pe.matmul(bank[:, k * T:(k + 1) * T], w[:, (2 * j + k) * P:(2 * j + k + 1) * P],
                                             x[:, :], start=True, stop=True)
                        last.then_inc(full, 1)
                use_b("front", m, 2)
                if cfg.wide_v:
                    pe.matmul(FB[:, 0:512], yT[p][:, 0:P], cfg.wv[:, :], start=True, stop=True).then_inc(s.b_full, 1)
                    use_a("front", m, 3)
                    pe.matmul(FA[:, 0:512], yT[p][:, P:2 * P], cfg.wv[:, :], start=True, stop=True
                              ).then_inc(s.a_full, 1)
                else:
                    for t in range(NT):
                        last = pe.matmul(FB[:, t * P:(t + 1) * P], yT[p][:, t * P:(t + 1) * P], cfg.wv[:, :],
                                         start=True, stop=True)
                    last.then_inc(s.b_full, 1)

            def piece(m, i, p):
                qt, j, g0, nh, keys = pieces[i]
                if i == 0:
                    pe.wait_ge(s.low, m + 1)
                if i >= 2:
                    pe.wait_ge(s.max_free, NPC * m + i - 1)
                bank = MX[i % 2]
                masks = cfg.causal
                if masks:
                    out = bank[:, 0:512].rearrange("p (h k) -> p h k", h=nh)[:, :, keys - P:keys]
                    pe.matmul(out, g.identh[:, :], g.causal[:, :].unsqueeze(1).to_broadcast([P, nh, P]),
                              start=True, stop=False, skip_group_check=True)
                r = SLOT * j
                for k in range(nh):
                    last = pe.matmul(bank[:, k * keys:(k + 1) * keys], qh[p][r:r + D, g0 + k, qt * P:(qt + 1) * P],
                                     kh[p][r:r + D, g0 + k, 0:keys], start=not masks, stop=True,
                                     skip_group_check=True)
                last.then_inc(s.max_full, 1)

            def shift(m):
                pe.wait_ge(s.negmax_ready, m + 1)
                use_a("middle", m, 0)
                for t in range(NT):
                    last = pe.transpose(FA[:, 0:P].bitcast(BF16)[:, t * P:(t + 1) * P],
                                        g.negmax4[:, t, :, :].rearrange("p r c -> p (r c)"), g.identh[:, :])
                last.then_inc(s.a_full, 1)

            def scores(n, h, p):
                if h == 0:
                    pe.wait_ge(s.a_free, fa("middle", n, 0) + 1)
                    pe.wait_ge(s.b_free, fb("front", n, 2) + 1)
                if h >= 2:
                    pe.wait_ge(s.exp_done, H * n + h - 1)
                r, gr = SLOT * (h % HG), h // HG
                bank = SC[h % 2]
                pe.matmul(bank[:, 0:T], g.sel_head[r:r + SLOT, h, :], g.negmaxT[p][r:r + SLOT, :],
                          start=True, stop=False, skip_group_check=True)
                pe.matmul(bank[:, K1:SW], g.sel_head[r:r + SLOT, h, :], g.negmaxT[p][r:r + SLOT, K1Q:T],
                          start=False, stop=False, skip_group_check=True)
                pe.matmul(bank[:, 0:T], kT[p][r:r + D, gr, 0:P], qT[p][r:r + D, gr, :],
                          start=False, stop=False, skip_group_check=True)
                pe.matmul(bank[:, K1:SW], kT[p][r:r + D, gr, P:T], qT[p][r:r + D, gr, K1Q:T],
                          start=False, stop=True, skip_group_check=True).then_inc(s.scores_ready, 1)

            def weigh(n, h, p):
                pe.wait_ge(s.masked, H * n + h + 1)
                if h == 8:
                    pe.wait_ge(s.heads_normed, 2 * n + 1)
                a = g.prob[h % 3]
                o = [O[qt][:, (h % 8) * (D + 1):(h % 8 + 1) * (D + 1)] for qt in range(NT)]
                if cfg.causal:
                    pe.matmul(o[0], a[:, 0:P], V[p][:, 0, h, :], start=True, stop=True)
                    pe.matmul(o[1], a[:, P:T], V[p][:, 0, h, :], start=True, stop=False)
                    last = pe.matmul(o[1], a[:, K1:K1 + P], V[p][:, 1, h, :], start=False, stop=True)
                else:
                    m = g.probm[h % 3]
                    pe.matmul(o[0], a[:, K1:K1 + P], V[p][:, 1, h, :], start=True, stop=False, skip_group_check=True)
                    pe.matmul(o[0][:, 0:D], m[:, 0, :], V[p][:, 0, h, 0:D], start=False, stop=False, skip_group_check=True)
                    pe.matmul(o[0][:, D:D + 1], a[:, 0:P], V[p][:, 0, h, D:D + 1], start=False, stop=True, skip_group_check=True)
                    pe.matmul(o[1][:, 0:D], m[:, 1, :], V[p][:, 1, h, 0:D], start=True, stop=False, skip_group_check=True)
                    pe.matmul(o[1][:, D:D + 1], a[:, P:T], V[p][:, 0, h, D:D + 1], start=False, stop=False, skip_group_check=True)
                    last = pe.matmul(o[1][:, D:D + 1], a[:, K1 + P:K1 + T], V[p][:, 1, h, D:D + 1], start=False, stop=True, skip_group_check=True)
                last.then_inc(s.pv_done, 1)

            def tail(n):
                pe.wait_ge(s.heads_normed, 2 * n + 2)
                use_a("tail", n, 0)
                for k in range(min(NO, 2)):
                    for t in range(NT):
                        last = pe.transpose(FA[:, k * T + t * P:k * T + (t + 1) * P],
                                            osb[:, t, k * P:(k + 1) * P], g.ident[:, :])
                last.then_inc(s.a_full, 1)
                if NO > 1:
                    use_b("tail", n, 0)
                    for k in range(2):
                        for t in range(NT):
                            last = pe.transpose(FB[:, k * T + t * P:k * T + (t + 1) * P],
                                                osb[:, t, (2 + k) * P:(3 + k) * P], g.ident[:, :])
                    last.then_inc(s.b_full, 1)
                pe.wait_ge(s.a_free, fa("tail", n, 0) + 1)
                use_b("tail", n, NO > 1)
                for t in range(NT):
                    for k in range(NO):
                        last = pe.matmul(FB[:, t * P:(t + 1) * P], oT[:, k, t * P:(t + 1) * P], cfg.wo[:, k, :],
                                         start=(k == 0), stop=(k == NO - 1))
                last.then_inc(s.b_full, 1)

            def prologue():
                front(0, 0)
                for i in range(NPC):
                    piece(0, i, 0)
                shift(0)

            def body(n, p, has_next):
                if has_next:
                    front(n + 1, 1 - p)
                for h in range(H + 1):
                    if h < H:
                        scores(n, h, p)
                        if has_next:
                            for i in piece_at[h]:
                                piece(n + 1, i, 1 - p)
                    if h >= 1:
                        weigh(n, h - 1, p)
                if has_next:
                    shift(n + 1)
                tail(n)

            per_batch(pe, prologue, body)



def cross_attention(nc, g, name, cfg):
    D = cfg.D
    NO = H * D // P
    HT = H // NO
    QC = max(1, NO // 2)
    QW = min(NO, 2)
    VC = max(1, H * D // 512)
    VW = H * D // VC
    front_a = 1 + QC // 2 + VC // 2
    front_b = (QC + 1) // 2 + 1 + (VC + 1) // 2
    fa = bank_uses(front_a, 1, (QC + 1) // 2)
    fb = bank_uses(front_b, 0, QC // 2 + 1)
    GROUPS = PAIRS // 2
    PU = max(k for k in (2, 4, 8) if 2 * k * (D + 1) <= 512)
    NU = PAIRS // PU
    q_use = [(c % 2, 1 + c // 2 if c % 2 else c // 2) for c in range(QC)]
    k_use = (QC + 1) // 2
    v_use = [(c % 2, 1 + QC // 2 + c // 2 if c % 2 else k_use + 1 + c // 2) for c in range(VC)]
    B_, A_ = 0, 1
    with ExitStack() as ctx:
        s = sem_space(nc, ctx, name, LN_SEMS + " a_full a_free b_full b_free low max_full max_free "
                      "negmax_ready scores_ready exp_done pv_done recip_done ctx_ready k_spread "
                      "heads_normed ones_ready bias_added v_ready")
        qT = [g.qT[p][:, 0:NO * T].rearrange("p (n q) -> p n q", n=NO) for p in range(2)]
        qh = [g.qh[p][:, 0:NO * T].rearrange("p (n q) -> p n q", n=NO) for p in range(2)]
        V = [g.V[p][:, 0:H * (D + 1)].rearrange("p (j i d) -> p j i d", j=PAIRS, i=2) for p in range(2)]
        osb = g.osb[:, 0:NT * H * D].rearrange("p (t f) -> p t f", t=NT)
        oT = g.oT[:, 0:NO * T].rearrange("p (n q) -> p n q", n=NO)
        FA, FB, MX, SC, O = g.bank[0], g.bank[1], g.bank[2:4], g.bank[4:6], g.bank[6:8]
        block = ctx.enter_context(nc.Block())
        load_later(block, cfg)

        def spread_v(eng, p, c, bank):
            j0, nj = c * PAIRS // VC, PAIRS // VC
            for i in range(2):
                rows = slice(i * TC, (i + 1) * TC)
                dst = V[p][rows, j0:j0 + nj, i, 0:D]
                src = bank[rows, 0:VW].rearrange("p (j i d) -> p j i d", j=nj, i=2)[:, :, i, :]
                if eng == "act":
                    last = nc.scalar.activation(dst, src, ACT.Copy)
                elif cfg.bv is None:
                    last = nc.vector.tensor_copy(dst, src)
                else:
                    last = nc.vector.tensor_tensor(
                        out=dst, in0=src, op=ALU.add,
                        in1=cfg.bv[rows, :].rearrange("p (j i d) -> p j i d", j=nj, i=2)[:, :, i, :])
            return last

        @block.vector
        def _(dve):
            for p in range(2):
                dve.memset(V[p][:, :, :, :], 0.0).then_inc(s.ones_ready, 1)
            dve.wait_ge(s.ones_ready, 2)
            for p in range(2):
                dve.memset(V[p][0:TC, :, 0, D:D + 1], 1.0)
                dve.memset(V[p][TC:P, :, 1, D:D + 1], 1.0).then_inc(s.ones_ready, 1)
            dve.wait_ge(s.ones_ready, 4)

            def front(m, p):
                front_vector(dve, s, g, cfg, m, p)
                for c, (bank, use) in enumerate(q_use):
                    if bank == B_:
                        dve.wait_ge(s.b_full, fb("front", m, use) + 1)
                        dst = qT[p][:, QW * c:QW * (c + 1), :]
                        src = FB[:, 0:QW * T].rearrange("p (n q) -> p n q", n=QW)
                        if cfg.bq is None:
                            dve.tensor_copy(dst, src).then_inc(s.b_free, 1)
                        else:
                            dve.tensor_scalar(dst, src, cfg.bq, None, ALU.add).then_inc(s.b_free, 1)
                dve.wait_ge(s.b_full, fb("front", m, k_use) + 1)
                k = FB[:, 0:NO * TC].rearrange("p (n k) -> p n k", n=NO)
                if NO == 1:
                    dst = g.kmask[p][:, :].rearrange("p (h k) -> p h k", h=H)
                    kb = k[:, 0, :].unsqueeze(1).to_broadcast([P, H, TC])
                    hm = cfg.head_mask[:, :].unsqueeze(2).to_broadcast([P, H, TC])
                    if cfg.bk is None:
                        last = dve.tensor_tensor(out=dst, in0=kb, in1=hm, op=ALU.mult)
                    else:
                        last = dve.scalar_tensor_tensor(out=dst, in0=kb, scalar=cfg.bk, in1=hm,
                                                        op0=ALU.add, op1=ALU.mult)
                else:
                    for h in range(HT):
                        dst = g.kmask[p][:, :].rearrange("p (n h k) -> p n h k", n=NO, h=HT)[:, :, h, :]
                        last = dve.tensor_scalar(dst, k, cfg.head_mask[:, h:h + 1], None, ALU.mult)
                last.then_inc(s.b_free, 1)
                for c, (bank, use) in enumerate(v_use):
                    if bank == B_:
                        dve.wait_ge(s.b_full, fb("front", m, use) + 1)
                        spread_v("dve", p, c, FB).then_inc(s.b_free, 1)

            def piece(m, i):
                qt, half = divmod(i, 2)
                dve.wait_ge(s.max_full, 4 * m + i + 1)
                dve.tensor_reduce(g.negmax[:, qt, 8 * half:8 * half + 8],
                                  MX[i % 2][:, 0:512].rearrange("p (h k) -> p h k", h=8),
                                  AX_X, ALU.max, negate=True).then_inc(s.max_free, 1)

            def spread(m):
                dve.wait_ge(s.max_free, 4 * (m + 1))
                dve.tensor_copy(g.negmax4[:, :, 0, 0:H], g.negmax[:, :, :]).then_inc(s.negmax_ready, 1)

            def normalise(n, u):
                dve.wait_ge(s.pv_done, GROUPS * n + (u + 1) * PU // 2)
                for qt in range(NT):
                    o = O[qt][:, 0:2 * PU * (D + 1)].rearrange("p (h d) -> p h d", h=2 * PU)
                    dve.reciprocal(g.recip16[:, qt, 0:2 * PU], o[:, :, D]).then_inc(s.recip_done, 1)
                dve.wait_ge(s.recip_done, NT * (NU * n + u + 1))
                for qt in range(NT):
                    o = O[qt][:, 0:2 * PU * (D + 1)].rearrange("p (h d) -> p h d", h=2 * PU)
                    last = dve.tensor_tensor(
                        out=osb[:, qt, u * 2 * PU * D:(u + 1) * 2 * PU * D].rearrange("p (h d) -> p h d", h=2 * PU),
                        in0=o[:, :, 0:D], in1=g.recip16[:, qt, 0:2 * PU].unsqueeze(2).to_broadcast([P, 2 * PU, D]),
                        op=ALU.mult)
                last.then_inc(s.heads_normed, 1)

            def tail(n, p):
                for c in range(QC):
                    if c % 2:
                        dve.wait_ge(s.b_full, fb("tail", n, c // 2) + 1)
                        dve.tensor_copy(oT[:, 2 * c:2 * c + 2, :], FB[:, 0:512].rearrange("p (n q) -> p n q", n=2)
                                        ).then_inc(s.b_free, 1)
                dve.wait_ge(s.b_full, fb("tail", n, QC // 2) + 1)
                if cfg.bias is not None:
                    dve.wait_ge(s.bias_added, n + 1)
                res = tokens(cfg.residual, n) if cfg.bias is None else g.resb[p][:, :, :]
                dve.tensor_tensor(out=tokens(cfg.target, n), in0=FB[:, 0:T].rearrange("p (t c) -> p t c", t=NT),
                                  in1=res, op=ALU.add).then_inc(s.b_free, 1)

            def prologue():
                front(0, 0)
                for i in range(4):
                    piece(0, i)
                spread(0)

            def body(n, p, has_next):
                if has_next:
                    front(n + 1, 1 - p)
                done = 0
                for e in range(GROUPS + 1):
                    if e < GROUPS and has_next:
                        piece(n + 1, e)
                    if e < GROUPS and e * 2 % PU == 0 and e:
                        normalise(n, done)
                        done += 1
                if has_next:
                    spread(n + 1)
                normalise(n, NU - 1)
                tail(n, p)

            per_batch(dve, prologue, body)

        @block.gpsimd
        def _(pool):
            def front(m, p):
                front_pool(pool, s, g, cfg, m)
                pool.tensor_copy(g.ctxb[p][:, :, :], (cfg.ctxT[:, bass.ds(m, 1), :] if not isinstance(m, int)
                                                      else cfg.ctxT[:, m:m + 1, :]).to_broadcast([CC, 2, TC])
                                 ).then_inc(s.ctx_ready, 1)
                if cfg.bias is not None:
                    wait_normed(pool, s, cfg, m)
                    pool.tensor_tensor(out=g.resb[p][:, :, :], in0=tokens(cfg.residual, m),
                                       in1=cfg.bias.unsqueeze(1).to_broadcast([P, NT, C]),
                                       op=ALU.add).then_inc(s.bias_added, 1)
                wait_apart(pool, s.b_free, fb("front", m, k_use) + 1)
                pool.tensor_copy(g.kmaskh[p][:, :], g.kmask[p][:, :])
                if QC > 1:
                    wait_apart(pool, s.a_free, fa("front", m, QC // 2) + 1)
                pool.tensor_copy(qh[p][:, :, :], qT[p][:, :, :]).then_inc(s.low, 1)

            def body(n, p, has_next):
                if has_next:
                    front(n + 1, 1 - p)

            per_batch(pool, lambda: front(0, 0), body)

        @block.scalar
        def _(act):
            act.wait_ge(s.ones_ready, 4)
            def front(m, p):
                act.wait_ge(s.a_full, fa("front", m, 0) + 1)
                if cfg.q_gain is None:
                    act.activation(g.xT[p][:, :], FA[:, 0:T], ACT.Copy).then_inc(s.a_free, 1)
                else:
                    act.activation(g.xT[p][:, :], FA[:, 0:T], ACT.Identity, scale=cfg.q_gain,
                                   bias=cfg.q_shift).then_inc(s.a_free, 1)
                for c, (bank, use) in enumerate(q_use):
                    if bank == A_:
                        act.wait_ge(s.a_full, fa("front", m, use) + 1)
                        act.activation(qT[p][:, 2 * c:2 * c + 2, :], FA[:, 0:512].rearrange("p (n q) -> p n q", n=2),
                                       ACT.Copy).then_inc(s.a_free, 1)
                for c, (bank, use) in enumerate(v_use):
                    if bank == A_:
                        act.wait_ge(s.a_full, fa("front", m, use) + 1)
                        spread_v("act", p, c, FA).then_inc(s.a_free, 1)

            def shift(m, p):
                act.wait_ge(s.a_full, fa("middle", m, 0) + 1)
                act.activation(g.negmaxT[p][0:H, :], FA[0:H, 0:P].bitcast(BF16), ACT.Copy).then_inc(s.a_free, 1)

            def tail(n):
                for c in range(0, QC, 2):
                    act.wait_ge(s.a_full, fa("tail", n, c // 2) + 1)
                    act.activation(oT[:, 2 * c:2 * c + QW, :], FA[:, 0:QW * T].rearrange("p (n q) -> p n q", n=QW),
                                   ACT.Copy).then_inc(s.a_free, 1)

            def prologue():
                front(0, 0)
                shift(0, 0)

            def body(n, p, has_next):
                if has_next:
                    front(n + 1, 1 - p)
                for e in range(GROUPS):
                    act.wait_ge(s.scores_ready, GROUPS * n + e + 1)
                    if e >= 3:
                        act.wait_ge(s.pv_done, GROUPS * n + e - 2)
                    act.activation(g.prob[e % 3][:, :], SC[e % 2][:, :], ACT.Exp,
                                   scale=cfg.scale).then_inc(s.exp_done, 1)
                if has_next:
                    shift(n + 1, 1 - p)
                tail(n)

            per_batch(act, prologue, body)

        @block.tensor
        def _(pe):
            cfg.loaded(pe)
            pe.wait_ge(s.ones_ready, 4)

            def use(bank, step, m, k):
                if bank == A_:
                    wait(pe, s.a_free, fa(step, m, k))
                else:
                    wait(pe, s.b_free, fb(step, m, k))

            BANK, FULL = (FB, FA), (s.b_full, s.a_full)

            def front(m, p):
                wait_normed(pe, s, cfg, m)
                use(A_, "front", m, 0)
                for t in range(NT):
                    last = pe.transpose(FA[:, t * P:(t + 1) * P], g.xn[p][:, t, :], g.ident[:, :])
                last.then_inc(s.a_full, 1)
                pe.wait_ge(s.a_free, fa("front", m, 0) + 1)
                for c, (bank, k) in enumerate(q_use):
                    use(bank, "front", m, k)
                    for i in range(QW):
                        n = QW * c + i
                        last = pe.matmul(BANK[bank][:, i * T:(i + 1) * T], cfg.wq[:, n * P:(n + 1) * P],
                                         g.xT[p][:, :], start=True, stop=True)
                    last.then_inc(FULL[bank], 1)
                pe.wait_ge(s.ctx_ready, m + 1)
                use(B_, "front", m, k_use)
                for n in range(NO):
                    last = pe.matmul(FB[:, n * TC:(n + 1) * TC], cfg.wk[:, n * P:(n + 1) * P], g.ctxb[p][:, 0, :],
                                     start=True, stop=True)
                last.then_inc(s.b_full, 1)
                for c, (bank, k) in enumerate(v_use):
                    use(bank, "front", m, k)
                    pe.matmul(BANK[bank][:, 0:VW], g.ctxb[p][:, :, :].rearrange("p i k -> p (i k)"),
                              cfg.wv[:, c * VW:(c + 1) * VW], start=True, stop=True).then_inc(FULL[bank], 1)

            def piece(m, i, p):
                qt, half = divmod(i, 2)
                if i == 0:
                    pe.wait_ge(s.low, m + 1)
                if i >= 2:
                    pe.wait_ge(s.max_free, 4 * m + i - 1)
                tiles = range(NO) if NO == 1 else range(half * NO // 2, (half + 1) * NO // 2)
                w = 512 if NO == 1 else HT * TC
                for k, n in enumerate(tiles):
                    last = pe.matmul(MX[i % 2][:, k * w:(k + 1) * w], qh[p][:, n, qt * P:(qt + 1) * P],
                                     g.kmaskh[p][:, half * 512 + k * w:half * 512 + (k + 1) * w],
                                     start=True, stop=True, skip_group_check=True)
                last.then_inc(s.max_full, 1)

            def shift(m):
                pe.wait_ge(s.negmax_ready, m + 1)
                use(A_, "middle", m, 0)
                for t in range(NT):
                    last = pe.transpose(FA[0:H, 0:P].bitcast(BF16)[:, t * P:(t + 1) * P],
                                        g.negmax4[:, t, 0, 0:H], g.identh[:, :])
                last.then_inc(s.a_full, 1)

            def scores(n, e, p):
                if e == 0:
                    pe.wait_ge(s.a_free, fa("middle", n, 0) + 1)
                    pe.wait_ge(s.b_free, fb("front", n, front_b - 1) + 1)
                    if VC > 1:
                        pe.wait_ge(s.a_free, fa("front", n, front_a - 1) + 1)
                if e >= 2:
                    pe.wait_ge(s.exp_done, GROUPS * n + e - 1)
                for i in range(2):
                    j = 2 * e + i
                    out = SC[e % 2][:, i * T:(i + 1) * T]
                    pe.matmul(out, g.sel_pair[0:H, j, :], g.negmaxT[p][0:H, :], start=True, stop=False)
                    last = pe.matmul(out, g.kmask[p][:, j * P:(j + 1) * P], qT[p][:, j * NO // PAIRS, :],
                                     start=False, stop=True)
                last.then_inc(s.scores_ready, 1)

            def weigh(n, e, p):
                pe.wait_ge(s.exp_done, GROUPS * n + e + 1)
                u = e * 2 // PU
                if e * 2 % PU == 0 and u:
                    pe.wait_ge(s.heads_normed, NU * n + u)
                for i in range(2):
                    j = 2 * e + i
                    w = 2 * (D + 1)
                    for qt in range(NT):
                        last = pe.matmul(O[qt][:, (j % PU) * w:(j % PU + 1) * w],
                                         g.prob[e % 3][:, i * T + qt * P:i * T + (qt + 1) * P],
                                         V[p][:, j, :, :].rearrange("p i d -> p (i d)"), start=True, stop=True)
                last.then_inc(s.pv_done, 1)

            def tail(n):
                pe.wait_ge(s.heads_normed, NU * (n + 1))
                for c in range(QC):
                    bank = A_ if c % 2 == 0 else B_
                    use(bank, "tail", n, c // 2)
                    for i in range(QW):
                        for t in range(NT):
                            k = QW * c + i
                            last = pe.transpose(BANK[bank][:, i * T + t * P:i * T + (t + 1) * P],
                                                osb[:, t, k * P:(k + 1) * P], g.ident[:, :])
                    last.then_inc(FULL[bank], 1)
                pe.wait_ge(s.a_free, fa("tail", n, (QC + 1) // 2 - 1) + 1)
                use(B_, "tail", n, QC // 2)
                for t in range(NT):
                    for k in range(NO):
                        last = pe.matmul(FB[:, t * P:(t + 1) * P], oT[:, k, t * P:(t + 1) * P], cfg.wo[:, k, :],
                                         start=(k == 0), stop=(k == NO - 1))
                last.then_inc(s.b_full, 1)

            def prologue():
                front(0, 0)
                for i in range(4):
                    piece(0, i, 0)
                shift(0)

            def body(n, p, has_next):
                if has_next:
                    front(n + 1, 1 - p)
                for e in range(GROUPS + 1):
                    if e < GROUPS:
                        scores(n, e, p)
                        if has_next:
                            piece(n + 1, e, 1 - p)
                    if e >= 1:
                        weigh(n, e - 1, p)
                if has_next:
                    shift(n + 1)
                tail(n)

            per_batch(pe, prologue, body)



def feed_forward(nc, g, name, cfg):
    HT = 4
    with ExitStack() as ctx:
        s = sem_space(nc, ctx, name, LN_SEMS + " xt_full xt_ready hidden_full hidden_ready out_full "
                      "residual_a residual_b target_ready")
        hT = [g.qT[p][:, 0:HT * T].rearrange("p (n q) -> p n q", n=HT) for p in range(2)]
        XT = g.bank[0:2]
        HID = [g.bank[2:4], g.bank[4:6]]
        OUT = g.bank[6:8]
        block = ctx.enter_context(nc.Block())
        load_later(block, cfg)

        @block.vector
        def _(dve):
            def front(m, p):
                front_vector(dve, s, g, cfg, m, p)
                if cfg.relu:
                    for k in range(HT):
                        dve.wait_ge(s.hidden_full, 2 * m + k // 2 + 1)
                        last = dve.tensor_scalar(hT[p][:, k, :], HID[p][k // 2][:, (k % 2) * T:(k % 2 + 1) * T],
                                                 cfg.b1[:, k:k + 1], 0.0, ALU.add, ALU.max)
                    last.then_inc(s.hidden_ready, 1)

            def tail(n, p):
                dve.wait_ge(s.out_full, n + 1)
                dve.wait_ge(s.residual_a, n + 1)
                if len(cfg.residuals) == 3:
                    dve.wait_ge(s.residual_b, 2 * (n + 1))
                elif len(cfg.residuals) == 2:
                    dve.wait_ge(s.residual_b, n + 1)
                dve.tensor_tensor(out=tokens(cfg.target, n), in0=OUT[p][:, 0:T].rearrange("p (t c) -> p t c", t=NT),
                                  in1=g.resb[p][:, :, :], op=ALU.add).then_inc(s.target_ready, 1)

            def body(n, p, has_next):
                if has_next:
                    front(n + 1, 1 - p)
                tail(n, p)

            per_batch(dve, lambda: front(0, 0), body)

        @block.gpsimd
        def _(pool):
            def front(m, p):
                front_pool(pool, s, g, cfg, m)
                wait_normed(pool, s, cfg, m)
                res = g.resb[p][:, :, :]
                pool.tensor_tensor(out=res, in0=tokens(cfg.residuals[0], m),
                                   in1=cfg.bias.unsqueeze(1).to_broadcast([P, NT, C]),
                                   op=ALU.add).then_inc(s.residual_a, 1)
                pool.wait_ge(s.residual_a, m + 1)
                extra = len(cfg.residuals) - 1
                for i, r in enumerate(cfg.residuals[1:]):
                    pool.tensor_tensor(out=res, in0=res, in1=tokens(r, m), op=ALU.add).then_inc(s.residual_b, 1)
                    if i < extra - 1:
                        pool.wait_ge(s.residual_b, extra * m + i + 1)

            per_batch(pool, lambda: front(0, 0), lambda n, p, nx: front(n + 1, 1 - p) if nx else None)

        @block.scalar
        def _(act):
            def front(m, p):
                act.wait_ge(s.xt_full, m + 1)
                if cfg.x_gain is None:
                    act.activation(g.xT[p][:, :], XT[p][:, 0:T], ACT.Copy).then_inc(s.xt_ready, 1)
                else:
                    act.activation(g.xT[p][:, :], XT[p][:, 0:T], ACT.Identity, scale=cfg.x_gain,
                                   bias=cfg.x_shift).then_inc(s.xt_ready, 1)
                if not cfg.relu:
                    for k in range(HT):
                        act.wait_ge(s.hidden_full, 2 * m + k // 2 + 1)
                        last = act.activation(hT[p][:, k, :], HID[p][k // 2][:, (k % 2) * T:(k % 2 + 1) * T],
                                              ACT.Gelu, bias=cfg.b1[:, k:k + 1])
                    last.then_inc(s.hidden_ready, 1)

            per_batch(act, lambda: front(0, 0), lambda n, p, nx: front(n + 1, 1 - p) if nx else None)

        @block.tensor
        def _(pe):
            cfg.loaded(pe)

            def front(m, p):
                wait_normed(pe, s, cfg, m)
                for t in range(NT):
                    last = pe.transpose(XT[p][:, t * P:(t + 1) * P], g.xn[p][:, t, :], g.ident[:, :])
                last.then_inc(s.xt_full, 1)
                pe.wait_ge(s.xt_ready, m + 1)
                for k in range(HT):
                    mm = pe.matmul(HID[p][k // 2][:, (k % 2) * T:(k % 2 + 1) * T], cfg.w1[:, k * P:(k + 1) * P],
                                   g.xT[p][:, :], start=True, stop=True)
                    if k % 2:
                        mm.then_inc(s.hidden_full, 1)

            def tail(n, p):
                pe.wait_ge(s.hidden_ready, n + 1)
                for t in range(NT):
                    for k in range(HT):
                        last = pe.matmul(OUT[p][:, t * P:(t + 1) * P], hT[p][:, k, t * P:(t + 1) * P],
                                         cfg.w2[:, k, :], start=(k == 0), stop=(k == HT - 1))
                last.then_inc(s.out_full, 1)

            def body(n, p, has_next):
                if has_next:
                    front(n + 1, 1 - p)
                tail(n, p)

            per_batch(pe, lambda: front(0, 0), body)



GATE_SEMS = (" logits_full shifted exped maxed shift_done summed rsum probs_ready topped keys_ready "
             "replaced weighed wsum wguard wrecip combined split_a split_b split_c split_d pbias pbias_sum")


def gate_vector(dve, s, g, cfg, m, p, LG):
    E, K, S = cfg.experts, cfg.top, 8 - cfg.top
    gb = g.gate
    lg = LG[:, 0:NT * E].rearrange("p (t e) -> p t e", t=NT)
    dve.wait_ge(s.logits_full, m + 1)
    dve.tensor_reduce(gb.nmax[:, :], lg, AX_X, ALU.max, negate=True).then_inc(s.maxed, 1)
    dve.wait_ge(s.maxed, m + 1)
    dve.tensor_tensor(out=gb.e[:, :, 0:E], in0=lg, in1=gb.nmax[:, :].unsqueeze(2).to_broadcast([P, NT, E]),
                      op=ALU.add).then_inc(s.shifted, 1)
    dve.wait_ge(s.exped, m + 1)
    dve.tensor_reduce(gb.sum[:, :], gb.e[:, :, 0:E], AX_X, ALU.add).then_inc(s.summed, 1)
    dve.wait_ge(s.summed, m + 1)
    dve.reciprocal(gb.rsum[:, :], gb.sum[:, :]).then_inc(s.rsum, 1)
    dve.wait_ge(s.rsum, m + 1)
    dve.tensor_tensor(out=gb.probs[:, :, 0:E], in0=gb.e[:, :, 0:E],
                      in1=gb.rsum[:, :].unsqueeze(2).to_broadcast([P, NT, E]), op=ALU.mult).then_inc(s.probs_ready, 1)
    wait_apart(dve, s.probs_ready, m + 1)
    for t in range(NT):
        dve.max(gb.top[:, t, :], gb.probs[:, t, 0:E]).then_inc(s.topped, 1)
    dve.wait_ge(s.topped, NT * (m + 1))
    dve.tensor_copy(gb.keys[:, :, 0:K], gb.top[:, :, 0:K]).then_inc(s.keys_ready, 1)
    wait_apart(dve, s.keys_ready, m + 1)
    for t in range(NT):
        dve.match_replace(gb.marked[:, t, 0:E + S], gb.keys[:, t, :], gb.probs[:, t, 0:E + S], -2.0
                          ).then_inc(s.replaced, 1)
    dve.wait_ge(s.replaced, NT * (m + 1))
    dve.scalar_tensor_tensor(out=gb.w[:, :, 0:E], in0=gb.marked[:, :, 0:E], scalar=0.0, in1=gb.probs[:, :, 0:E],
                             op0=ALU.is_lt, op1=ALU.mult).then_inc(s.weighed, 1)
    dve.wait_ge(s.weighed, m + 1)
    dve.tensor_reduce(gb.wsum[:, :], gb.w[:, :, 0:E], AX_X, ALU.add).then_inc(s.wsum, 1)
    dve.wait_ge(s.wsum, m + 1)
    total = gb.wsum
    if cfg.guard:
        dve.tensor_scalar(gb.wguard[:, :], gb.wsum[:, :], cfg.guard, None, ALU.add).then_inc(s.wguard, 1)
        dve.wait_ge(s.wguard, m + 1)
        total = gb.wguard
    dve.reciprocal(gb.wrecip[:, :], total[:, :]).then_inc(s.wrecip, 1)
    dve.wait_ge(s.wrecip, m + 1)
    dve.tensor_tensor(out=gb.c[p][:, :, 0:E], in0=gb.w[:, :, 0:E],
                      in1=gb.wrecip[:, :].unsqueeze(2).to_broadcast([P, NT, E]), op=ALU.mult).then_inc(s.combined, 1)
    dve.wait_ge(s.combined, m + 1)


def gate_exp(act, s, g, cfg, m):
    act.wait_ge(s.shifted, m + 1)
    act.activation(g.gate.e[:, :, 0:cfg.experts], g.gate.e[:, :, 0:cfg.experts], ACT.Exp).then_inc(s.exped, 1)


def route(nc, g, name, cfg):
    E = cfg.experts
    with ExitStack() as ctx:
        s = sem_space(nc, ctx, name, LN_SEMS + GATE_SEMS + " xt_full xt_ready parts_full parts_ready sentinels")
        XT, LG, PT = g.bank[0:2], g.bank[2:4], g.bank[4:6]
        gb = g.gate
        block = ctx.enter_context(nc.Block())
        load_later(block, cfg)

        @block.vector
        def _(dve):
            dve.memset(gb.probs[:, :, :], -1.0)
            dve.memset(gb.keys[:, :, :], -1.0).then_inc(s.sentinels, 1)
            dve.wait_ge(s.sentinels, 1)

            def front(m, p):
                front_vector(dve, s, g, cfg, m, p)

            def tail(n, p):
                gate_vector(dve, s, g, cfg, n, p, LG[p])
                c, part, rest = gb.c[p], gb.part[p], gb.rest
                dve.tensor_copy(part[:, :, 0, :], c[:, :, :]).then_inc(s.split_a, 1)
                dve.wait_ge(s.split_a, n + 1)
                dve.tensor_tensor(out=rest[:, 0, :, :], in0=c[:, :, :], in1=part[:, :, 0, :], op=ALU.subtract
                                  ).then_inc(s.split_b, 1)
                dve.wait_ge(s.split_b, n + 1)
                dve.tensor_copy(part[:, :, 1, :], rest[:, 0, :, :]).then_inc(s.split_c, 1)
                dve.wait_ge(s.split_c, n + 1)
                dve.tensor_tensor(out=part[:, :, 2, :], in0=rest[:, 0, :, :], in1=part[:, :, 1, :], op=ALU.subtract
                                  ).then_inc(s.split_d, 1)

            def body(n, p, has_next):
                if has_next:
                    front(n + 1, 1 - p)
                tail(n, p)

            per_batch(dve, lambda: front(0, 0), body)

        @block.gpsimd
        def _(pool):
            per_batch(pool, lambda: front_pool(pool, s, g, cfg, 0),
                      lambda n, p, nx: front_pool(pool, s, g, cfg, n + 1) if nx else None)

        @block.scalar
        def _(act):
            def front(m, p):
                act.wait_ge(s.xt_full, m + 1)
                act.activation(g.xT[p][:, :], XT[p][:, 0:T], ACT.Copy).then_inc(s.xt_ready, 1)

            def body(n, p, has_next):
                if has_next:
                    front(n + 1, 1 - p)
                gate_exp(act, s, g, cfg, n)
                act.wait_ge(s.parts_full, n + 1)
                dst = g.combT[:, bass.ds(T * n, T)] if not isinstance(n, int) else g.combT[:, T * n:T * n + T]
                act.activation(dst, PT[p][0:3 * E, 0:P].bitcast(BF16), ACT.Copy).then_inc(s.parts_ready, 1)

            per_batch(act, lambda: front(0, 0), body)

        @block.tensor
        def _(pe):
            cfg.loaded(pe)

            def front(m, p):
                wait_normed(pe, s, cfg, m)
                for t in range(NT):
                    last = pe.transpose(XT[p][:, t * P:(t + 1) * P], g.xn[p][:, t, :], g.ident[:, :])
                last.then_inc(s.xt_full, 1)
                pe.wait_ge(s.xt_ready, m + 1)
                for t in range(NT):
                    last = pe.matmul(LG[p][:, t * E:(t + 1) * E], g.xT[p][:, t * P:(t + 1) * P], cfg.gate_w[:, :],
                                     start=True, stop=True)
                last.then_inc(s.logits_full, 1)

            def body(n, p, has_next):
                if has_next:
                    front(n + 1, 1 - p)
                wait_apart(pe, s.split_d, n + 1)
                for t in range(NT):
                    last = pe.transpose(PT[p][0:3 * E, 0:P].bitcast(BF16)[:, t * P:(t + 1) * P],
                                        gb.part[p][:, t, :, :].rearrange("p k e -> p (k e)"), g.identh[:, :])
                last.then_inc(s.parts_full, 1)

            per_batch(pe, lambda: front(0, 0), body)


def gated_experts(nc, g, name, cfg):
    E, HID = 16, 64
    U = E // 2 + 1
    with ExitStack() as ctx:
        s = sem_space(nc, ctx, name, LN_SEMS + " xt_full xt_ready hidden_full silu_done gated scaled "
                      "used target_ready")
        XT, HB, CB, Y = g.bank[0], g.bank[1:3], g.bank[3:5], g.bank[5:7]
        block = ctx.enter_context(nc.Block())

        def rows(u):
            return P if u < U - 1 else HID

        @block.vector
        def _(dve):
            def front(m, p):
                front_vector(dve, s, g, cfg, m, p)

            def body(n, p, has_next):
                if has_next:
                    front(n + 1, 1 - p)
                for u in range(U):
                    r = rows(u)
                    dve.wait_ge(s.silu_done, U * n + u + 1)
                    if u >= 3:
                        dve.wait_ge(s.used, U * n + u - 2)
                    a = g.prob[u % 3][0:r, 0:T]
                    dve.tensor_tensor(out=a, in0=g.silu[u % 2][0:r, :], in1=HB[u % 2][0:r, T:2 * T], op=ALU.mult
                                      ).then_inc(s.gated, 1)
                    if u < U - 1:
                        dve.wait_ge(s.gated, U * n + u + 1)
                        dve.tensor_tensor(out=a, in0=a, in1=CB[u % 2][:, 0:T], op=ALU.mult).then_inc(s.scaled, 1)
                dve.wait_ge(s.used, U * (n + 1))
                for t in range(NT):
                    last = dve.tensor_tensor(out=tile_of(cfg.target, n, t)[:, 0, :], in0=Y[t][:, 0:C],
                                             in1=tile_of(cfg.residual, n, t)[:, 0, :], op=ALU.add)
                last.then_inc(s.target_ready, 1)

            per_batch(dve, lambda: front(0, 0), body)

        @block.gpsimd
        def _(pool):
            per_batch(pool, lambda: front_pool(pool, s, g, cfg, 0),
                      lambda n, p, nx: front_pool(pool, s, g, cfg, n + 1) if nx else None)

        @block.scalar
        def _(act):
            def front(m, p):
                act.wait_ge(s.xt_full, m + 1)
                act.activation(g.xT[p][:, :], XT[:, 0:T], ACT.Copy).then_inc(s.xt_ready, 1)

            def body(n, p, has_next):
                if has_next:
                    front(n + 1, 1 - p)
                for u in range(U):
                    act.wait_ge(s.hidden_full, U * n + u + 1)
                    if u >= 2:
                        act.wait_ge(s.gated, U * n + u - 1)
                    act.activation(g.silu[u % 2][0:rows(u), :], HB[u % 2][0:rows(u), 0:T], ACT.Silu
                                   ).then_inc(s.silu_done, 1)

            per_batch(act, lambda: front(0, 0), body)

        @block.tensor
        def _(pe):
            cfg.loaded(pe)

            def front(m, p):
                wait_normed(pe, s, cfg, m)
                for t in range(NT):
                    last = pe.transpose(XT[:, t * P:(t + 1) * P], g.xn[p][:, t, :], g.ident[:, :])
                last.then_inc(s.xt_full, 1)

            def hidden(n, u, p):
                if u >= 2:
                    pe.wait_ge(s.gated, U * n + u - 1)
                    wait_apart(pe, s.scaled, (U - 1) * n + u - 1)
                r = rows(u)
                w1 = cfg.w1[:, u * P:(u + 1) * P] if u < U - 1 else cfg.sw1[:, :]
                w3 = cfg.w3[:, u * P:(u + 1) * P] if u < U - 1 else cfg.sw3[:, :]
                if u < U - 1:
                    comb = g.combT[:, bass.ds(T * n, T)] if not isinstance(n, int) else g.combT[:, T * n:T * n + T]
                    pe.matmul(CB[u % 2][:, 0:T], g.sel_expert[:, u, :], comb, start=True, stop=True)
                pe.matmul(HB[u % 2][0:r, 0:T], w1, g.xT[p][:, :], start=True, stop=True)
                pe.matmul(HB[u % 2][0:r, T:2 * T], w3, g.xT[p][:, :], start=True, stop=True).then_inc(s.hidden_full, 1)

            def output(n, u):
                r = rows(u)
                if u < U - 1:
                    pe.wait_ge(s.scaled, (U - 1) * n + u + 1)
                else:
                    pe.wait_ge(s.gated, U * n + u + 1)
                if u == 0 and isinstance(n, int) and n > 0:
                    pe.wait_ge(s.target_ready, n)
                w2 = cfg.w2[:, u, :] if u < U - 1 else cfg.sw2[:, :]
                for t in range(NT):
                    last = pe.matmul(Y[t][:, 0:C], g.prob[u % 3][0:r, t * P:(t + 1) * P], w2,
                                     start=(u == 0), stop=(u == U - 1))
                last.then_inc(s.used, 1)

            def body(n, p, has_next):
                pe.wait_ge(s.xt_ready, n + 1)
                if has_next:
                    front(n + 1, 1 - p)
                for u in range(U + 1):
                    if u < U:
                        hidden(n, u, p)
                    if u >= 1:
                        output(n, u - 1)

            per_batch(pe, lambda: front(0, 0), body)



def quantise(dve, s, q, buf, source, p, n):
    peak, guard, recip, level, rounded, clipped = q
    dve.tensor_reduce(buf.peak[:, :], source, AX_X, ALU.max, apply_absolute_value=True).then_inc(peak, 1)
    dve.wait_ge(peak, n + 1)
    dve.tensor_scalar(buf.peakc[:, :], buf.peak[:, :], 1e-5, None, ALU.max).then_inc(guard, 1)
    dve.wait_ge(guard, n + 1)
    dve.reciprocal(buf.recip[:, :], buf.peakc[:, :]).then_inc(recip, 1)
    dve.wait_ge(recip, n + 1)
    dve.tensor_scalar(buf.scale[:, :], buf.recip[:, :], 127.0, None, ALU.mult)
    dve.tensor_scalar(buf.level[p][:, :], buf.peakc[:, :], 1.0 / 127.0, buf.wlevel, ALU.mult, ALU.mult
                      ).then_inc(level, 1)
    dve.wait_ge(level, n + 1)
    for t in range(NT):
        dve.tensor_scalar(source[:, t, :], source[:, t, :], buf.scale[:, t:t + 1], ROUND, ALU.mult, ALU.add
                          ).then_inc(rounded, 1)
    dve.wait_ge(rounded, NT * (n + 1))
    dve.tensor_scalar(source, source, ROUND + 127.0, ROUND - 128.0, ALU.min, ALU.max).then_inc(clipped, 1)


def quantised_feed_forward(nc, g, name, cfg):
    HT, F = 4, 512
    Q = "peak guard recip level rounded clipped"
    with ExitStack() as ctx:
        s = sem_space(nc, ctx, name, LN_SEMS + " low_a at_full at_ready hidden_full biased geled "
                      "stats_h mean_h veps_h rstd_h norm_h gain_h shift_h low_b bt_full bt_ready out_full "
                      "residual_added target_ready " + " ".join(f"{x}_{k}" for k in "ab" for x in Q.split()))
        qa = (s.peak_a, s.guard_a, s.recip_a, s.level_a, s.rounded_a, s.clipped_a)
        qb = (s.peak_b, s.guard_b, s.recip_b, s.level_b, s.rounded_b, s.clipped_b)
        hid = [g.qT[p][:, 0:NT * F].rearrange("p (t f) -> p t f", t=NT) for p in range(2)]
        intsT = [g.qh[p][:, 0:HT * T].rearrange("p (n q) -> p n q", n=HT) for p in range(2)]
        ints_b = g.kh[0][:, 0:NT * F].rearrange("p (t f) -> p t f", t=NT)
        ints_a = g.kh[1][:, 0:NT * C].rearrange("p (t f) -> p t f", t=NT)
        xTh = g.negmaxT[0]
        AT, HB, BT, OUT = g.bank[0], g.bank[1:5], g.bank[5], g.bank[6:8]
        block = ctx.enter_context(nc.Block())
        load_later(block, cfg)

        @block.vector
        def _(dve):
            def front(m, p):
                front_vector(dve, s, g, cfg, m, p)
                quantise(dve, s, qa, g.quant_a, g.xn[p][:, :, :], p, m)
                for t in range(NT):
                    dve.wait_ge(s.hidden_full, NT * m + t + 1)
                    last = dve.scalar_tensor_tensor(out=hid[p][:, t, :], in0=HB[2 * p + t][:, :],
                                                    scalar=g.quant_a.level[p][:, t:t + 1], in1=cfg.b1,
                                                    op0=ALU.mult, op1=ALU.add)
                last.then_inc(s.biased, 1)

            def tail(n, p):
                h = hid[p]
                wait_apart(dve, s.geled, n + 1)
                for t in range(NT):
                    dve.bn_stats(g.stats[0][:, t, :], h[:, t, :]).then_inc(s.stats_h, 1)
                wait_apart(dve, s.stats_h, NT * (n + 1))
                for t in range(NT):
                    dve.bn_aggr(g.mvh[:, t, :], g.stats[0][:, t, :]).then_inc(s.mean_h, 1)
                dve.wait_ge(s.mean_h, NT * (n + 1))
                dve.wait_ge(s.rstd_h, n + 1)
                for t in range(NT):
                    dve.tensor_scalar(h[:, t, :], h[:, t, :], g.mvh[:, t, 0:1], g.rstdh[:, t:t + 1],
                                      ALU.subtract, ALU.mult).then_inc(s.norm_h, 1)
                dve.wait_ge(s.norm_h, NT * (n + 1))
                dve.tensor_tensor(out=h, in0=h, in1=cfg.gain2.unsqueeze(1).to_broadcast([P, NT, F]), op=ALU.mult
                                  ).then_inc(s.gain_h, 1)
                dve.wait_ge(s.gain_h, n + 1)
                dve.tensor_tensor(out=h, in0=h, in1=cfg.shift2.unsqueeze(1).to_broadcast([P, NT, F]), op=ALU.add
                                  ).then_inc(s.shift_h, 1)
                dve.wait_ge(s.shift_h, n + 1)
                quantise(dve, s, qb, g.quant_b, h, p, n)
                dve.wait_ge(s.out_full, n + 1)
                dve.wait_ge(s.residual_added, n + 1)
                for t in range(NT):
                    last = dve.scalar_tensor_tensor(out=tile_of(cfg.target, n, t)[:, 0, :], in0=OUT[p][:, t * P:(t + 1) * P],
                                                    scalar=g.quant_b.level[p][:, t:t + 1], in1=g.resb[p][:, t, :],
                                                    op0=ALU.mult, op1=ALU.add)
                last.then_inc(s.target_ready, 1)

            def body(n, p, has_next):
                if has_next:
                    front(n + 1, 1 - p)
                tail(n, p)

            per_batch(dve, lambda: front(0, 0), body)

        @block.gpsimd
        def _(pool):
            def front(m, p):
                front_pool(pool, s, g, cfg, m)
                pool.tensor_tensor(out=g.resb[p][:, :, :], in0=tokens(cfg.residual, m),
                                   in1=cfg.bias.unsqueeze(1).to_broadcast([P, NT, C]),
                                   op=ALU.add).then_inc(s.residual_added, 1)

            def body(n, p, has_next):
                if has_next:
                    front(n + 1, 1 - p)
                wait_apart(pool, s.mean_h, NT * (n + 1))
                pool.tensor_scalar(g.veps[0][:, :], g.mvh[:, :, 1], EPS, None, ALU.add).then_inc(s.veps_h, 1)
                pool.wait_ge(s.veps_h, n + 1)
                pool.tensor_tensor(out=g.rstdh[:, :], in0=g.veps[0][:, :], in1=g.minus_half[:, :],
                                   op=ALU.pow).then_inc(s.rstd_h, 1)

            per_batch(pool, lambda: front(0, 0), body)

        @block.scalar
        def _(act):
            def front(m, p):
                act.wait_ge(s.clipped_a, m + 1)
                act.activation(ints_a, g.xn[p][:, :, :], ACT.Identity, bias=g.minus_round[:, :]).then_inc(s.low_a, 1)
                act.wait_ge(s.at_full, m + 1)
                act.activation(xTh[:, :], AT[:, 0:P].bitcast(BF16), ACT.Copy).then_inc(s.at_ready, 1)
                act.wait_ge(s.biased, m + 1)
                act.activation(hid[p], hid[p], ACT.Gelu).then_inc(s.geled, 1)

            def body(n, p, has_next):
                if has_next:
                    front(n + 1, 1 - p)
                act.wait_ge(s.clipped_b, n + 1)
                act.activation(ints_b, hid[p], ACT.Identity, bias=g.minus_round[:, :]).then_inc(s.low_b, 1)
                act.wait_ge(s.bt_full, n + 1)
                act.activation(intsT[p][:, :, :], BT[:, :].bitcast(BF16).rearrange("p (n q) -> p n q", n=HT),
                               ACT.Copy).then_inc(s.bt_ready, 1)

            per_batch(act, lambda: front(0, 0), body)

        @block.tensor
        def _(pe):
            def front(m, p):
                pe.wait_ge(s.low_a, m + 1)
                for t in range(NT):
                    last = pe.transpose(AT[:, 0:P].bitcast(BF16)[:, t * P:(t + 1) * P], ints_a[:, t, :], g.identh[:, :])
                last.then_inc(s.at_full, 1)
                pe.wait_ge(s.at_ready, m + 1)
                for t in range(NT):
                    pe.matmul(HB[2 * p + t][:, :], xTh[:, t * P:(t + 1) * P], cfg.w1[:, :], start=True, stop=True
                              ).then_inc(s.hidden_full, 1)

            def body(n, p, has_next):
                if has_next:
                    front(n + 1, 1 - p)
                pe.wait_ge(s.low_b, n + 1)
                for k in range(HT):
                    for t in range(NT):
                        last = pe.transpose(BT[:, :].bitcast(BF16)[:, k * T + t * P:k * T + (t + 1) * P],
                                            ints_b[:, t, k * P:(k + 1) * P], g.identh[:, :])
                last.then_inc(s.bt_full, 1)
                pe.wait_ge(s.bt_ready, n + 1)
                for t in range(NT):
                    for k in range(HT):
                        last = pe.matmul(OUT[p][:, t * P:(t + 1) * P], intsT[p][:, k, t * P:(t + 1) * P],
                                         cfg.w2[:, k, :], start=(k == 0), stop=(k == HT - 1))
                last.then_inc(s.out_full, 1)

            per_batch(pe, lambda: front(0, 0), body)



def routed_experts(nc, g, name, cfg, out):
    E = cfg.experts
    with ExitStack() as ctx:
        s = sem_space(nc, ctx, name, LN_SEMS + GATE_SEMS + " xt_full xt_ready experts_full summed_in "
                      "sentinels stored started")
        XT, LG, EX = g.bank[0:2], g.bank[2:4], g.bank[4:8]
        gb = g.gate
        out_v = out.rearrange("b (t p) c -> p (b t) c", p=P)
        block = ctx.enter_context(nc.Block())

        @block.sync
        def _(sp):
            def body(n, p, has_next):
                sp.wait_ge(s.summed_in, NT * E * (n + 1))
                dst = out_v[:, bass.ds(NT * n, NT), :] if not isinstance(n, int) else out_v[:, NT * n:NT * n + NT, :]
                sp.dma_start(dst, tokens(cfg.target, n)).then_inc(s.stored, 16)

            per_batch(sp, lambda: None, body)
            sp.wait_ge(s.stored, 16 * B)

        @block.vector
        def _(dve):
            dve.memset(gb.probs[:, :, :], -1.0)
            dve.memset(gb.keys[:, :, :], -1.0).then_inc(s.sentinels, 1)
            dve.wait_ge(s.sentinels, 1)

            def front(m, p):
                front_vector(dve, s, g, cfg, m, p)

            def tail(n, p):
                gate_vector(dve, s, g, cfg, n, p, LG[p])
                c = gb.c[p]
                dve.tensor_tensor(out=gb.w[:, :, 0:E], in0=c[:, :, 0:E], in1=gb.probs[:, :, 0:E], op=ALU.mult
                                  ).then_inc(s.pbias, 1)
                dve.wait_ge(s.pbias, n + 1)
                dve.tensor_reduce(gb.wsum[:, :], gb.w[:, :, 0:E], AX_X, ALU.add).then_inc(s.pbias_sum, 1)
                dve.wait_ge(s.pbias_sum, n + 1)
                for t in range(NT):
                    last = dve.tensor_scalar(g.resb[p][:, t, :], tile_of(cfg.residual, n, t)[:, 0, :],
                                             gb.wsum[:, t:t + 1], None, ALU.add)
                last.then_inc(s.started, 1)
                dve.wait_ge(s.started, n + 1)
                for e in range(E):
                    for t in range(NT):
                        if e % 4 == 0:
                            dve.wait_ge(s.experts_full, 4 * n + 2 * (e // 4) + t + 1)
                        if e:
                            dve.wait_ge(s.summed_in, NT * (E * n + e - 1) + t + 1)
                        acc = g.resb[p][:, t, :]
                        dst = acc if e < E - 1 else tile_of(cfg.target, n, t)[:, 0, :]
                        dve.scalar_tensor_tensor(out=dst, in0=EX[2 * (e // 4) + t][:, (e % 4) * P:(e % 4 + 1) * P],
                                                 scalar=c[:, t, e:e + 1], in1=acc, op0=ALU.mult, op1=ALU.add
                                                 ).then_inc(s.summed_in, 1)

            def body(n, p, has_next):
                if has_next:
                    front(n + 1, 1 - p)
                tail(n, p)

            per_batch(dve, lambda: front(0, 0), body)

        @block.gpsimd
        def _(pool):
            per_batch(pool, lambda: front_pool(pool, s, g, cfg, 0),
                      lambda n, p, nx: front_pool(pool, s, g, cfg, n + 1) if nx else None)

        @block.scalar
        def _(act):
            def front(m, p):
                act.wait_ge(s.xt_full, m + 1)
                act.activation(g.xT[p][:, :], XT[p][:, 0:T], ACT.Copy).then_inc(s.xt_ready, 1)

            def body(n, p, has_next):
                if has_next:
                    front(n + 1, 1 - p)
                gate_exp(act, s, g, cfg, n)

            per_batch(act, lambda: front(0, 0), body)

        @block.tensor
        def _(pe):
            cfg.loaded(pe)

            def front(m, p):
                wait_normed(pe, s, cfg, m)
                for t in range(NT):
                    last = pe.transpose(XT[p][:, t * P:(t + 1) * P], g.xn[p][:, t, :], g.ident[:, :])
                last.then_inc(s.xt_full, 1)
                pe.wait_ge(s.xt_ready, m + 1)
                for t in range(NT):
                    last = pe.matmul(LG[p][:, t * E:(t + 1) * E], g.xT[p][:, t * P:(t + 1) * P], cfg.gate_w[:, :],
                                     start=True, stop=True)
                last.then_inc(s.logits_full, 1)

            def body(n, p, has_next):
                if isinstance(n, int) and n > 0:
                    pe.wait_ge(s.summed_in, NT * E * n)
                if has_next:
                    front(n + 1, 1 - p)
                for k in range(2):
                    for t in range(NT):
                        pe.matmul(EX[2 * k + t][:, :], g.xT[p][:, t * P:(t + 1) * P],
                                  cfg.w[:, 4 * k * P:4 * (k + 1) * P], start=True, stop=True
                                  ).then_inc(s.experts_full, 1)

            per_batch(pe, lambda: front(0, 0), body)



def prepare(nc, g, w, dram):
    with ExitStack() as ctx:
        s = sem_space(nc, ctx, "prepare", "zeroed built")
        block = ctx.enter_context(nc.Block())

        @block.sync
        def _(sp):
            sp.dma_start(g.X[:, :, :], dram.x.rearrange("b (t p) c -> p (b t) c", p=P)).then_inc(w.sem_x, 16)
            for dst, src, sem in w.loads:
                sp.dma_start(dst, src).then_inc(sem, 16)
            sp.wait_ge(w.sem_x, 16)
            sp.wait_ge(w.sem_small, 16 * w.small_count)

        @block.gpsimd
        def _(pool):
            pool.memset(g.ident[:, :], 0.0)
            pool.memset(g.identh[:, :], 0.0)
            pool.memset(g.causal[:, :], 0.0)
            pool.memset(g.ones[:, :], 1.0)
            pool.memset(g.sel_head[:, :, :], 1.0)
            pool.memset(g.sel_pair[:, :, :], 1.0)
            for part in g.sel_part:
                pool.memset(part[:, :, :], 1.0)
            pool.memset(g.minus_half[:, :], -0.5)
            pool.memset(g.minus_round[:, :], -ROUND)
            pool.memset(g.negmax4[:, :, :, :], 0.0)
            for hm in g.head_mask.values():
                last = pool.memset(hm[:, :], 1.0)
            last.then_inc(s.zeroed, 1)
            pool.wait_ge(s.zeroed, 1)

            count = [0]

            def keep(view, cmp, fill, base, pattern, mult):
                pool.affine_select(out=view, in_=view, compare_op=cmp, fill=fill, base=base, pattern=pattern,
                                   channel_multiplier=mult).then_inc(s.built, 1)
                count[0] += 1
                pool.wait_ge(s.built, count[0])

            for ident in (g.ident, g.identh):
                keep(ident[:, :], ALU.not_equal, 1.0, 0, [[-1, P]], 1)
            keep(g.causal[:, :], ALU.is_ge, MASKED, 0, [[-1, P]], 1)
            keep(g.sel_head[:, :, :].rearrange("p (g j) k -> p g j k", g=G), ALU.is_equal, 0.0, 0,
                 [[-HG, G], [-(SLOT + 1), HG], [0, P]], 1)
            keep(g.sel_pair[:, :, :].rearrange("p j (i k) -> p j i k", i=2), ALU.is_equal, 0.0, 0,
                 [[-2, PAIRS], [-1, 2], [0, TC]], 1)
            for part in range(3):
                view = g.sel_part[part][:, :, :].rearrange("p j (i k) -> p j i k", i=2)
                keep(view, ALU.is_equal, 0.0, -16 * part, [[-2, PAIRS], [-1, 2], [0, 64]], 1)
            for D, hm in g.head_mask.items():
                keep(hm[:, :], ALU.is_ge, 0.0, 0, [[-D, P // D]], 1)
                keep(hm[:, :], ALU.is_ge, 0.0, D - 1, [[D, P // D]], -1)
            pool.tensor_tensor(out=g.sel_part[0][:, :, :], in0=g.sel_part[0][:, :, :], in1=g.sel_part[1][:, :, :],
                               op=ALU.add).then_inc(s.built, 1)
            pool.wait_ge(s.built, count[0] + 1)
            pool.tensor_tensor(out=g.sel_expert[:, :, :], in0=g.sel_part[0][0:48, :, :], in1=g.sel_part[2][0:48, :, :],
                               op=ALU.add).then_inc(s.built, 1)


def load_later(block, cfg):
    if cfg.loads:
        @block.sync
        def _(sp):
            for dst, src, sem in cfg.loads:
                sp.dma_start(dst, src).then_inc(sem, 16)


def normalise_context(nc, g, w, v):
    n = B * TC // P
    with ExitStack() as ctx:
        s = sem_space(nc, ctx, "context", "stats mean veps rstd norm full done")
        raw, st, mv, ve, rs = g.ctx_tok, g.ctx_stats, g.ctx_mv, g.ctx_veps, g.ctx_rstd
        block = ctx.enter_context(nc.Block())

        @block.vector
        def _(dve):
            dve.wait_ge(w.sem_ctx, 32)
            for t in range(n):
                dve.bn_stats(st[:, t, :], raw[:, t, :]).then_inc(s.stats, 1)
            dve.wait_ge(s.stats, n)
            for t in range(n):
                dve.bn_aggr(mv[:, t, :], st[:, t, :]).then_inc(s.mean, 1)
            dve.wait_ge(s.rstd, 1)
            for t in range(n):
                dve.tensor_scalar(raw[:, t, :], raw[:, t, :], mv[:, t, 0:1], rs[:, t:t + 1], ALU.subtract, ALU.mult
                                  ).then_inc(s.norm, 1)

        @block.gpsimd
        def _(pool):
            pool.wait_ge(s.mean, n)
            pool.tensor_scalar(ve[:, :], mv[:, :, 1], EPS, None, ALU.add).then_inc(s.veps, 1)
            pool.wait_ge(s.veps, 1)
            pool.memset(g.ctx_half[:, :], -0.5).then_inc(s.veps, 1)
            pool.wait_ge(s.veps, 2)
            pool.tensor_tensor(out=rs[:, :], in0=ve[:, :], in1=g.ctx_half[:, :], op=ALU.pow).then_inc(s.rstd, 1)

        @block.tensor
        def _(pe):
            pe.wait_ge(s.norm, n)
            for t in range(n):
                mm = pe.transpose(g.bank[t // 4][0:CC, (t % 4) * P:(t % 4 + 1) * P], raw[:, t, :], g.ident[:, :])
                if t % 4 == 3:
                    mm.then_inc(s.full, 1)

        @block.scalar
        def _(act):
            for k in range(n // 4):
                act.wait_ge(s.full, k + 1)
                act.activation(g.ctxnT[:, k * 4 * NT:(k + 1) * 4 * NT, :],
                               g.bank[k][0:CC, :].rearrange("p (b k) -> p b k", k=TC),
                               ACT.Identity, scale=v.ctx_gain, bias=v.ctx_shift).then_inc(s.done, 1)


def ternary_weights(nc, g, name, w, sem, value, pairs, mode):
    with ExitStack() as ctx:
        s = sem_space(nc, ctx, name, "sums total mean recip scaled rounded clipped")
        block = ctx.enter_context(nc.Block())
        k = len(pairs)

        @block.vector
        def _(dve):
            dve.wait_ge(sem, value)
            for i, (src, _dst, _level) in enumerate(pairs):
                dve.tensor_reduce(g.tern_sum[:, i:i + 1], src, AX_X, ALU.add, apply_absolute_value=True
                                  ).then_inc(s.sums, 1)
            dve.wait_ge(s.total, 1)
            scale = 1.0 / (C * 512)
            for i, (_src, _dst, level) in enumerate(pairs):
                dve.tensor_scalar(level, g.bank[0][:, i:i + 1], scale, EPS, ALU.mult,
                                  ALU.add if mode == "added" else ALU.max).then_inc(s.mean, 1)
            dve.wait_ge(s.mean, k)
            for i, (_src, _dst, level) in enumerate(pairs):
                dve.reciprocal(g.tern_recip[:, i:i + 1], level).then_inc(s.recip, 1)
            dve.wait_ge(s.recip, k)
            for i, (src, _dst, _level) in enumerate(pairs):
                dve.tensor_scalar(src, src, g.tern_recip[:, i:i + 1], ROUND, ALU.mult, ALU.add).then_inc(s.scaled, 1)
            dve.wait_ge(s.scaled, k)
            for src, _dst, _level in pairs:
                dve.tensor_scalar(src, src, ROUND, 1.0, ALU.subtract, ALU.min).then_inc(s.rounded, 1)
            dve.wait_ge(s.rounded, k)
            for src, dst, _level in pairs:
                dve.tensor_scalar(dst, src, -1.0, None, ALU.max).then_inc(s.clipped, 1)

        @block.tensor
        def _(pe):
            pe.wait_ge(s.sums, k)
            pe.matmul(g.bank[0][:, 0:k], g.ones[:, :], g.tern_sum[:, 0:k], start=True, stop=True).then_inc(s.total, 1)


ROWS = ["L0_xattn_bv", "L0_xattn_bcv", "L0_xattn_bp", "L1_xattn_ln1_g", "L1_xattn_ln1_b", "L1_xattn_ln2_g",
        "L1_xattn_ln2_b", "L1_xattn_a1_li1_b", "L1_xattn_a1_li3_b", "L1_xattn_a2_li1_b", "L1_xattn_a2_li3_b",
        "L1_ffn_b2", "L2_ffn_ln1_g", "L2_ffn_ln1_b", "L2_ffn_b1", "L2_ffn_ln2_g", "L2_ffn_ln2_b", "L2_ffn_b2",
        "L3_xattn_bo"]


def build(nc, dram, cols, rows):
    with ExitStack() as ctx:
        def sb(name, shape, dt=F32):
            return ctx.enter_context(nc.sbuf_tensor(name, shape, dt))

        def sem(name):
            return ctx.enter_context(nc.semaphore(name))

        def two(name, shape, dt=F32):
            return [sb(f"{name}{p}", shape, dt) for p in range(2)]

        g = Store()
        g.X, g.A, g.XA = (sb(n, [P, B * NT, C]) for n in ("X", "A", "XA"))
        g.xn, g.xT, g.yT, g.resb = two("xn", [P, NT, C]), two("xT", [P, T]), two("yT", [P, T]), two("resb", [P, NT, C])
        g.qT, g.qh = two("qT", [P, 8 * T]), two("qh", [P, 8 * T], BF16)
        g.kT, g.kh = two("kT", [P, G * T]), two("kh", [P, G * T], BF16)
        g.V = two("V", [P, NT * H * (SLOT + 1)])
        g.kmask, g.kmaskh = g.kT, g.kh
        g.ctxb = two("ctxb", [CC, 2, TC])
        g.prob = [sb(f"prob{i}", [P, 512]) for i in range(3)]
        g.probm = [sb(f"probm{i}", [P, NT, P]) for i in range(3)]
        g.silu = g.yT
        g.osb, g.oT = sb("osb", [P, NT * H * 64]), sb("oT", [P, 8 * T])
        g.negmax, g.negmax4 = sb("negmax", [P, NT, H]), sb("negmax4", [P, NT, 4, SLOT], BF16)
        g.negmaxT = two("negmaxT", [P, T], BF16)
        g.recip, g.recip16 = sb("recip", [P, NT, 8]), sb("recip16", [P, NT, H])
        g.stats = [sb(f"stats{k}", [P, NT, 6]) for k in range(3)]
        g.mv = [sb(f"mv{k}", [P, NT, 2]) for k in range(3)]
        g.veps = [sb(f"veps{k}", [P, NT]) for k in range(3)]
        g.rstd = [sb(f"rstd{k}", [P, NT]) for k in range(3)]
        g.mvh, g.rstdh = sb("mvh", [P, NT, 2]), sb("rstdh", [P, NT])
        g.ident, g.identh = sb("ident", [P, P]), sb("identh", [P, P], BF16)
        g.causal, g.ones = sb("causal", [P, P], BF16), sb("ones", [P, P])
        g.sel_head, g.sel_pair = sb("sel_head", [P, H, P], BF16), sb("sel_pair", [P, PAIRS, P], BF16)
        g.sel_part = [g.qT[0][:, :].bitcast(BF16)[:, i * PAIRS * P:(i + 1) * PAIRS * P]
                      .rearrange("p (j k) -> p j k", j=PAIRS) for i in range(3)]
        g.sel_expert = sb("sel_expert", [48, PAIRS, P], BF16)
        g.head_mask = {D: sb(f"head_mask{D}", [P, P // D]) for D in (8, 32, 64)}
        g.minus_half, g.minus_round = sb("minus_half", [P, NT]), sb("minus_round", [P, 1])
        g.gate = record(
            nmax=sb("g_nmax", [P, NT]), e=sb("g_e", [P, NT, 16]), sum=sb("g_sum", [P, NT]), rsum=sb("g_rsum", [P, NT]),
            probs=sb("g_probs", [P, NT, 24]), top=sb("g_top", [P, NT, 8]), keys=sb("g_keys", [P, NT, 8]),
            marked=sb("g_marked", [P, NT, 24]), w=sb("g_w", [P, NT, 16]), wsum=sb("g_wsum", [P, NT]),
            wguard=sb("g_wguard", [P, NT]), wrecip=sb("g_wrecip", [P, NT]), c=two("g_c", [P, NT, 16]),
            part=two("g_part", [P, NT, 3, 16], BF16), rest=sb("g_rest", [P, 1, NT, 16]))
        g.combT = g.XA[0:48, :, :].rearrange("p t c -> p (t c)").bitcast(BF16)[:, 0:B * T]
        n_ctx = B * TC // P
        g.ctx_tok, g.ctx_stats = sb("ctx_tok", [P, n_ctx, CC]), sb("ctx_stats", [P, n_ctx, 6])
        g.ctx_mv, g.ctx_veps = sb("ctx_mv", [P, n_ctx, 2]), sb("ctx_veps", [P, n_ctx])
        g.ctx_rstd, g.ctx_half = sb("ctx_rstd", [P, n_ctx]), sb("ctx_half", [P, n_ctx])
        g.ctxnT, ctxT = sb("ctxnT", [CC, B, TC]), sb("ctxT", [CC, B, TC])
        g.tern_sum, g.tern_recip = sb("tern_sum", [P, 2]), sb("tern_recip", [P, 2])
        g.bank = [ctx.enter_context(nc.psum_tensor(f"bank{i}", [P, 512], F32)) for i in range(8)]

        w = record(loads=[], sem_x=sem("x_loaded"), sem_small=sem("small_loaded"), sem_ctx=sem("ctx_loaded"),
                            small_count=2)
        row_tile = sb("row_tile", [P, dram.rows.shape[0]])
        col_tile = sb("col_tile", [P, dram.cols.shape[1]])
        w.loads.extend([(row_tile[:, :], dram.rows.partition_broadcast(P), w.sem_small), (col_tile[:, :], dram.cols, w.sem_small),
                    (ctxT[:, :, :], dram.ctxT, w.sem_ctx),
                    (g.ctx_tok[:, :, :], dram.ctx.rearrange("b k c -> (b k) c").rearrange("(n p) c -> p n c", p=P), w.sem_ctx)])

        def row(name):
            a, n = rows[name]
            return row_tile[:, a:a + n]

        def col(name, count=1):
            a, _ = cols[name]
            return col_tile[:, a:a + count]

        layer = [(sem(f"weights{i}_loaded"), [0]) for i in range(7)]
        later = {k: [] for k in range(3, 7)}

        flat = lambda x: x[:, :, :].rearrange("p t c -> p (t c)")
        first, second = sb("weights_first", [P, 5120]), sb("weights_second", [P, 3072])
        region = {0: first[:, :], 1: first[:, :], 2: second[:, :], 3: first[:, :], 4: second[:, :], 5: flat(g.A),
                  6: flat(g.XA)}
        starts = {0: 0, 2: 0, 3: 0, 4: 0, 5: 0, 6: 0}

        def weight(name, k, shape):
            src = dram.weights[name]
            start = 0 if k == 1 else k
            n = int(np.prod(shape[1:]))
            at = starts[start]
            starts[start] += n
            assert starts[start] <= region[k].shape[1], name
            view = region[k][0:shape[0], at:at + n]
            if len(shape) == 3:
                view = view.rearrange("p (k c) -> p k c", k=shape[1])
            (w.loads if k <= 2 else later[k]).append((view, src, layer[k][0]))
            layer[k][1][0] += 16
            return view

        def loaded(k, and_ctx=False):
            def wait_for(eng):
                eng.wait_ge(layer[k][0], layer[k][1][0])
                if and_ctx:
                    eng.wait_ge(w.sem_ctx, 32)
            return wait_for

        W = record(
            q0=weight("L0_q", 0, [P, G * P]), k0=weight("L0_k", 0, [P, G * P]), v0=weight("L0_v", 0, [P, P]),
            cq0=weight("L0_cq", 0, [P, P]), ck0=weight("L0_ck", 0, [CC, P]), cv0=weight("L0_cv", 0, [CC, P]),
            p0=weight("L0_p", 0, [P, 1, C]),
            gate0=weight("L0_gate", 1, [P, 16]), w10=weight("L0_w1", 1, [P, 1024]), w30=weight("L0_w3", 1, [P, 1024]),
            w20=weight("L0_w2", 1, [P, 8, C]), sw1=weight("L0_sw1", 1, [P, 64]), sw3=weight("L0_sw3", 1, [P, 64]),
            sw2=weight("L0_sw2", 1, [64, C]),
            q1=weight("L1_q1", 2, [P, 512]), k1=weight("L1_k1", 2, [P, 512]), v1=weight("L1_v1", 2, [P, 512]),
            o1=weight("L1_o1", 2, [P, 4, C]), f1=weight("L1_f1", 2, [P, 512]), e1=weight("L1_e1", 2, [P, 4, C]),
            q2=weight("L1_q2", 3, [P, 512]), k2=weight("L1_k2", 3, [CC, 512]), v2=weight("L1_v2", 3, [CC, 512]),
            o2=weight("L1_o2", 3, [P, 4, C]), f2=weight("L1_f2", 3, [P, 512]), e2=weight("L1_e2", 3, [P, 4, C]),
            t1=weight("L1_w1", 3, [P, 512]), t2=weight("L1_w2", 3, [P, 4, C]),
            l2q=weight("L2_q", 4, [P, P]), l2k=weight("L2_k", 4, [CC, P]), l2v=weight("L2_v", 4, [CC, P]),
            l2o=weight("L2_o", 4, [P, 1, C]), l2w1=weight("L2_w1", 4, [P, 512]), l2w2=weight("L2_w2", 4, [P, 4, C]),
            q3=weight("L3_q", 5, [P, 1024]), k3=weight("L3_k", 5, [CC, 1024]), v3=weight("L3_v", 5, [CC, 1024]),
            o3=weight("L3_o", 5, [P, 8, C]), gate3=weight("L3_gate", 6, [P, 8]), w3=weight("L3_w", 6, [P, 8 * C]))
        w1q, w2q = sb("w1q", [P, 512], BF16), sb("w2q", [P, 4, C], BF16)
        levels = sb("levels", [P, 4])
        for k in "ab":
            buf = record(peak=sb(f"peak_{k}", [P, NT]), peakc=sb(f"peakc_{k}", [P, NT]),
                                  recip=sb(f"qrecip_{k}", [P, NT]), scale=sb(f"qscale_{k}", [P, NT]),
                                  level=two(f"level_{k}", [P, NT]),
                                  wlevel=levels[:, 2:3] if k == "a" else levels[:, 3:4])
            if k == "a":
                g.quant_a = buf
            else:
                g.quant_b = buf

        plain = [(None, None, None)]
        att = dict(q_gain=None, q_shift=None, kv_gain=None, kv_shift=None, bq=None, bk=None, bv=None, bias=None,
                   wide_v=0, causal=False, norms=plain, loads=())
        prepare(nc, g, w, dram)
        self_attention(nc, g, "own0", record(**(att | dict(
            source=g.X, residual=g.X, target=g.A, D=8, scale=8 ** -0.5, causal=True, wq=W.q0, wk=W.k0, wv=W.v0, wo=W.p0,
            bq=col("bq", 4), bk=col("bk", 4), bv=row("L0_xattn_bv"), bias=row("L0_xattn_bp"), loaded=loaded(0)))))
        cross_attention(nc, g, "ctx0", record(**(att | dict(
            source=g.X, residual=g.A, target=g.A, D=8, scale=8 ** -0.5, ctxT=ctxT, wq=W.cq0, wk=W.ck0, wv=W.cv0, wo=W.p0,
            bq=col("bcq"), bk=col("bck"), bv=row("L0_xattn_bcv"), head_mask=g.head_mask[8], loaded=loaded(0, True)))))
        moe0 = dict(source=g.A, norms=plain, experts=16, top=4, guard=0.0, loaded=loaded(1), loads=())
        route(nc, g, "route0", record(**moe0, gate_w=W.gate0))
        gated_experts(nc, g, "moe0", record(**moe0, residual=g.A, target=g.X, w1=W.w10, w3=W.w30, w2=W.w20,
                                                     sw1=W.sw1, sw3=W.sw3, sw2=W.sw2))
        a1, a2 = "L1_xattn_a1_", "L1_xattn_a2_"
        self_attention(nc, g, "own1", record(**(att | dict(
            source=g.X, residual=g.XA, target=g.A, D=32, scale=32 ** -0.5, wide_v=1,
            norms=[(None, None, None), (row("L1_xattn_ln1_g"), row("L1_xattn_ln1_b"), g.XA), (None, None, None)],
            wq=W.q1, wk=W.k1, wv=W.v1, wo=W.o1, q_gain=col(a1 + "lnx_g"), q_shift=col(a1 + "lnx_b"),
            kv_gain=col(a1 + "lny_g"), kv_shift=col(a1 + "lny_b"), bias=row(a1 + "li1_b"), loaded=loaded(2), loads=later[3]))))
        feed_forward(nc, g, "net1", record(
            source=g.A, norms=plain, residuals=[g.A, g.XA], target=g.A, relu=False, x_gain=col(a1 + "ln3_g"),
            x_shift=col(a1 + "ln3_b"), w1=W.f1, b1=col(a1 + "li2_b", 4), w2=W.e1, bias=row(a1 + "li3_b"), loaded=loaded(2), loads=()))
        normalise_context(nc, g, w, record(ctx_gain=col(a2 + "lny_g")[0:CC, :], ctx_shift=col(a2 + "lny_b")[0:CC, :]))
        cross_attention(nc, g, "ctx1", record(**(att | dict(
            source=g.A, residual=g.XA, target=g.A, D=32, scale=32 ** -0.5, ctxT=g.ctxnT,
            norms=[(row("L1_xattn_ln2_g"), row("L1_xattn_ln2_b"), g.XA), (None, None, None)],
            wq=W.q2, wk=W.k2, wv=W.v2, wo=W.o2, q_gain=col(a2 + "lnx_g"), q_shift=col(a2 + "lnx_b"),
            bias=row(a2 + "li1_b"), head_mask=g.head_mask[32], loaded=loaded(3), loads=later[4]))))
        feed_forward(nc, g, "net2", record(
            source=g.A, norms=plain, residuals=[g.A, g.XA, g.X], target=g.X, relu=False, x_gain=col(a2 + "ln3_g"),
            x_shift=col(a2 + "ln3_b"), w1=W.f2, b1=col(a2 + "li2_b", 4), w2=W.e2, bias=row(a2 + "li3_b"), loaded=loaded(3), loads=()))
        ternary_weights(nc, g, "tern1", w, layer[3][0], layer[3][1][0],
                        [(W.t1[:, :], W.t1[:, :], levels[:, 0:1]),
                         (W.t2[:, :, :].rearrange("p k c -> p (k c)"), W.t2[:, :, :].rearrange("p k c -> p (k c)"),
                          levels[:, 1:2])], "added")
        feed_forward(nc, g, "net3", record(
            source=g.X, norms=plain, residuals=[g.X], target=g.X, relu=True, x_gain=None, x_shift=None,
            w1=W.t1, b1=col("L1_ffn_b1", 4), w2=W.t2, bias=row("L1_ffn_b2"), loaded=loaded(3), loads=later[5] + later[6]))
        cross_attention(nc, g, "ctx2", record(**(att | dict(
            source=g.X, residual=g.X, target=g.X, D=8, scale=8 ** -0.5, ctxT=ctxT, wq=W.l2q, wk=W.l2k, wv=W.l2v,
            wo=W.l2o, head_mask=g.head_mask[8], loaded=loaded(4)))))
        ternary_weights(nc, g, "tern2", w, layer[4][0], layer[4][1][0],
                        [(W.l2w1[:, :], w1q[:, :], levels[:, 2:3]),
                         (W.l2w2[:, :, :].rearrange("p k c -> p (k c)"), w2q[:, :, :].rearrange("p k c -> p (k c)"),
                          levels[:, 3:4])], "clipped")
        quantised_feed_forward(nc, g, "net4", record(
            source=g.X, residual=g.X, target=g.X, norms=[(None, None, None), (row("L2_ffn_ln1_g"), row("L2_ffn_ln1_b"), None)],
            w1=w1q, b1=row("L2_ffn_b1"), gain2=row("L2_ffn_ln2_g"), shift2=row("L2_ffn_ln2_b"), w2=w2q,
            bias=row("L2_ffn_b2"), loads=()))
        cross_attention(nc, g, "ctx3", record(**(att | dict(
            source=g.X, residual=g.X, target=g.X, D=64, scale=64 ** -0.5, ctxT=ctxT, wq=W.q3, wk=W.k3, wv=W.v3,
            wo=W.o3, bias=row("L3_xattn_bo"), head_mask=g.head_mask[64], loaded=loaded(5)))))
        routed_experts(nc, g, "moe3", record(
            source=g.X, residual=g.X, target=g.X, norms=plain, experts=8, top=2, guard=1e-6, gate_w=W.gate3, w=W.w3,
            loaded=loaded(6)), dram.out)


def kernel(**inputs):
    import concourse.bacc as bacc
    from concourse.bass_utils import run_bass_kernel_spmd

    v = {k: np.asarray(a) for k, a in inputs.items()}

    def slots(a):
        out = np.zeros((*a.shape[:-1], G, HG, SLOT), a.dtype)
        out[..., 0:8] = a.reshape(*a.shape[:-1], G, HG, 8)
        return out.reshape(*a.shape[:-1], G * P)

    def heads(a):
        return a.transpose(1, 0, 2).reshape(a.shape[1], -1)

    def tiles(a):
        return a.reshape(-1, P, a.shape[-1]).transpose(1, 0, 2)

    a1, a2 = "L1_xattn_a1_", "L1_xattn_a2_"
    weights = {
        "L0_q": slots(v["L0_xattn_Wq"]), "L0_k": slots(v["L0_xattn_Wk"]), "L0_v": v["L0_xattn_Wv"],
        "L0_cq": v["L0_xattn_Wcq"], "L0_ck": v["L0_xattn_Wck"], "L0_cv": v["L0_xattn_Wcv"],
        "L0_p": tiles(v["L0_xattn_Wp"]), "L0_gate": v["L0_ffn_gate_w"].T,
        "L0_w1": v["L0_ffn_w1"].reshape(1024, C).T, "L0_w3": v["L0_ffn_w3"].reshape(1024, C).T,
        "L0_w2": tiles(v["L0_ffn_w2"].transpose(0, 2, 1).reshape(1024, C)),
        "L0_sw1": v["L0_ffn_sw1"].T, "L0_sw3": v["L0_ffn_sw3"].T, "L0_sw2": v["L0_ffn_sw2"].T,
        "L1_q1": heads(v[a1 + "wq"]), "L1_k1": heads(v[a1 + "wk"]), "L1_v1": heads(v[a1 + "wv"]),
        "L1_o1": tiles(v[a1 + "li1_w"]), "L1_f1": v[a1 + "li2_w"], "L1_e1": tiles(v[a1 + "li3_w"]),
        "L1_q2": heads(v[a2 + "wq"]), "L1_k2": heads(v[a2 + "wk"]), "L1_v2": heads(v[a2 + "wv"]),
        "L1_o2": tiles(v[a2 + "li1_w"]), "L1_f2": v[a2 + "li2_w"], "L1_e2": tiles(v[a2 + "li3_w"]),
        "L1_w1": v["L1_ffn_W1"].T, "L1_w2": tiles(v["L1_ffn_W2"].T),
        "L2_q": v["L2_xattn_Wq"].T, "L2_k": v["L2_xattn_Wkv"][0:P].T, "L2_v": v["L2_xattn_Wkv"][P:2 * P].T,
        "L2_o": tiles(v["L2_xattn_Wo"].T), "L2_w1": v["L2_ffn_w1"].T, "L2_w2": tiles(v["L2_ffn_w2"].T),
        "L3_q": v["L3_xattn_Wq"], "L3_k": v["L3_xattn_Wk"], "L3_v": v["L3_xattn_Wv"], "L3_o": tiles(v["L3_xattn_Wo"]),
        "L3_gate": v["L3_ffn_router_w"].T, "L3_w": v["L3_ffn_expert_weights"].transpose(1, 0, 2).reshape(P, 8 * C),
    }
    columns = {"bq": slots(v["L0_xattn_bq"]).reshape(G, P).T, "bk": slots(v["L0_xattn_bk"]).reshape(G, P).T,
               "bcq": v["L0_xattn_bcq"][:, None], "bck": v["L0_xattn_bck"][:, None],
               "L1_ffn_b1": v["L1_ffn_b1"].reshape(4, P).T}
    for a in (a1, a2):
        for n in ("lnx_g", "lnx_b", "lny_g", "lny_b", "ln3_g", "ln3_b"):
            x = v[a + n]
            columns[a + n] = np.concatenate([x, np.zeros(P - len(x), x.dtype)])[:, None]
        columns[a + "li2_b"] = v[a + "li2_b"].reshape(4, P).T
    cols, rows, at = {}, {}, 0
    for n, x in columns.items():
        cols[n] = (at, x.shape[1])
        at += x.shape[1]
    at = 0
    for n in ROWS:
        rows[n] = (at, v[n].shape[0])
        at += v[n].shape[0]

    nc = bacc.Bacc("TRN2", target_bir_lowering=False, num_devices=1)
    arrays = {}

    def feed(name, a):
        a = np.ascontiguousarray(a)
        arrays["in_" + name] = a
        return nc.dram_tensor("in_" + name, a.shape, mybir.dt.from_np(a.dtype), kind="ExternalInput").ap()

    dram = record(
        x=feed("x", v["x"]), ctx=feed("ctx", v["ctx_512"]), ctxT=feed("ctxT", v["ctx_512"].transpose(2, 0, 1)),
        cols=feed("cols", np.concatenate(list(columns.values()), axis=1)),
        rows=feed("rows", np.concatenate([v[n] for n in ROWS])),
        weights={n: feed(n, a) for n, a in weights.items()},
        out=nc.dram_tensor("out_x", (B, T, C), F32, kind="ExternalOutput").ap())
    build(nc, dram, cols, rows)
    r = run_bass_kernel_spmd(nc, [arrays], core_ids=[0])
    return r.results[0]["out_x"]
```

```python
from collections import namedtuple
from contextlib import ExitStack, contextmanager

import numpy as np

import concourse.bass as bass
from concourse import mybir

F32 = mybir.dt.float32
BF16 = mybir.dt.bfloat16
ALU = mybir.AluOpType
ACT = mybir.ActivationFunctionType
AX_X = mybir.AxisListType.X

P = 128
B, T, C = 16, 256, 128
NT = T // P
TC, CC = 64, 64
H = 16
SLOT = 32
HG = P // SLOT
G = H // HG
PAIRS = H // 2
EPS = 1e-5
MASKED = -1e30
ROUND = 1.5 * 2.0 ** 23


class Store:
    pass


def record(**fields):
    return namedtuple("record", fields)(**fields)


def per_element(eng, prologue, body):
    prologue()
    with eng.Fori(0, B // 2 - 1) as pair:
        body(2 * pair, 0, True)
        body(2 * pair + 1, 1, True)
    body(B - 2, 0, True)
    body(B - 1, 1, False)


def per_batch(eng, prologue, body, epilogue=None):
    prologue()
    body(0, 0)
    with eng.Fori(0, (B - 4) // 2) as pair:
        body(2 * pair + 1, 1)
        body(2 * pair + 2, 0)
    for n in range(B - 3, B):
        body(n, n % 2)
    if epilogue:
        epilogue()


def has(n, ahead):
    return not isinstance(n, int) or 0 <= n + ahead < B


def wait(eng, sem, value):
    if not isinstance(value, int) or value > 0:
        eng.wait_ge(sem, value)


def wait_apart(eng, sem, value):
    eng.wait_ge(sem, value)
    eng.nop(nofuse=True)


def bank_uses(front, middle, tail):
    def before(step, m, k):
        if step == "tail":
            done = m + 1 if isinstance(m, int) and m == B - 1 else m + 2
            return (front + middle) * done + tail * m + k
        ahead = front if step == "middle" else 0
        if isinstance(m, int) and m == 0:
            return ahead + k
        return (front + middle) * m + tail * (m - 1) + ahead + k
    return before


def bank_order(events):
    front = sum(a == 1 for _, a in events)
    own = sum(a == 0 for _, a in events)

    def before(name, element):
        i, ahead = next((i, a) for i, (e, a) in enumerate(events) if e == name)
        body = element - ahead
        same = sum(has(body, a) for _, a in events[:i]) if not isinstance(body, int) or 0 <= body < B else \
            sum(a == ahead for _, a in events[:i])
        if isinstance(body, int) and body <= 0:
            return front * (body + 1) + same
        done = 2 * front + own + len(events) * (body - 1) + same
        return done - front if isinstance(body, int) and body == B else done
    return before


def tokens(array, n):
    return array[:, bass.ds(NT * n, NT), :] if not isinstance(n, int) else array[:, NT * n:NT * n + NT, :]


def tile_of(array, n, t):
    at = NT * n + t
    return array[:, bass.ds(at, 1), :] if not isinstance(at, int) else array[:, at:at + 1, :]


@contextmanager
def stage_semaphores(nc, prefix, names):
    sems = {s: nc.alloc_semaphore(f"{prefix}_{s}") for s in names.split()}
    yield record(**sems)
    nc.clear_and_free_semaphores(list(sems.values()))
    nc.all_engine_barrier()


def sem_space(nc, ctx, prefix, names):
    return ctx.enter_context(stage_semaphores(nc, prefix, names))



LN_SEMS = " ".join(f"{s}{k}" for k in range(3) for s in ("stats", "mean", "veps", "rstd", "norm", "gain", "shift"))


def ln_sems(s, k):
    return [(s.stats0, s.mean0, s.rstd0, s.norm0), (s.stats1, s.mean1, s.rstd1, s.norm1),
            (s.stats2, s.mean2, s.rstd2, s.norm2)][k]


def ln_pool(pool, s, buf, k, n):
    _, mean, rstd, _ = ln_sems(s, k)
    veps = (s.veps0, s.veps1, s.veps2)[k]
    wait_apart(pool, mean, NT * (n + 1))
    pool.tensor_scalar(buf.veps[k][:, :], buf.mv[k][:, :, 1], EPS, None, ALU.add).then_inc(veps, 1)
    pool.wait_ge(veps, n + 1)
    pool.tensor_tensor(out=buf.rstd[k][:, :], in0=buf.veps[k][:, :], in1=buf.minus_half[:, :],
                       op=ALU.pow).then_inc(rstd, 1)


def ln_chain(s, g, cfg, n, p):
    src = [tile_of(cfg.source, n, t)[:, 0, :] for t in range(NT)]
    out = []
    for k, (gain, shift, keep) in enumerate(cfg.norms):
        last = k == len(cfg.norms) - 1
        dst = ([g.xn[p][:, t, :] for t in range(NT)] if last or keep is None
               else [tile_of(keep, n, t)[:, 0, :] for t in range(NT)])
        out.append((src, dst, gain, shift))
        src = dst
    return out


def ln_steps(dve, s, g, cfg, n, p):
    steps = []
    for k, (src, dst, gain, shift) in enumerate(ln_chain(s, g, cfg, n, p)):
        stats, mean, rstd, norm = ln_sems(s, k)
        gs, ss = [(s.gain0, s.shift0), (s.gain1, s.shift1), (s.gain2, s.shift2)][k]

        def gather(k=k, src=src, stats=stats, mean=mean):
            for t in range(NT):
                dve.bn_stats(g.stats[k][:, t, :], src[t]).then_inc(stats, 1)
            wait_apart(dve, stats, NT * (n + 1))
            for t in range(NT):
                dve.bn_aggr(g.mv[k][:, t, :], g.stats[k][:, t, :]).then_inc(mean, 1)

        def apply(k=k, src=src, dst=dst, mean=mean, rstd=rstd, norm=norm, last=gain is None):
            dve.wait_ge(mean, NT * (n + 1))
            dve.wait_ge(rstd, n + 1)
            for t in range(NT):
                dve.tensor_scalar(dst[t], src[t], g.mv[k][:, t, 0:1], g.rstd[k][:, t:t + 1],
                                  ALU.subtract, ALU.mult).then_inc(norm, 1)
            if last:
                wait_apart(dve, norm, NT * (n + 1))

        def scale(dst=dst, gain=gain, norm=norm, gs=gs):
            dve.wait_ge(norm, NT * (n + 1))
            for t in range(NT):
                dve.tensor_tensor(out=dst[t], in0=dst[t], in1=gain, op=ALU.mult).then_inc(gs, 1)

        def move(dst=dst, shift=shift, gs=gs, ss=ss):
            dve.wait_ge(gs, NT * (n + 1))
            for t in range(NT):
                dve.tensor_tensor(out=dst[t], in0=dst[t], in1=shift, op=ALU.add).then_inc(ss, 1)
            wait_apart(dve, ss, NT * (n + 1))

        steps += [gather, apply] + ([scale, move] if gain is not None else [])
    return steps


def front_vector(dve, s, g, cfg, n, p):
    for step in ln_steps(dve, s, g, cfg, n, p):
        step()


def spread_over(steps, slots):
    return {slot: [step for i, step in enumerate(steps) if slots[i * len(slots) // len(steps)] == slot]
            for slot in slots}


def front_pool(pool, s, g, cfg, n):
    for k in range(len(cfg.norms)):
        ln_pool(pool, s, g, k, n)


def wait_normed(eng, s, cfg, n):
    k = len(cfg.norms) - 1
    if cfg.norms[k][0] is not None:
        eng.wait_ge((s.shift0, s.shift1, s.shift2)[k], NT * (n + 1))
    else:
        eng.wait_ge(ln_sems(s, k)[3], NT * (n + 1))



def self_attention(nc, g, name, cfg):
    D = cfg.D
    a_events = ["x", "q", "k"] + ["v"] * cfg.wide_v + ["shift"]
    fa = bank_order([(e, 1) for e in a_events])
    fb = bank_order([("out", -1), ("q", 1), ("k", 1), ("v", 1)])
    pieces = [(0, j, 0, 4, P) for j in range(HG)] if cfg.causal else []
    pieces += [(qt, j, i, 2, T) for qt in range(1 if cfg.causal else 0, 2) for j in range(HG) for i in (0, 2)]
    NPC = len(pieces)
    AT = dict(x=1, out=2, qb=3, qa=4, kb=5, ka=6, v=7, pieces=8, shift=15)
    piece_at = {h: [i for i in range(NPC) if AT["pieces"] + i * 7 // NPC == h] for h in range(H)}
    SW = 384 if cfg.causal else 512
    K1 = 256
    K1Q = P if cfg.causal else 0
    with ExitStack() as ctx:
        s = sem_space(nc, ctx, name, LN_SEMS + " a_full a_free b_full b_free max_full max_free "
                      "negmax_ready scores_ready exp_done masked pv_done recip_done low_a "
                      "heads_normed ones_ready bias_added summed")
        qT = [g.qT[p][:, 0:G * T].rearrange("p (g q) -> p g q", g=G) for p in range(2)]
        kT = [g.kT[p][:, 0:G * T].rearrange("p (g q) -> p g q", g=G) for p in range(2)]
        qh = [g.qh[p][:, 0:G * T].rearrange("p (g q) -> p g q", g=G) for p in range(2)]
        kh = [g.kh[p][:, 0:G * T].rearrange("p (g q) -> p g q", g=G) for p in range(2)]
        V = [g.V[p][:, 0:NT * H * SLOT].rearrange("p (t h d) -> p t h d", t=NT, h=H) for p in range(2)]
        yT = g.yT if cfg.kv_gain is not None else g.xT
        oT = g.oT[:, 0:G * T].rearrange("p (n q) -> p n q", n=G)
        FA, FB, MX, SC, O = g.bank[0], g.bank[1], g.bank[2:4], g.bank[4:6], g.bank[6:8]
        block = ctx.enter_context(nc.Block())
        load_later(block, cfg)

        def two_groups(bank):
            return bank[:, 0:512].rearrange("p (g q) -> p g q", g=2)

        @block.vector
        def _(dve):
            for p in range(2):
                last = dve.memset(V[p][:, :, :, :], 0.0)
            last.then_inc(s.ones_ready, 1)
            dve.wait_ge(s.ones_ready, 1)

            def project(m, p, what):
                dst, low, bias = (qT[p], qh[p], cfg.bq) if what == "q" else (kT[p], kh[p], cfg.bk)
                dve.wait_ge(s.b_full, fb(what, m) + 1)
                src = two_groups(FB)
                for out in (low, dst):
                    if bias is None:
                        last = dve.tensor_copy(out[:, 0:2, :], src)
                    else:
                        last = dve.tensor_tensor(out=out[:, 0:2, :], in0=src,
                                                 in1=bias[:, 0:2].unsqueeze(2).to_broadcast([P, 2, T]), op=ALU.add)
                last.then_inc(s.b_free, 1)

            def values(m, p):
                dve.wait_ge(s.b_full, fb("v", m) + 1)
                for t in range(1 if cfg.wide_v else NT):
                    src = FB[:, t * H * D:(t + 1) * H * D].rearrange("p (h d) -> p h d", h=H)
                    if cfg.bv is None:
                        last = dve.tensor_copy(V[p][:, t, :, 0:D], src)
                    else:
                        last = dve.tensor_tensor(out=V[p][:, t, :, 0:D], in0=src,
                                                 in1=cfg.bv.rearrange("p (h d) -> p h d", h=H), op=ALU.add)
                last.then_inc(s.b_free, 1)

            def piece(m, i):
                qt, j, g0, nh, keys = pieces[i]
                dve.wait_ge(s.max_full, NPC * m + i + 1)
                dve.tensor_reduce(g.negmax[:, qt, :].rearrange("p (g j) -> p g j", g=G)[:, g0:g0 + nh, j],
                                  MX[i % 2][:, 0:512].rearrange("p (h k) -> p h k", h=nh),
                                  AX_X, ALU.max, negate=True).then_inc(s.max_free, 1)

            def spread(m):
                dve.wait_ge(s.max_free, NPC * (m + 1))
                dve.tensor_copy(g.negmax4[:, :, :, 0:H],
                                g.negmax[:, :, :].unsqueeze(2).to_broadcast([P, NT, 4, H])
                                ).then_inc(s.negmax_ready, 1)

            def key_sum(n, h):
                a, b = g.prob[h % 3], g.probsum[h % 3]
                if cfg.causal:
                    dve.wait_ge(s.masked, H * n + h + 1)
                    dve.tensor_tensor(out=b[:, P:T], in0=a[:, P:T], in1=a[:, K1:SW], op=ALU.add).then_inc(s.summed, 1)
                else:
                    dve.wait_ge(s.exp_done, H * n + h + 1)
                    dve.tensor_tensor(out=b[:, :], in0=a[:, 0:T], in1=a[:, K1:SW], op=ALU.add).then_inc(s.summed, 1)

            def normalise(n, gr):
                dve.wait_ge(s.pv_done, H * n + HG * (gr + 1))
                dve.reciprocal(g.rec[:, :], O[gr % 2][:, T:2 * T]).then_inc(s.recip_done, 1)
                dve.wait_ge(s.recip_done, G * n + gr + 1)
                dve.tensor_tensor(out=oT[:, gr, :], in0=O[gr % 2][:, 0:T], in1=g.rec[:, :], op=ALU.mult
                                  ).then_inc(s.heads_normed, 1)

            def tail(n, p):
                dve.wait_ge(s.b_full, fb("out", n) + 1)
                dve.wait_ge(s.bias_added, n + 1)
                dve.tensor_tensor(out=tokens(cfg.target, n), in0=FB[:, 0:T].rearrange("p (t c) -> p t c", t=NT),
                                  in1=g.resb[p][:, :, :], op=ALU.add).then_inc(s.b_free, 1)

            def prologue():
                front_vector(dve, s, g, cfg, 0, 0)
                front_vector(dve, s, g, cfg, 1, 1)
                project(0, 0, "q")
                project(0, 0, "k")
                values(0, 0)
                for i in range(NPC):
                    piece(0, i)
                spread(0)

            def body(n, p):
                ln = spread_over(ln_steps(dve, s, g, cfg, n + 2, p), list(range(6, 15))) if has(n, 2) else {}
                for h in range(H):
                    if h == AT["shift"] and has(n, 1):
                        spread(n + 1)
                    key_sum(n, h)
                    if h == AT["out"] and has(n, -1):
                        tail(n - 1, 1 - p)
                    if has(n, 1):
                        if h == AT["qb"]:
                            project(n + 1, 1 - p, "q")
                        if h == AT["kb"]:
                            project(n + 1, 1 - p, "k")
                        if h == AT["v"]:
                            values(n + 1, 1 - p)
                        for i in piece_at[h]:
                            piece(n + 1, i)
                    if h in (4, 8, 12):
                        normalise(n, h // 4 - 1)
                    for step in ln.get(h, ()):
                        step()
                normalise(n, G - 1)

            per_batch(dve, prologue, body, lambda: tail(B - 1, 1))

        @block.gpsimd
        def _(pool):
            def mask(n, h):
                wait_apart(pool, s.exp_done, H * n + h + 1)
                if cfg.causal:
                    diag = g.prob[h % 3][:, 0:512].rearrange("p (b q) -> p b q", b=2)[:, :, 0:P]
                    pool.affine_select(out=diag, in_=diag, compare_op=ALU.is_ge, fill=0.0, base=0,
                                       pattern=[[0, 2], [1, P]], channel_multiplier=-1).then_inc(s.masked, 1)
                else:
                    for t in range(NT):
                        last = pool.affine_select(out=g.probm[h % 3][:, t, :],
                                                  in_=g.prob[h % 3][:, t * (K1 + P):t * (K1 + P) + P],
                                                  compare_op=ALU.is_gt, fill=0.0, base=0,
                                                  pattern=[[-1, P]], channel_multiplier=1)
                    last.then_inc(s.masked, 1)

            def body(n, p):
                for h in range(H):
                    mask(n, h)
                    if h == 1:
                        pool.tensor_tensor(out=g.resb[p][:, :, :], in0=tokens(cfg.residual, n),
                                           in1=cfg.bias.unsqueeze(1).to_broadcast([P, NT, C]),
                                           op=ALU.add).then_inc(s.bias_added, 1)
                    if has(n, 2) and h >= 7 and (h - 7) % 3 == 0 and (h - 7) // 3 < len(cfg.norms):
                        ln_pool(pool, s, g, (h - 7) // 3, n + 2)

            def prologue():
                front_pool(pool, s, g, cfg, 0)
                front_pool(pool, s, g, cfg, 1)

            per_batch(pool, prologue, body)

        @block.scalar
        def _(act):
            def transposed(m, p):
                act.wait_ge(s.a_full, fa("x", m) + 1)
                if cfg.q_gain is None:
                    act.activation(g.xT[p][:, :], FA[:, 0:T], ACT.Copy).then_inc(s.a_free, 1)
                else:
                    act.activation(g.yT[p][:, :], FA[:, 0:T], ACT.Identity, scale=cfg.kv_gain, bias=cfg.kv_shift)
                    act.activation(g.xT[p][:, :], FA[:, 0:T], ACT.Identity, scale=cfg.q_gain,
                                   bias=cfg.q_shift).then_inc(s.a_free, 1)

            def project(m, p, what):
                dst, low, bias = (qT[p], qh[p], cfg.bq) if what == "q" else (kT[p], kh[p], cfg.bk)
                act.wait_ge(s.a_full, fa(what, m) + 1)
                for out in (low, dst):
                    if bias is None:
                        last = act.activation(out[:, 2:4, :], two_groups(FA), ACT.Copy)
                    else:
                        act.activation(out[:, 2, :], FA[:, 0:T], ACT.Identity, bias=bias[:, 2:3])
                        last = act.activation(out[:, 3, :], FA[:, T:2 * T], ACT.Identity, bias=bias[:, 3:4])
                last.then_inc(s.a_free, 1)

            def values(m, p):
                act.wait_ge(s.a_full, fa("v", m) + 1)
                act.activation(V[p][:, 1, :, 0:D], FA[:, 0:512].rearrange("p (h d) -> p h d", h=H),
                               ACT.Copy).then_inc(s.a_free, 1)

            def shift(m, p):
                act.wait_ge(s.a_full, fa("shift", m) + 1)
                act.activation(g.negmaxT[p][:, :], FA[:, 0:P].bitcast(BF16), ACT.Copy).then_inc(s.a_free, 1)

            def exponent(n, h):
                act.wait_ge(s.scores_ready, H * n + h + 1)
                wait(act, s.pv_done, H * n + h - 2)
                act.activation(g.prob[h % 3][:, 0:SW], SC[h % 2][:, 0:SW], ACT.Exp,
                               scale=cfg.scale).then_inc(s.exp_done, 1)

            def prologue():
                act.wait_ge(s.ones_ready, 1)
                transposed(0, 0)
                project(0, 0, "q")
                project(0, 0, "k")
                if cfg.wide_v:
                    values(0, 0)
                shift(0, 0)

            def body(n, p):
                for h in range(H):
                    exponent(n, h)
                    if has(n, 1):
                        if h == AT["x"]:
                            transposed(n + 1, 1 - p)
                        if h == AT["qa"]:
                            project(n + 1, 1 - p, "q")
                        if h == AT["ka"]:
                            project(n + 1, 1 - p, "k")
                        if h == AT["v"] and cfg.wide_v:
                            values(n + 1, 1 - p)
                        if h == AT["shift"]:
                            shift(n + 1, 1 - p)

            per_batch(act, prologue, body)

        @block.tensor
        def _(pe):
            cfg.loaded(pe)
            pe.wait_ge(s.ones_ready, 1)

            def transposed(m, p):
                wait_normed(pe, s, cfg, m)
                wait(pe, s.a_free, fa("x", m))
                for t in range(NT):
                    last = pe.transpose(FA[:, t * P:(t + 1) * P], g.xn[p][:, t, :], g.ident[:, :])
                last.then_inc(s.a_full, 1)

            def project(m, p, what, bank):
                w, x = (cfg.wq, g.xT[p]) if what == "q" else (cfg.wk, yT[p])
                if what == "q" and bank == "b":
                    pe.wait_ge(s.a_free, fa("x", m) + 1)
                if bank == "b":
                    wait(pe, s.b_free, fb(what, m))
                else:
                    wait(pe, s.a_free, fa(what, m))
                dst, full, g0 = (FB, s.b_full, 0) if bank == "b" else (FA, s.a_full, 2)
                for k in range(2):
                    last = pe.matmul(dst[:, k * T:(k + 1) * T], w[:, (g0 + k) * P:(g0 + k + 1) * P], x[:, :],
                                     start=True, stop=True)
                last.then_inc(full, 1)

            def values(m, p):
                wait(pe, s.b_free, fb("v", m))
                if cfg.wide_v:
                    pe.matmul(FB[:, 0:512], yT[p][:, 0:P], cfg.wv[:, :], start=True, stop=True).then_inc(s.b_full, 1)
                    wait(pe, s.a_free, fa("v", m))
                    pe.matmul(FA[:, 0:512], yT[p][:, P:2 * P], cfg.wv[:, :], start=True, stop=True
                              ).then_inc(s.a_full, 1)
                else:
                    for t in range(NT):
                        last = pe.matmul(FB[:, t * P:(t + 1) * P], yT[p][:, t * P:(t + 1) * P], cfg.wv[:, :],
                                         start=True, stop=True)
                    last.then_inc(s.b_full, 1)

            def piece(m, i, p):
                qt, j, g0, nh, keys = pieces[i]
                if i == 0:
                    pe.wait_ge(s.b_free, fb("k", m) + 1)
                    pe.wait_ge(s.a_free, fa("k", m) + 1)
                wait(pe, s.max_free, NPC * m + i - 1)
                bank = MX[i % 2]
                if cfg.causal:
                    out = bank[:, 0:512].rearrange("p (h k) -> p h k", h=nh)[:, :, keys - P:keys]
                    pe.matmul(out, g.identh[:, :], g.causal[:, :].unsqueeze(1).to_broadcast([P, nh, P]),
                              start=True, stop=False, skip_group_check=True)
                r = SLOT * j
                for k in range(nh):
                    last = pe.matmul(bank[:, k * keys:(k + 1) * keys], qh[p][r:r + D, g0 + k, qt * P:(qt + 1) * P],
                                     kh[p][r:r + D, g0 + k, 0:keys], start=not cfg.causal, stop=True,
                                     skip_group_check=True)
                last.then_inc(s.max_full, 1)

            def shift(m):
                pe.wait_ge(s.negmax_ready, m + 1)
                wait(pe, s.a_free, fa("shift", m))
                for t in range(NT):
                    last = pe.transpose(FA[:, 0:P].bitcast(BF16)[:, t * P:(t + 1) * P],
                                        g.negmax4[:, t, :, :].rearrange("p r c -> p (r c)"), g.identh[:, :])
                last.then_inc(s.a_full, 1)

            def scores(n, h, p):
                if h == 0:
                    pe.wait_ge(s.a_free, fa("shift", n) + 1)
                    pe.wait_ge(s.b_free, fb("v", n) + 1)
                wait(pe, s.exp_done, H * n + h - 1)
                r, gr = SLOT * (h % HG), h // HG
                bank = SC[h % 2]
                pe.matmul(bank[:, 0:T], g.sel_head[r:r + SLOT, h, :], g.negmaxT[p][r:r + SLOT, :],
                          start=True, stop=False, skip_group_check=True)
                pe.matmul(bank[:, K1:SW], g.sel_head[r:r + SLOT, h, :], g.negmaxT[p][r:r + SLOT, K1Q:T],
                          start=False, stop=False, skip_group_check=True)
                pe.matmul(bank[:, 0:T], kT[p][r:r + D, gr, 0:P], qT[p][r:r + D, gr, :],
                          start=False, stop=False, skip_group_check=True)
                pe.matmul(bank[:, K1:SW], kT[p][r:r + D, gr, P:T], qT[p][r:r + D, gr, K1Q:T],
                          start=False, stop=True, skip_group_check=True).then_inc(s.scores_ready, 1)

            def weigh(n, h, p):
                pe.wait_ge(s.masked, H * n + h + 1)
                pe.wait_ge(s.summed, H * n + h + 1)
                if h % HG == 0:
                    wait(pe, s.heads_normed, G * n + h // HG - 1)
                r, bank, a = SLOT * (h % HG), O[(h // HG) % 2], g.prob[h % 3]
                v0, v1, ones = V[p][:, 0, h, :], V[p][:, 1, h, :], g.ones[:, 0:SLOT]

                def product(columns, lhs, rhs, start=False, stop=False):
                    return pe.matmul(bank[r:r + SLOT, columns], lhs, rhs, start=start, stop=stop,
                                     skip_group_check=True)

                if cfg.causal:
                    product(slice(0, T), v0, a[:, 0:T], start=True)
                    product(slice(P, T), v1, a[:, K1:SW])
                    product(slice(T, T + P), ones, a[:, 0:P])
                    last = product(slice(T + P, 2 * T), ones, g.probsum[h % 3][:, P:T], stop=True)
                else:
                    product(slice(0, P), v0, g.probm[h % 3][:, 0, :], start=True)
                    product(slice(0, P), v1, a[:, K1:K1 + P])
                    product(slice(P, T), v1, g.probm[h % 3][:, 1, :])
                    last = product(slice(T, 2 * T), ones, g.probsum[h % 3][:, :], stop=True)
                last.then_inc(s.pv_done, 1)

            def out(n):
                pe.wait_ge(s.heads_normed, G * (n + 1))
                wait(pe, s.b_free, fb("out", n))
                for t in range(NT):
                    for k in range(G):
                        last = pe.matmul(FB[:, t * P:(t + 1) * P], oT[:, k, t * P:(t + 1) * P], cfg.wo[:, k, :],
                                         start=(k == 0), stop=(k == G - 1))
                last.then_inc(s.b_full, 1)

            def prologue():
                transposed(0, 0)
                for what in "qk":
                    project(0, 0, what, "b")
                    project(0, 0, what, "a")
                values(0, 0)
                for i in range(NPC):
                    piece(0, i, 0)
                shift(0)

            def body(n, p):
                for h in range(H + 1):
                    if h < H:
                        scores(n, h, p)
                    if h == AT["out"] and has(n, -1):
                        out(n - 1)
                    if has(n, 1):
                        if h == AT["x"]:
                            transposed(n + 1, 1 - p)
                        for what in "qk":
                            for bank in "ba":
                                if h == AT[what + bank]:
                                    project(n + 1, 1 - p, what, bank)
                        if h == AT["v"]:
                            values(n + 1, 1 - p)
                        for i in piece_at.get(h, ()):
                            piece(n + 1, i, 1 - p)
                        if h == AT["shift"]:
                            shift(n + 1)
                    if h >= 1:
                        weigh(n, h - 1, p)

            per_batch(pe, prologue, body, lambda: out(B - 1))



def cross_attention(nc, g, name, cfg):
    D = cfg.D
    NO = H * D // P
    HT = H // NO
    QC = max(1, NO // 2)
    QW = min(NO, 2)
    VC = max(1, H * D // 512)
    VW = H * D // VC
    GROUPS = PAIRS // 2
    PU = max(k for k in (2, 4, 8) if 2 * k * (D + 1) <= 512)
    NU = PAIRS // PU
    T_AT = {4: [(2, 0), (3, 0), (0, -1), (1, -1)], 2: [(3, 0), (1, -1)], 1: [(1, -1)]}[NU]
    assert NU == QC
    turned = [[(f"turned{u}", "BA"[u % 2 == 0], ahead) for u, (step, ahead) in enumerate(T_AT) if step == i]
              for i in range(GROUPS)]
    queries = [(f"q{c}", "BA"[c % 2], 1) for c in range(QC)]
    values = [(f"v{c}", "BA"[c % 2], 1) for c in range(VC)]
    order = ([("x", "A", 1)] + turned[0] + queries[:2] + turned[1] + queries[2:] + [("k", "B", 1), ("out", "B", -1)]
             + turned[2] + values + turned[3] + [("shift", "A", 1)])
    fa = bank_order([(name, ahead) for name, bank, ahead in order if bank == "A"])
    fb = bank_order([(name, ahead) for name, bank, ahead in order if bank == "B"])
    with ExitStack() as ctx:
        s = sem_space(nc, ctx, name, LN_SEMS + " a_full a_free b_full b_free low max_full max_free "
                      "negmax_ready scores_ready exp_done pv_done recip_done ctx_ready k_spread "
                      "heads_normed ones_ready bias_added v_ready")
        qT = [g.qT[p][:, 0:NO * T].rearrange("p (n q) -> p n q", n=NO) for p in range(2)]
        qh = [g.qh[p][:, 0:NO * T].rearrange("p (n q) -> p n q", n=NO) for p in range(2)]
        V = [g.V[p][:, 0:H * (D + 1)].rearrange("p (j i d) -> p j i d", j=PAIRS, i=2) for p in range(2)]
        osb = g.osb[:, 0:NT * H * D].rearrange("p (t f) -> p t f", t=NT)
        oT = g.oT[:, 0:NO * T].rearrange("p (n q) -> p n q", n=NO)
        FA, FB, MX, SC, O = g.bank[0], g.bank[1], g.bank[2:4], g.bank[4:6], g.bank[6:8]
        block = ctx.enter_context(nc.Block())
        load_later(block, cfg)

        def spread_v(eng, p, c, bank):
            j0, nj = c * PAIRS // VC, PAIRS // VC
            for i in range(2):
                rows = slice(i * TC, (i + 1) * TC)
                dst = V[p][rows, j0:j0 + nj, i, 0:D]
                src = bank[rows, 0:VW].rearrange("p (j i d) -> p j i d", j=nj, i=2)[:, :, i, :]
                if eng == "act":
                    last = nc.scalar.activation(dst, src, ACT.Copy)
                elif cfg.bv is None:
                    last = nc.vector.tensor_copy(dst, src)
                else:
                    last = nc.vector.tensor_tensor(
                        out=dst, in0=src, op=ALU.add,
                        in1=cfg.bv[rows, :].rearrange("p (j i d) -> p j i d", j=nj, i=2)[:, :, i, :])
            return last

        @block.vector
        def _(dve):
            for p in range(2):
                dve.memset(V[p][:, :, :, :], 0.0).then_inc(s.ones_ready, 1)
            dve.wait_ge(s.ones_ready, 2)
            for p in range(2):
                dve.memset(V[p][0:TC, :, 0, D:D + 1], 1.0)
                dve.memset(V[p][TC:P, :, 1, D:D + 1], 1.0).then_inc(s.ones_ready, 1)
            dve.wait_ge(s.ones_ready, 4)

            def queries_to(m, p, c):
                dve.wait_ge(s.b_full, fb(f"q{c}", m) + 1)
                src = FB[:, 0:QW * T].rearrange("p (n q) -> p n q", n=QW)
                for out in (qh, qT):
                    dst = out[p][:, QW * c:QW * (c + 1), :]
                    if cfg.bq is None:
                        last = dve.tensor_copy(dst, src)
                    else:
                        last = dve.tensor_scalar(dst, src, cfg.bq, None, ALU.add)
                last.then_inc(s.b_free, 1)

            def keys(m, p):
                dve.wait_ge(s.b_full, fb("k", m) + 1)
                k = FB[:, 0:NO * TC].rearrange("p (n k) -> p n k", n=NO)
                if NO == 1:
                    dst = g.kmask[p][:, :].rearrange("p (h k) -> p h k", h=H)
                    kb = k[:, 0, :].unsqueeze(1).to_broadcast([P, H, TC])
                    hm = cfg.head_mask[:, :].unsqueeze(2).to_broadcast([P, H, TC])
                    if cfg.bk is None:
                        last = dve.tensor_tensor(out=dst, in0=kb, in1=hm, op=ALU.mult)
                    else:
                        last = dve.scalar_tensor_tensor(out=dst, in0=kb, scalar=cfg.bk, in1=hm,
                                                        op0=ALU.add, op1=ALU.mult)
                else:
                    for h in range(HT):
                        dst = g.kmask[p][:, :].rearrange("p (n h k) -> p n h k", n=NO, h=HT)[:, :, h, :]
                        last = dve.tensor_scalar(dst, k, cfg.head_mask[:, h:h + 1], None, ALU.mult)
                last.then_inc(s.b_free, 1)

            def values_to(m, p):
                dve.wait_ge(s.b_full, fb("v0", m) + 1)
                spread_v("dve", p, 0, FB).then_inc(s.b_free, 1)

            def piece(m, i):
                qt, half = divmod(i, 2)
                dve.wait_ge(s.max_full, 4 * m + i + 1)
                dve.tensor_reduce(g.negmax[:, qt, 8 * half:8 * half + 8],
                                  MX[i % 2][:, 0:512].rearrange("p (h k) -> p h k", h=8),
                                  AX_X, ALU.max, negate=True).then_inc(s.max_free, 1)

            def spread(m):
                dve.wait_ge(s.max_free, 4 * (m + 1))
                dve.tensor_copy(g.negmax4[:, :, 0, 0:H], g.negmax[:, :, :]).then_inc(s.negmax_ready, 1)

            def normalise(n, u):
                dve.wait_ge(s.pv_done, GROUPS * n + (u + 1) * PU // 2)
                for qt in range(NT):
                    o = O[qt][:, 0:2 * PU * (D + 1)].rearrange("p (h d) -> p h d", h=2 * PU)
                    dve.reciprocal(g.recip16[:, qt, 0:2 * PU], o[:, :, D]).then_inc(s.recip_done, 1)
                dve.wait_ge(s.recip_done, NT * (NU * n + u + 1))
                for qt in range(NT):
                    o = O[qt][:, 0:2 * PU * (D + 1)].rearrange("p (h d) -> p h d", h=2 * PU)
                    last = dve.tensor_tensor(
                        out=osb[:, qt, u * 2 * PU * D:(u + 1) * 2 * PU * D].rearrange("p (h d) -> p h d", h=2 * PU),
                        in0=o[:, :, 0:D], in1=g.recip16[:, qt, 0:2 * PU].unsqueeze(2).to_broadcast([P, 2 * PU, D]),
                        op=ALU.mult)
                last.then_inc(s.heads_normed, 1)

            def turned_to(n, u):
                dve.wait_ge(s.b_full, fb(f"turned{u}", n) + 1)
                dve.tensor_copy(oT[:, QW * u:QW * (u + 1), :], FB[:, 0:512].rearrange("p (n q) -> p n q", n=2)
                                ).then_inc(s.b_free, 1)

            def final(n, p):
                dve.wait_ge(s.b_full, fb("out", n) + 1)
                if cfg.bias is not None:
                    dve.wait_ge(s.bias_added, n + 1)
                res = tokens(cfg.residual, n) if cfg.bias is None else g.resb[p][:, :, :]
                dve.tensor_tensor(out=tokens(cfg.target, n), in0=FB[:, 0:T].rearrange("p (t c) -> p t c", t=NT),
                                  in1=res, op=ALU.add).then_inc(s.b_free, 1)

            def prologue():
                front_vector(dve, s, g, cfg, 0, 0)
                front_vector(dve, s, g, cfg, 1, 1)
                for c in range(0, QC, 2):
                    queries_to(0, 0, c)
                keys(0, 0)
                for i in range(4):
                    piece(0, i)
                spread(0)
                values_to(0, 0)

            def body(n, p):
                ln = spread_over(ln_steps(dve, s, g, cfg, n + 2, p), list(range(GROUPS))) if has(n, 2) else {}
                for e in range(GROUPS):
                    for step in ln.get(e, ()):
                        step()
                    if e == 1:
                        if has(n, 1):
                            queries_to(n + 1, 1 - p, 0)
                        if (1, -1) in T_AT and (NU - 1) % 2 and has(n, -1):
                            turned_to(n - 1, NU - 1)
                        if has(n, 1):
                            if QC > 2:
                                queries_to(n + 1, 1 - p, 2)
                            keys(n + 1, 1 - p)
                    if e == 2:
                        if has(n, 1):
                            piece(n + 1, 0)
                            piece(n + 1, 1)
                        if NU == 4:
                            normalise(n, 0)
                        if has(n, -1):
                            final(n - 1, 1 - p)
                        if has(n, 1):
                            piece(n + 1, 2)
                    if e == 3:
                        if has(n, 1):
                            piece(n + 1, 3)
                            spread(n + 1)
                            values_to(n + 1, 1 - p)
                        if NU > 1:
                            normalise(n, NU // 2 - 1)
                        if NU == 4:
                            turned_to(n, 1)
                            normalise(n, 2)
                normalise(n, NU - 1)

            def epilogue():
                if (NU - 1) % 2:
                    turned_to(B - 1, NU - 1)
                final(B - 1, 1)

            per_batch(dve, prologue, body, epilogue)

        @block.gpsimd
        def _(pool):
            def context(m, p):
                pool.tensor_copy(g.ctxb[p][:, :, :], (cfg.ctxT[:, bass.ds(m, 1), :] if not isinstance(m, int)
                                                      else cfg.ctxT[:, m:m + 1, :]).to_broadcast([CC, 2, TC])
                                 ).then_inc(s.ctx_ready, 1)

            def prologue():
                for m in range(2):
                    front_pool(pool, s, g, cfg, m)
                    context(m, m)

            def body(n, p):
                if has(n, 2):
                    ln_pool(pool, s, g, 0, n + 2)
                wait_apart(pool, s.exp_done, GROUPS * n + 1)
                if has(n, 2):
                    context(n + 2, p)
                if cfg.bias is not None:
                    pool.tensor_tensor(out=g.resb[p][:, :, :], in0=tokens(cfg.residual, n),
                                       in1=cfg.bias.unsqueeze(1).to_broadcast([P, NT, C]),
                                       op=ALU.add).then_inc(s.bias_added, 1)
                for k in range(1, len(cfg.norms)):
                    if has(n, 2):
                        ln_pool(pool, s, g, k, n + 2)

            per_batch(pool, prologue, body)

        @block.scalar
        def _(act):
            act.wait_ge(s.ones_ready, 4)

            def transposed(m, p):
                act.wait_ge(s.a_full, fa("x", m) + 1)
                if cfg.q_gain is None:
                    act.activation(g.xT[p][:, :], FA[:, 0:T], ACT.Copy).then_inc(s.a_free, 1)
                else:
                    act.activation(g.xT[p][:, :], FA[:, 0:T], ACT.Identity, scale=cfg.q_gain,
                                   bias=cfg.q_shift).then_inc(s.a_free, 1)

            def queries_to(m, p, c):
                act.wait_ge(s.a_full, fa(f"q{c}", m) + 1)
                for out in (qh, qT):
                    last = act.activation(out[p][:, 2 * c:2 * c + 2, :], FA[:, 0:512].rearrange("p (n q) -> p n q", n=2),
                                          ACT.Copy)
                last.then_inc(s.a_free, 1)

            def low_keys(m, p):
                act.wait_ge(s.b_free, fb("k", m) + 1)
                act.activation(g.kmaskh[p][:, :], g.kmask[p][:, :], ACT.Copy).then_inc(s.low, 1)

            def values_to(m, p):
                act.wait_ge(s.a_full, fa("v1", m) + 1)
                spread_v("act", p, 1, FA).then_inc(s.a_free, 1)

            def shift(m, p):
                act.wait_ge(s.a_full, fa("shift", m) + 1)
                act.activation(g.negmaxT[p][0:H, :], FA[0:H, 0:P].bitcast(BF16), ACT.Copy).then_inc(s.a_free, 1)

            def turned_to(n, u):
                act.wait_ge(s.a_full, fa(f"turned{u}", n) + 1)
                act.activation(oT[:, QW * u:QW * (u + 1), :], FA[:, 0:QW * T].rearrange("p (n q) -> p n q", n=QW),
                               ACT.Copy).then_inc(s.a_free, 1)

            def turn(n, step):
                for u, (at, ahead) in enumerate(T_AT):
                    if at == step and u % 2 == 0 and has(n, ahead):
                        turned_to(n + ahead, u)

            def prologue():
                transposed(0, 0)
                for c in range(1, QC, 2):
                    queries_to(0, 0, c)
                low_keys(0, 0)
                if VC > 1:
                    values_to(0, 0)
                shift(0, 0)

            def body(n, p):
                for e in range(GROUPS):
                    act.wait_ge(s.scores_ready, GROUPS * n + e + 1)
                    if e >= 3:
                        act.wait_ge(s.pv_done, GROUPS * n + e - 2)
                    act.activation(g.prob[e % 3][:, :], SC[e % 2][:, :], ACT.Exp,
                                   scale=cfg.scale).then_inc(s.exp_done, 1)
                    if e == 0:
                        if has(n, 1):
                            transposed(n + 1, 1 - p)
                        turn(n, 0)
                    if e == 1:
                        if QC > 1 and has(n, 1):
                            queries_to(n + 1, 1 - p, 1)
                        turn(n, 1)
                        if QC > 2 and has(n, 1):
                            queries_to(n + 1, 1 - p, 3)
                        if has(n, 1):
                            low_keys(n + 1, 1 - p)
                    if e == 2:
                        turn(n, 2)
                    if e == 3:
                        if VC > 1 and has(n, 1):
                            values_to(n + 1, 1 - p)
                        turn(n, 3)
                        if has(n, 1):
                            shift(n + 1, 1 - p)

            per_batch(act, prologue, body, lambda: (turn(B, 0), turn(B, 1)))

        @block.tensor
        def _(pe):
            cfg.loaded(pe)
            pe.wait_ge(s.ones_ready, 4)

            BANK, FULL = dict(A=FA, B=FB), dict(A=s.a_full, B=s.b_full)

            def use(bank, name, m):
                if bank == "A":
                    wait(pe, s.a_free, fa(name, m))
                else:
                    wait(pe, s.b_free, fb(name, m))

            def transposed(m, p):
                wait_normed(pe, s, cfg, m)
                use("A", "x", m)
                for t in range(NT):
                    last = pe.transpose(FA[:, t * P:(t + 1) * P], g.xn[p][:, t, :], g.ident[:, :])
                last.then_inc(s.a_full, 1)

            def project_q(m, p, c):
                if c == 0:
                    pe.wait_ge(s.a_free, fa("x", m) + 1)
                bank = "BA"[c % 2]
                use(bank, f"q{c}", m)
                for i in range(QW):
                    tile = QW * c + i
                    last = pe.matmul(BANK[bank][:, i * T:(i + 1) * T], cfg.wq[:, tile * P:(tile + 1) * P],
                                     g.xT[p][:, :], start=True, stop=True)
                last.then_inc(FULL[bank], 1)

            def project_k(m, p):
                pe.wait_ge(s.ctx_ready, m + 1)
                use("B", "k", m)
                for i in range(NO):
                    last = pe.matmul(FB[:, i * TC:(i + 1) * TC], cfg.wk[:, i * P:(i + 1) * P], g.ctxb[p][:, 0, :],
                                     start=True, stop=True)
                last.then_inc(s.b_full, 1)

            def project_v(m, p, c):
                bank = "BA"[c % 2]
                use(bank, f"v{c}", m)
                pe.matmul(BANK[bank][:, 0:VW], g.ctxb[p][:, :, :].rearrange("p i k -> p (i k)"),
                          cfg.wv[:, c * VW:(c + 1) * VW], start=True, stop=True).then_inc(FULL[bank], 1)

            def piece(m, i, p):
                qt, half = divmod(i, 2)
                if i == 0:
                    pe.wait_ge(s.low, m + 1)
                    if QC > 1:
                        pe.wait_ge(s.a_free, fa(f"q{QC - 1}", m) + 1)
                if i >= 2:
                    pe.wait_ge(s.max_free, 4 * m + i - 1)
                tiles = range(NO) if NO == 1 else range(half * NO // 2, (half + 1) * NO // 2)
                w = 512 if NO == 1 else HT * TC
                for k, n in enumerate(tiles):
                    last = pe.matmul(MX[i % 2][:, k * w:(k + 1) * w], qh[p][:, n, qt * P:(qt + 1) * P],
                                     g.kmaskh[p][:, half * 512 + k * w:half * 512 + (k + 1) * w],
                                     start=True, stop=True, skip_group_check=True)
                last.then_inc(s.max_full, 1)

            def shift(m):
                pe.wait_ge(s.negmax_ready, m + 1)
                use("A", "shift", m)
                for t in range(NT):
                    last = pe.transpose(FA[0:H, 0:P].bitcast(BF16)[:, t * P:(t + 1) * P],
                                        g.negmax4[:, t, 0, 0:H], g.identh[:, :])
                last.then_inc(s.a_full, 1)

            def scores(n, e, p):
                if e == 0:
                    pe.wait_ge(s.a_free, fa("shift", n) + 1)
                    pe.wait_ge(s.b_free, fb("v0", n) + 1)
                if e >= 2:
                    pe.wait_ge(s.exp_done, GROUPS * n + e - 1)
                for i in range(2):
                    j = 2 * e + i
                    out = SC[e % 2][:, i * T:(i + 1) * T]
                    pe.matmul(out, g.sel_pair[0:H, j, :], g.negmaxT[p][0:H, :], start=True, stop=False)
                    last = pe.matmul(out, g.kmask[p][:, j * P:(j + 1) * P], qT[p][:, j * NO // PAIRS, :],
                                     start=False, stop=True)
                last.then_inc(s.scores_ready, 1)

            def weigh(n, e, p):
                pe.wait_ge(s.exp_done, GROUPS * n + e + 1)
                u = e * 2 // PU
                if e * 2 % PU == 0:
                    wait(pe, s.heads_normed, NU * n + u)
                for i in range(2):
                    j = 2 * e + i
                    w = 2 * (D + 1)
                    for qt in range(NT):
                        last = pe.matmul(O[qt][:, (j % PU) * w:(j % PU + 1) * w],
                                         g.prob[e % 3][:, i * T + qt * P:i * T + (qt + 1) * P],
                                         V[p][:, j, :, :].rearrange("p i d -> p (i d)"), start=True, stop=True)
                last.then_inc(s.pv_done, 1)

            def turn(n, step):
                for u, (at, ahead) in enumerate(T_AT):
                    if at == step and has(n, ahead):
                        pe.wait_ge(s.heads_normed, NU * (n + ahead) + u + 1)
                        bank = "BA"[u % 2 == 0]
                        use(bank, f"turned{u}", n + ahead)
                        for i in range(QW):
                            for t in range(NT):
                                k = QW * u + i
                                last = pe.transpose(BANK[bank][:, i * T + t * P:i * T + (t + 1) * P],
                                                    osb[:, t, k * P:(k + 1) * P], g.ident[:, :])
                        last.then_inc(FULL[bank], 1)

            def out(n):
                last_a = (NU - 1) // 2 * 2
                pe.wait_ge(s.a_free, fa(f"turned{last_a}", n) + 1)
                use("B", "out", n)
                for t in range(NT):
                    for k in range(NO):
                        last = pe.matmul(FB[:, t * P:(t + 1) * P], oT[:, k, t * P:(t + 1) * P], cfg.wo[:, k, :],
                                         start=(k == 0), stop=(k == NO - 1))
                last.then_inc(s.b_full, 1)

            def prologue():
                transposed(0, 0)
                for c in range(QC):
                    project_q(0, 0, c)
                project_k(0, 0)
                for i in range(4):
                    piece(0, i, 0)
                for c in range(VC):
                    project_v(0, 0, c)
                shift(0)

            def body(n, p):
                nx = has(n, 1)
                scores(n, 0, p)
                if nx:
                    transposed(n + 1, 1 - p)
                turn(n, 0)
                scores(n, 1, p)
                if nx:
                    for c in range(min(QC, 2)):
                        project_q(n + 1, 1 - p, c)
                turn(n, 1)
                weigh(n, 0, p)
                if nx:
                    for c in range(2, QC):
                        project_q(n + 1, 1 - p, c)
                    project_k(n + 1, 1 - p)
                scores(n, 2, p)
                if nx:
                    piece(n + 1, 0, 1 - p)
                    piece(n + 1, 1, 1 - p)
                if has(n, -1):
                    out(n - 1)
                weigh(n, 1, p)
                if nx:
                    piece(n + 1, 2, 1 - p)
                turn(n, 2)
                scores(n, 3, p)
                if nx:
                    piece(n + 1, 3, 1 - p)
                    for c in range(VC):
                        project_v(n + 1, 1 - p, c)
                weigh(n, 2, p)
                turn(n, 3)
                if nx:
                    shift(n + 1)
                weigh(n, 3, p)

            def epilogue():
                turn(B, 0)
                turn(B, 1)
                out(B - 1)

            per_batch(pe, prologue, body, epilogue)



def feed_forward(nc, g, name, cfg):
    HT = 4
    with ExitStack() as ctx:
        s = sem_space(nc, ctx, name, LN_SEMS + " xt_full xt_ready hidden_full hidden_ready out_full "
                      "residual_a residual_b target_ready")
        hT = [g.qT[p][:, 0:HT * T].rearrange("p (n q) -> p n q", n=HT) for p in range(2)]
        XT = g.bank[0:2]
        HID = [g.bank[2:4], g.bank[4:6]]
        OUT = g.bank[6:8]
        block = ctx.enter_context(nc.Block())
        load_later(block, cfg)

        @block.vector
        def _(dve):
            def front(m, p):
                front_vector(dve, s, g, cfg, m, p)
                if cfg.relu:
                    for k in range(HT):
                        dve.wait_ge(s.hidden_full, 2 * m + k // 2 + 1)
                        last = dve.tensor_scalar(hT[p][:, k, :], HID[p][k // 2][:, (k % 2) * T:(k % 2 + 1) * T],
                                                 cfg.b1[:, k:k + 1], 0.0, ALU.add, ALU.max)
                    last.then_inc(s.hidden_ready, 1)

            def tail(n, p):
                dve.wait_ge(s.out_full, n + 1)
                dve.wait_ge(s.residual_a, n + 1)
                if len(cfg.residuals) == 3:
                    dve.wait_ge(s.residual_b, 2 * (n + 1))
                elif len(cfg.residuals) == 2:
                    dve.wait_ge(s.residual_b, n + 1)
                dve.tensor_tensor(out=tokens(cfg.target, n), in0=OUT[p][:, 0:T].rearrange("p (t c) -> p t c", t=NT),
                                  in1=g.resb[p][:, :, :], op=ALU.add).then_inc(s.target_ready, 1)

            def body(n, p, has_next):
                if has_next:
                    front(n + 1, 1 - p)
                tail(n, p)

            per_element(dve, lambda: front(0, 0), body)

        @block.gpsimd
        def _(pool):
            def front(m, p):
                front_pool(pool, s, g, cfg, m)
                wait_normed(pool, s, cfg, m)
                res = g.resb[p][:, :, :]
                pool.tensor_tensor(out=res, in0=tokens(cfg.residuals[0], m),
                                   in1=cfg.bias.unsqueeze(1).to_broadcast([P, NT, C]),
                                   op=ALU.add).then_inc(s.residual_a, 1)
                pool.wait_ge(s.residual_a, m + 1)
                extra = len(cfg.residuals) - 1
                for i, r in enumerate(cfg.residuals[1:]):
                    pool.tensor_tensor(out=res, in0=res, in1=tokens(r, m), op=ALU.add).then_inc(s.residual_b, 1)
                    if i < extra - 1:
                        pool.wait_ge(s.residual_b, extra * m + i + 1)

            per_element(pool, lambda: front(0, 0), lambda n, p, nx: front(n + 1, 1 - p) if nx else None)

        @block.scalar
        def _(act):
            def front(m, p):
                act.wait_ge(s.xt_full, m + 1)
                if cfg.x_gain is None:
                    act.activation(g.xT[p][:, :], XT[p][:, 0:T], ACT.Copy).then_inc(s.xt_ready, 1)
                else:
                    act.activation(g.xT[p][:, :], XT[p][:, 0:T], ACT.Identity, scale=cfg.x_gain,
                                   bias=cfg.x_shift).then_inc(s.xt_ready, 1)
                if not cfg.relu:
                    for k in range(HT):
                        act.wait_ge(s.hidden_full, 2 * m + k // 2 + 1)
                        last = act.activation(hT[p][:, k, :], HID[p][k // 2][:, (k % 2) * T:(k % 2 + 1) * T],
                                              ACT.Gelu, bias=cfg.b1[:, k:k + 1])
                    last.then_inc(s.hidden_ready, 1)

            per_element(act, lambda: front(0, 0), lambda n, p, nx: front(n + 1, 1 - p) if nx else None)

        @block.tensor
        def _(pe):
            cfg.loaded(pe)

            def front(m, p):
                wait_normed(pe, s, cfg, m)
                for t in range(NT):
                    last = pe.transpose(XT[p][:, t * P:(t + 1) * P], g.xn[p][:, t, :], g.ident[:, :])
                last.then_inc(s.xt_full, 1)
                pe.wait_ge(s.xt_ready, m + 1)
                for k in range(HT):
                    mm = pe.matmul(HID[p][k // 2][:, (k % 2) * T:(k % 2 + 1) * T], cfg.w1[:, k * P:(k + 1) * P],
                                   g.xT[p][:, :], start=True, stop=True)
                    if k % 2:
                        mm.then_inc(s.hidden_full, 1)

            def tail(n, p):
                pe.wait_ge(s.hidden_ready, n + 1)
                for t in range(NT):
                    for k in range(HT):
                        last = pe.matmul(OUT[p][:, t * P:(t + 1) * P], hT[p][:, k, t * P:(t + 1) * P],
                                         cfg.w2[:, k, :], start=(k == 0), stop=(k == HT - 1))
                last.then_inc(s.out_full, 1)

            def body(n, p, has_next):
                if has_next:
                    front(n + 1, 1 - p)
                tail(n, p)

            per_element(pe, lambda: front(0, 0), body)



GATE_SEMS = (" logits_full shifted exped maxed shift_done summed rsum probs_ready topped keys_ready "
             "replaced weighed wsum wguard wrecip combined split_a split_b split_c split_d pbias pbias_sum")


def gate_vector(dve, s, g, cfg, m, p, LG):
    E, K, S = cfg.experts, cfg.top, 8 - cfg.top
    gb = g.gate
    lg = LG[:, 0:NT * E].rearrange("p (t e) -> p t e", t=NT)
    dve.wait_ge(s.logits_full, m + 1)
    dve.tensor_reduce(gb.nmax[:, :], lg, AX_X, ALU.max, negate=True).then_inc(s.maxed, 1)
    dve.wait_ge(s.maxed, m + 1)
    dve.tensor_tensor(out=gb.e[:, :, 0:E], in0=lg, in1=gb.nmax[:, :].unsqueeze(2).to_broadcast([P, NT, E]),
                      op=ALU.add).then_inc(s.shifted, 1)
    dve.wait_ge(s.exped, m + 1)
    dve.tensor_reduce(gb.sum[:, :], gb.e[:, :, 0:E], AX_X, ALU.add).then_inc(s.summed, 1)
    dve.wait_ge(s.summed, m + 1)
    dve.reciprocal(gb.rsum[:, :], gb.sum[:, :]).then_inc(s.rsum, 1)
    dve.wait_ge(s.rsum, m + 1)
    dve.tensor_tensor(out=gb.probs[:, :, 0:E], in0=gb.e[:, :, 0:E],
                      in1=gb.rsum[:, :].unsqueeze(2).to_broadcast([P, NT, E]), op=ALU.mult).then_inc(s.probs_ready, 1)
    wait_apart(dve, s.probs_ready, m + 1)
    for t in range(NT):
        dve.max(gb.top[:, t, :], gb.probs[:, t, 0:E]).then_inc(s.topped, 1)
    dve.wait_ge(s.topped, NT * (m + 1))
    dve.tensor_copy(gb.keys[:, :, 0:K], gb.top[:, :, 0:K]).then_inc(s.keys_ready, 1)
    wait_apart(dve, s.keys_ready, m + 1)
    for t in range(NT):
        dve.match_replace(gb.marked[:, t, 0:E + S], gb.keys[:, t, :], gb.probs[:, t, 0:E + S], -2.0
                          ).then_inc(s.replaced, 1)
    dve.wait_ge(s.replaced, NT * (m + 1))
    dve.scalar_tensor_tensor(out=gb.w[:, :, 0:E], in0=gb.marked[:, :, 0:E], scalar=0.0, in1=gb.probs[:, :, 0:E],
                             op0=ALU.is_lt, op1=ALU.mult).then_inc(s.weighed, 1)
    dve.wait_ge(s.weighed, m + 1)
    dve.tensor_reduce(gb.wsum[:, :], gb.w[:, :, 0:E], AX_X, ALU.add).then_inc(s.wsum, 1)
    dve.wait_ge(s.wsum, m + 1)
    total = gb.wsum
    if cfg.guard:
        dve.tensor_scalar(gb.wguard[:, :], gb.wsum[:, :], cfg.guard, None, ALU.add).then_inc(s.wguard, 1)
        dve.wait_ge(s.wguard, m + 1)
        total = gb.wguard
    dve.reciprocal(gb.wrecip[:, :], total[:, :]).then_inc(s.wrecip, 1)
    dve.wait_ge(s.wrecip, m + 1)
    dve.tensor_tensor(out=gb.c[p][:, :, 0:E], in0=gb.w[:, :, 0:E],
                      in1=gb.wrecip[:, :].unsqueeze(2).to_broadcast([P, NT, E]), op=ALU.mult).then_inc(s.combined, 1)
    dve.wait_ge(s.combined, m + 1)


def gate_exp(act, s, g, cfg, m):
    act.wait_ge(s.shifted, m + 1)
    act.activation(g.gate.e[:, :, 0:cfg.experts], g.gate.e[:, :, 0:cfg.experts], ACT.Exp).then_inc(s.exped, 1)


def route(nc, g, name, cfg):
    E = cfg.experts
    with ExitStack() as ctx:
        s = sem_space(nc, ctx, name, LN_SEMS + GATE_SEMS + " xt_full xt_ready parts_full parts_ready sentinels")
        XT, LG, PT = g.bank[0:2], g.bank[2:4], g.bank[4:6]
        gb = g.gate
        block = ctx.enter_context(nc.Block())
        load_later(block, cfg)

        @block.vector
        def _(dve):
            dve.memset(gb.probs[:, :, :], -1.0)
            dve.memset(gb.keys[:, :, :], -1.0).then_inc(s.sentinels, 1)
            dve.wait_ge(s.sentinels, 1)

            def front(m, p):
                front_vector(dve, s, g, cfg, m, p)

            def tail(n, p):
                gate_vector(dve, s, g, cfg, n, p, LG[p])
                c, part, rest = gb.c[p], gb.part[p], gb.rest
                dve.tensor_copy(part[:, :, 0, :], c[:, :, :]).then_inc(s.split_a, 1)
                dve.wait_ge(s.split_a, n + 1)
                dve.tensor_tensor(out=rest[:, 0, :, :], in0=c[:, :, :], in1=part[:, :, 0, :], op=ALU.subtract
                                  ).then_inc(s.split_b, 1)
                dve.wait_ge(s.split_b, n + 1)
                dve.tensor_copy(part[:, :, 1, :], rest[:, 0, :, :]).then_inc(s.split_c, 1)
                dve.wait_ge(s.split_c, n + 1)
                dve.tensor_tensor(out=part[:, :, 2, :], in0=rest[:, 0, :, :], in1=part[:, :, 1, :], op=ALU.subtract
                                  ).then_inc(s.split_d, 1)

            def body(n, p, has_next):
                if has_next:
                    front(n + 1, 1 - p)
                tail(n, p)

            per_element(dve, lambda: front(0, 0), body)

        @block.gpsimd
        def _(pool):
            per_element(pool, lambda: front_pool(pool, s, g, cfg, 0),
                      lambda n, p, nx: front_pool(pool, s, g, cfg, n + 1) if nx else None)

        @block.scalar
        def _(act):
            def front(m, p):
                act.wait_ge(s.xt_full, m + 1)
                act.activation(g.xT[p][:, :], XT[p][:, 0:T], ACT.Copy).then_inc(s.xt_ready, 1)

            def body(n, p, has_next):
                if has_next:
                    front(n + 1, 1 - p)
                gate_exp(act, s, g, cfg, n)
                act.wait_ge(s.parts_full, n + 1)
                dst = g.combT[:, bass.ds(T * n, T)] if not isinstance(n, int) else g.combT[:, T * n:T * n + T]
                act.activation(dst, PT[p][0:3 * E, 0:P].bitcast(BF16), ACT.Copy).then_inc(s.parts_ready, 1)

            per_element(act, lambda: front(0, 0), body)

        @block.tensor
        def _(pe):
            cfg.loaded(pe)

            def front(m, p):
                wait_normed(pe, s, cfg, m)
                for t in range(NT):
                    last = pe.transpose(XT[p][:, t * P:(t + 1) * P], g.xn[p][:, t, :], g.ident[:, :])
                last.then_inc(s.xt_full, 1)
                pe.wait_ge(s.xt_ready, m + 1)
                for t in range(NT):
                    last = pe.matmul(LG[p][:, t * E:(t + 1) * E], g.xT[p][:, t * P:(t + 1) * P], cfg.gate_w[:, :],
                                     start=True, stop=True)
                last.then_inc(s.logits_full, 1)

            def body(n, p, has_next):
                if has_next:
                    front(n + 1, 1 - p)
                wait_apart(pe, s.split_d, n + 1)
                for t in range(NT):
                    last = pe.transpose(PT[p][0:3 * E, 0:P].bitcast(BF16)[:, t * P:(t + 1) * P],
                                        gb.part[p][:, t, :, :].rearrange("p k e -> p (k e)"), g.identh[:, :])
                last.then_inc(s.parts_full, 1)

            per_element(pe, lambda: front(0, 0), body)


def gated_experts(nc, g, name, cfg):
    E, HID = 16, 64
    U = E // 2 + 1
    with ExitStack() as ctx:
        s = sem_space(nc, ctx, name, LN_SEMS + " xt_full xt_ready hidden_full silu_done gated scaled "
                      "used target_ready")
        XT, HB, CB, Y = g.bank[0], g.bank[1:3], g.bank[3:5], g.bank[5:7]
        block = ctx.enter_context(nc.Block())

        def rows(u):
            return P if u < U - 1 else HID

        @block.vector
        def _(dve):
            def front(m, p):
                front_vector(dve, s, g, cfg, m, p)

            def body(n, p, has_next):
                if has_next:
                    front(n + 1, 1 - p)
                for u in range(U):
                    r = rows(u)
                    dve.wait_ge(s.silu_done, U * n + u + 1)
                    if u >= 3:
                        dve.wait_ge(s.used, U * n + u - 2)
                    a = g.prob[u % 3][0:r, 0:T]
                    dve.tensor_tensor(out=a, in0=g.silu[u % 2][0:r, :], in1=HB[u % 2][0:r, T:2 * T], op=ALU.mult
                                      ).then_inc(s.gated, 1)
                    if u < U - 1:
                        dve.wait_ge(s.gated, U * n + u + 1)
                        dve.tensor_tensor(out=a, in0=a, in1=CB[u % 2][:, 0:T], op=ALU.mult).then_inc(s.scaled, 1)
                dve.wait_ge(s.used, U * (n + 1))
                for t in range(NT):
                    last = dve.tensor_tensor(out=tile_of(cfg.target, n, t)[:, 0, :], in0=Y[t][:, 0:C],
                                             in1=tile_of(cfg.residual, n, t)[:, 0, :], op=ALU.add)
                last.then_inc(s.target_ready, 1)

            per_element(dve, lambda: front(0, 0), body)

        @block.gpsimd
        def _(pool):
            per_element(pool, lambda: front_pool(pool, s, g, cfg, 0),
                      lambda n, p, nx: front_pool(pool, s, g, cfg, n + 1) if nx else None)

        @block.scalar
        def _(act):
            def front(m, p):
                act.wait_ge(s.xt_full, m + 1)
                act.activation(g.xT[p][:, :], XT[:, 0:T], ACT.Copy).then_inc(s.xt_ready, 1)

            def body(n, p, has_next):
                if has_next:
                    front(n + 1, 1 - p)
                for u in range(U):
                    act.wait_ge(s.hidden_full, U * n + u + 1)
                    if u >= 2:
                        act.wait_ge(s.gated, U * n + u - 1)
                    act.activation(g.silu[u % 2][0:rows(u), :], HB[u % 2][0:rows(u), 0:T], ACT.Silu
                                   ).then_inc(s.silu_done, 1)

            per_element(act, lambda: front(0, 0), body)

        @block.tensor
        def _(pe):
            cfg.loaded(pe)

            def front(m, p):
                wait_normed(pe, s, cfg, m)
                for t in range(NT):
                    last = pe.transpose(XT[:, t * P:(t + 1) * P], g.xn[p][:, t, :], g.ident[:, :])
                last.then_inc(s.xt_full, 1)

            def hidden(n, u, p):
                if u >= 2:
                    pe.wait_ge(s.gated, U * n + u - 1)
                    wait_apart(pe, s.scaled, (U - 1) * n + u - 1)
                r = rows(u)
                w1 = cfg.w1[:, u * P:(u + 1) * P] if u < U - 1 else cfg.sw1[:, :]
                w3 = cfg.w3[:, u * P:(u + 1) * P] if u < U - 1 else cfg.sw3[:, :]
                if u < U - 1:
                    comb = g.combT[:, bass.ds(T * n, T)] if not isinstance(n, int) else g.combT[:, T * n:T * n + T]
                    pe.matmul(CB[u % 2][:, 0:T], g.sel_expert[:, u, :], comb, start=True, stop=True)
                pe.matmul(HB[u % 2][0:r, 0:T], w1, g.xT[p][:, :], start=True, stop=True)
                pe.matmul(HB[u % 2][0:r, T:2 * T], w3, g.xT[p][:, :], start=True, stop=True).then_inc(s.hidden_full, 1)

            def output(n, u):
                r = rows(u)
                if u < U - 1:
                    pe.wait_ge(s.scaled, (U - 1) * n + u + 1)
                else:
                    pe.wait_ge(s.gated, U * n + u + 1)
                if u == 0 and isinstance(n, int) and n > 0:
                    pe.wait_ge(s.target_ready, n)
                w2 = cfg.w2[:, u, :] if u < U - 1 else cfg.sw2[:, :]
                for t in range(NT):
                    last = pe.matmul(Y[t][:, 0:C], g.prob[u % 3][0:r, t * P:(t + 1) * P], w2,
                                     start=(u == 0), stop=(u == U - 1))
                last.then_inc(s.used, 1)

            def body(n, p, has_next):
                pe.wait_ge(s.xt_ready, n + 1)
                if has_next:
                    front(n + 1, 1 - p)
                for u in range(U + 1):
                    if u < U:
                        hidden(n, u, p)
                    if u >= 1:
                        output(n, u - 1)

            per_element(pe, lambda: front(0, 0), body)



def quantise(dve, s, q, buf, source, p, n):
    peak, guard, recip, level, rounded, clipped = q
    dve.tensor_reduce(buf.peak[:, :], source, AX_X, ALU.max, apply_absolute_value=True).then_inc(peak, 1)
    dve.wait_ge(peak, n + 1)
    dve.tensor_scalar(buf.peakc[:, :], buf.peak[:, :], 1e-5, None, ALU.max).then_inc(guard, 1)
    dve.wait_ge(guard, n + 1)
    dve.reciprocal(buf.recip[:, :], buf.peakc[:, :]).then_inc(recip, 1)
    dve.wait_ge(recip, n + 1)
    dve.tensor_scalar(buf.scale[:, :], buf.recip[:, :], 127.0, None, ALU.mult)
    dve.tensor_scalar(buf.level[p][:, :], buf.peakc[:, :], 1.0 / 127.0, buf.wlevel, ALU.mult, ALU.mult
                      ).then_inc(level, 1)
    dve.wait_ge(level, n + 1)
    for t in range(NT):
        dve.tensor_scalar(source[:, t, :], source[:, t, :], buf.scale[:, t:t + 1], ROUND, ALU.mult, ALU.add
                          ).then_inc(rounded, 1)
    dve.wait_ge(rounded, NT * (n + 1))
    dve.tensor_scalar(source, source, ROUND + 127.0, ROUND - 128.0, ALU.min, ALU.max).then_inc(clipped, 1)


def quantised_feed_forward(nc, g, name, cfg):
    HT, F = 4, 512
    Q = "peak guard recip level rounded clipped"
    with ExitStack() as ctx:
        s = sem_space(nc, ctx, name, LN_SEMS + " low_a at_full at_ready hidden_full biased geled "
                      "stats_h mean_h veps_h rstd_h norm_h gain_h shift_h low_b bt_full bt_ready out_full "
                      "residual_added target_ready " + " ".join(f"{x}_{k}" for k in "ab" for x in Q.split()))
        qa = (s.peak_a, s.guard_a, s.recip_a, s.level_a, s.rounded_a, s.clipped_a)
        qb = (s.peak_b, s.guard_b, s.recip_b, s.level_b, s.rounded_b, s.clipped_b)
        hid = [g.qT[p][:, 0:NT * F].rearrange("p (t f) -> p t f", t=NT) for p in range(2)]
        intsT = [g.qh[p][:, 0:HT * T].rearrange("p (n q) -> p n q", n=HT) for p in range(2)]
        ints_b = g.kh[0][:, 0:NT * F].rearrange("p (t f) -> p t f", t=NT)
        ints_a = g.kh[1][:, 0:NT * C].rearrange("p (t f) -> p t f", t=NT)
        xTh = g.negmaxT[0]
        AT, HB, BT, OUT = g.bank[0], g.bank[1:5], g.bank[5], g.bank[6:8]
        block = ctx.enter_context(nc.Block())
        load_later(block, cfg)

        @block.vector
        def _(dve):
            def front(m, p):
                front_vector(dve, s, g, cfg, m, p)
                quantise(dve, s, qa, g.quant_a, g.xn[p][:, :, :], p, m)
                for t in range(NT):
                    dve.wait_ge(s.hidden_full, NT * m + t + 1)
                    last = dve.scalar_tensor_tensor(out=hid[p][:, t, :], in0=HB[2 * p + t][:, :],
                                                    scalar=g.quant_a.level[p][:, t:t + 1], in1=cfg.b1,
                                                    op0=ALU.mult, op1=ALU.add)
                last.then_inc(s.biased, 1)

            def tail(n, p):
                h = hid[p]
                wait_apart(dve, s.geled, n + 1)
                for t in range(NT):
                    dve.bn_stats(g.stats[0][:, t, :], h[:, t, :]).then_inc(s.stats_h, 1)
                wait_apart(dve, s.stats_h, NT * (n + 1))
                for t in range(NT):
                    dve.bn_aggr(g.mvh[:, t, :], g.stats[0][:, t, :]).then_inc(s.mean_h, 1)
                dve.wait_ge(s.mean_h, NT * (n + 1))
                dve.wait_ge(s.rstd_h, n + 1)
                for t in range(NT):
                    dve.tensor_scalar(h[:, t, :], h[:, t, :], g.mvh[:, t, 0:1], g.rstdh[:, t:t + 1],
                                      ALU.subtract, ALU.mult).then_inc(s.norm_h, 1)
                dve.wait_ge(s.norm_h, NT * (n + 1))
                dve.tensor_tensor(out=h, in0=h, in1=cfg.gain2.unsqueeze(1).to_broadcast([P, NT, F]), op=ALU.mult
                                  ).then_inc(s.gain_h, 1)
                dve.wait_ge(s.gain_h, n + 1)
                dve.tensor_tensor(out=h, in0=h, in1=cfg.shift2.unsqueeze(1).to_broadcast([P, NT, F]), op=ALU.add
                                  ).then_inc(s.shift_h, 1)
                dve.wait_ge(s.shift_h, n + 1)
                quantise(dve, s, qb, g.quant_b, h, p, n)
                dve.wait_ge(s.out_full, n + 1)
                dve.wait_ge(s.residual_added, n + 1)
                for t in range(NT):
                    last = dve.scalar_tensor_tensor(out=tile_of(cfg.target, n, t)[:, 0, :], in0=OUT[p][:, t * P:(t + 1) * P],
                                                    scalar=g.quant_b.level[p][:, t:t + 1], in1=g.resb[p][:, t, :],
                                                    op0=ALU.mult, op1=ALU.add)
                last.then_inc(s.target_ready, 1)

            def body(n, p, has_next):
                if has_next:
                    front(n + 1, 1 - p)
                tail(n, p)

            per_element(dve, lambda: front(0, 0), body)

        @block.gpsimd
        def _(pool):
            def front(m, p):
                front_pool(pool, s, g, cfg, m)
                pool.tensor_tensor(out=g.resb[p][:, :, :], in0=tokens(cfg.residual, m),
                                   in1=cfg.bias.unsqueeze(1).to_broadcast([P, NT, C]),
                                   op=ALU.add).then_inc(s.residual_added, 1)

            def body(n, p, has_next):
                if has_next:
                    front(n + 1, 1 - p)
                wait_apart(pool, s.mean_h, NT * (n + 1))
                pool.tensor_scalar(g.veps[0][:, :], g.mvh[:, :, 1], EPS, None, ALU.add).then_inc(s.veps_h, 1)
                pool.wait_ge(s.veps_h, n + 1)
                pool.tensor_tensor(out=g.rstdh[:, :], in0=g.veps[0][:, :], in1=g.minus_half[:, :],
                                   op=ALU.pow).then_inc(s.rstd_h, 1)

            per_element(pool, lambda: front(0, 0), body)

        @block.scalar
        def _(act):
            def front(m, p):
                act.wait_ge(s.clipped_a, m + 1)
                act.activation(ints_a, g.xn[p][:, :, :], ACT.Identity, bias=g.minus_round[:, :]).then_inc(s.low_a, 1)
                act.wait_ge(s.at_full, m + 1)
                act.activation(xTh[:, :], AT[:, 0:P].bitcast(BF16), ACT.Copy).then_inc(s.at_ready, 1)
                act.wait_ge(s.biased, m + 1)
                act.activation(hid[p], hid[p], ACT.Gelu).then_inc(s.geled, 1)

            def body(n, p, has_next):
                if has_next:
                    front(n + 1, 1 - p)
                act.wait_ge(s.clipped_b, n + 1)
                act.activation(ints_b, hid[p], ACT.Identity, bias=g.minus_round[:, :]).then_inc(s.low_b, 1)
                act.wait_ge(s.bt_full, n + 1)
                act.activation(intsT[p][:, :, :], BT[:, :].bitcast(BF16).rearrange("p (n q) -> p n q", n=HT),
                               ACT.Copy).then_inc(s.bt_ready, 1)

            per_element(act, lambda: front(0, 0), body)

        @block.tensor
        def _(pe):
            def front(m, p):
                pe.wait_ge(s.low_a, m + 1)
                for t in range(NT):
                    last = pe.transpose(AT[:, 0:P].bitcast(BF16)[:, t * P:(t + 1) * P], ints_a[:, t, :], g.identh[:, :])
                last.then_inc(s.at_full, 1)
                pe.wait_ge(s.at_ready, m + 1)
                for t in range(NT):
                    pe.matmul(HB[2 * p + t][:, :], xTh[:, t * P:(t + 1) * P], cfg.w1[:, :], start=True, stop=True
                              ).then_inc(s.hidden_full, 1)

            def body(n, p, has_next):
                if has_next:
                    front(n + 1, 1 - p)
                pe.wait_ge(s.low_b, n + 1)
                for k in range(HT):
                    for t in range(NT):
                        last = pe.transpose(BT[:, :].bitcast(BF16)[:, k * T + t * P:k * T + (t + 1) * P],
                                            ints_b[:, t, k * P:(k + 1) * P], g.identh[:, :])
                last.then_inc(s.bt_full, 1)
                pe.wait_ge(s.bt_ready, n + 1)
                for t in range(NT):
                    for k in range(HT):
                        last = pe.matmul(OUT[p][:, t * P:(t + 1) * P], intsT[p][:, k, t * P:(t + 1) * P],
                                         cfg.w2[:, k, :], start=(k == 0), stop=(k == HT - 1))
                last.then_inc(s.out_full, 1)

            per_element(pe, lambda: front(0, 0), body)



def routed_experts(nc, g, name, cfg, out):
    E = cfg.experts
    with ExitStack() as ctx:
        s = sem_space(nc, ctx, name, LN_SEMS + GATE_SEMS + " xt_full xt_ready experts_full summed_in "
                      "sentinels stored started")
        XT, LG, EX = g.bank[0:2], g.bank[2:4], g.bank[4:8]
        gb = g.gate
        out_v = out.rearrange("b (t p) c -> p (b t) c", p=P)
        block = ctx.enter_context(nc.Block())

        @block.sync
        def _(sp):
            def body(n, p, has_next):
                sp.wait_ge(s.summed_in, NT * E * (n + 1))
                dst = out_v[:, bass.ds(NT * n, NT), :] if not isinstance(n, int) else out_v[:, NT * n:NT * n + NT, :]
                sp.dma_start(dst, tokens(cfg.target, n)).then_inc(s.stored, 16)

            per_element(sp, lambda: None, body)
            sp.wait_ge(s.stored, 16 * B)

        @block.vector
        def _(dve):
            dve.memset(gb.probs[:, :, :], -1.0)
            dve.memset(gb.keys[:, :, :], -1.0).then_inc(s.sentinels, 1)
            dve.wait_ge(s.sentinels, 1)

            def front(m, p):
                front_vector(dve, s, g, cfg, m, p)

            def tail(n, p):
                gate_vector(dve, s, g, cfg, n, p, LG[p])
                c = gb.c[p]
                dve.tensor_tensor(out=gb.w[:, :, 0:E], in0=c[:, :, 0:E], in1=gb.probs[:, :, 0:E], op=ALU.mult
                                  ).then_inc(s.pbias, 1)
                dve.wait_ge(s.pbias, n + 1)
                dve.tensor_reduce(gb.wsum[:, :], gb.w[:, :, 0:E], AX_X, ALU.add).then_inc(s.pbias_sum, 1)
                dve.wait_ge(s.pbias_sum, n + 1)
                for t in range(NT):
                    last = dve.tensor_scalar(g.resb[p][:, t, :], tile_of(cfg.residual, n, t)[:, 0, :],
                                             gb.wsum[:, t:t + 1], None, ALU.add)
                last.then_inc(s.started, 1)
                dve.wait_ge(s.started, n + 1)
                for e in range(E):
                    for t in range(NT):
                        if e % 4 == 0:
                            dve.wait_ge(s.experts_full, 4 * n + 2 * (e // 4) + t + 1)
                        if e:
                            dve.wait_ge(s.summed_in, NT * (E * n + e - 1) + t + 1)
                        acc = g.resb[p][:, t, :]
                        dst = acc if e < E - 1 else tile_of(cfg.target, n, t)[:, 0, :]
                        dve.scalar_tensor_tensor(out=dst, in0=EX[2 * (e // 4) + t][:, (e % 4) * P:(e % 4 + 1) * P],
                                                 scalar=c[:, t, e:e + 1], in1=acc, op0=ALU.mult, op1=ALU.add
                                                 ).then_inc(s.summed_in, 1)

            def body(n, p, has_next):
                if has_next:
                    front(n + 1, 1 - p)
                tail(n, p)

            per_element(dve, lambda: front(0, 0), body)

        @block.gpsimd
        def _(pool):
            per_element(pool, lambda: front_pool(pool, s, g, cfg, 0),
                      lambda n, p, nx: front_pool(pool, s, g, cfg, n + 1) if nx else None)

        @block.scalar
        def _(act):
            def front(m, p):
                act.wait_ge(s.xt_full, m + 1)
                act.activation(g.xT[p][:, :], XT[p][:, 0:T], ACT.Copy).then_inc(s.xt_ready, 1)

            def body(n, p, has_next):
                if has_next:
                    front(n + 1, 1 - p)
                gate_exp(act, s, g, cfg, n)

            per_element(act, lambda: front(0, 0), body)

        @block.tensor
        def _(pe):
            cfg.loaded(pe)

            def front(m, p):
                wait_normed(pe, s, cfg, m)
                for t in range(NT):
                    last = pe.transpose(XT[p][:, t * P:(t + 1) * P], g.xn[p][:, t, :], g.ident[:, :])
                last.then_inc(s.xt_full, 1)
                pe.wait_ge(s.xt_ready, m + 1)
                for t in range(NT):
                    last = pe.matmul(LG[p][:, t * E:(t + 1) * E], g.xT[p][:, t * P:(t + 1) * P], cfg.gate_w[:, :],
                                     start=True, stop=True)
                last.then_inc(s.logits_full, 1)

            def body(n, p, has_next):
                if isinstance(n, int) and n > 0:
                    pe.wait_ge(s.summed_in, NT * E * n)
                if has_next:
                    front(n + 1, 1 - p)
                for k in range(2):
                    for t in range(NT):
                        pe.matmul(EX[2 * k + t][:, :], g.xT[p][:, t * P:(t + 1) * P],
                                  cfg.w[:, 4 * k * P:4 * (k + 1) * P], start=True, stop=True
                                  ).then_inc(s.experts_full, 1)

            per_element(pe, lambda: front(0, 0), body)



def prepare(nc, g, w, dram):
    with ExitStack() as ctx:
        s = sem_space(nc, ctx, "prepare", "zeroed built")
        block = ctx.enter_context(nc.Block())

        @block.sync
        def _(sp):
            sp.dma_start(g.X[:, :, :], dram.x.rearrange("b (t p) c -> p (b t) c", p=P)).then_inc(w.sem_x, 16)
            for dst, src, sem in w.loads:
                sp.dma_start(dst, src).then_inc(sem, 16)
            sp.wait_ge(w.sem_x, 16)
            sp.wait_ge(w.sem_small, 16 * w.small_count)

        @block.gpsimd
        def _(pool):
            pool.memset(g.ident[:, :], 0.0)
            pool.memset(g.identh[:, :], 0.0)
            pool.memset(g.causal[:, :], 0.0)
            pool.memset(g.ones[:, :], 1.0)
            pool.memset(g.sel_head[:, :, :], 1.0)
            pool.memset(g.sel_pair[:, :, :], 1.0)
            for part in g.sel_part:
                pool.memset(part[:, :, :], 1.0)
            pool.memset(g.minus_half[:, :], -0.5)
            pool.memset(g.minus_round[:, :], -ROUND)
            pool.memset(g.negmax4[:, :, :, :], 0.0)
            for hm in g.head_mask.values():
                last = pool.memset(hm[:, :], 1.0)
            last.then_inc(s.zeroed, 1)
            pool.wait_ge(s.zeroed, 1)

            count = [0]

            def keep(view, cmp, fill, base, pattern, mult):
                pool.affine_select(out=view, in_=view, compare_op=cmp, fill=fill, base=base, pattern=pattern,
                                   channel_multiplier=mult).then_inc(s.built, 1)
                count[0] += 1
                pool.wait_ge(s.built, count[0])

            for ident in (g.ident, g.identh):
                keep(ident[:, :], ALU.not_equal, 1.0, 0, [[-1, P]], 1)
            keep(g.causal[:, :], ALU.is_ge, MASKED, 0, [[-1, P]], 1)
            keep(g.sel_head[:, :, :].rearrange("p (g j) k -> p g j k", g=G), ALU.is_equal, 0.0, 0,
                 [[-HG, G], [-(SLOT + 1), HG], [0, P]], 1)
            keep(g.sel_pair[:, :, :].rearrange("p j (i k) -> p j i k", i=2), ALU.is_equal, 0.0, 0,
                 [[-2, PAIRS], [-1, 2], [0, TC]], 1)
            for part in range(3):
                view = g.sel_part[part][:, :, :].rearrange("p j (i k) -> p j i k", i=2)
                keep(view, ALU.is_equal, 0.0, -16 * part, [[-2, PAIRS], [-1, 2], [0, 64]], 1)
            for D, hm in g.head_mask.items():
                keep(hm[:, :], ALU.is_ge, 0.0, 0, [[-D, P // D]], 1)
                keep(hm[:, :], ALU.is_ge, 0.0, D - 1, [[D, P // D]], -1)
            pool.tensor_tensor(out=g.sel_part[0][:, :, :], in0=g.sel_part[0][:, :, :], in1=g.sel_part[1][:, :, :],
                               op=ALU.add).then_inc(s.built, 1)
            pool.wait_ge(s.built, count[0] + 1)
            pool.tensor_tensor(out=g.sel_expert[:, :, :], in0=g.sel_part[0][0:48, :, :], in1=g.sel_part[2][0:48, :, :],
                               op=ALU.add).then_inc(s.built, 1)


def load_later(block, cfg):
    if cfg.loads:
        @block.sync
        def _(sp):
            for dst, src, sem in cfg.loads:
                sp.dma_start(dst, src).then_inc(sem, 16)


def normalise_context(nc, g, w, v):
    n = B * TC // P
    with ExitStack() as ctx:
        s = sem_space(nc, ctx, "context", "stats mean veps rstd norm full done")
        raw, st, mv, ve, rs = g.ctx_tok, g.ctx_stats, g.ctx_mv, g.ctx_veps, g.ctx_rstd
        block = ctx.enter_context(nc.Block())

        @block.vector
        def _(dve):
            dve.wait_ge(w.sem_ctx, 32)
            for t in range(n):
                dve.bn_stats(st[:, t, :], raw[:, t, :]).then_inc(s.stats, 1)
            dve.wait_ge(s.stats, n)
            for t in range(n):
                dve.bn_aggr(mv[:, t, :], st[:, t, :]).then_inc(s.mean, 1)
            dve.wait_ge(s.rstd, 1)
            for t in range(n):
                dve.tensor_scalar(raw[:, t, :], raw[:, t, :], mv[:, t, 0:1], rs[:, t:t + 1], ALU.subtract, ALU.mult
                                  ).then_inc(s.norm, 1)

        @block.gpsimd
        def _(pool):
            pool.wait_ge(s.mean, n)
            pool.tensor_scalar(ve[:, :], mv[:, :, 1], EPS, None, ALU.add).then_inc(s.veps, 1)
            pool.wait_ge(s.veps, 1)
            pool.memset(g.ctx_half[:, :], -0.5).then_inc(s.veps, 1)
            pool.wait_ge(s.veps, 2)
            pool.tensor_tensor(out=rs[:, :], in0=ve[:, :], in1=g.ctx_half[:, :], op=ALU.pow).then_inc(s.rstd, 1)

        @block.tensor
        def _(pe):
            pe.wait_ge(s.norm, n)
            for t in range(n):
                mm = pe.transpose(g.bank[t // 4][0:CC, (t % 4) * P:(t % 4 + 1) * P], raw[:, t, :], g.ident[:, :])
                if t % 4 == 3:
                    mm.then_inc(s.full, 1)

        @block.scalar
        def _(act):
            for k in range(n // 4):
                act.wait_ge(s.full, k + 1)
                act.activation(g.ctxnT[:, k * 4 * NT:(k + 1) * 4 * NT, :],
                               g.bank[k][0:CC, :].rearrange("p (b k) -> p b k", k=TC),
                               ACT.Identity, scale=v.ctx_gain, bias=v.ctx_shift).then_inc(s.done, 1)


def ternary_weights(nc, g, name, w, sem, value, pairs, mode):
    with ExitStack() as ctx:
        s = sem_space(nc, ctx, name, "sums total mean recip scaled rounded clipped")
        block = ctx.enter_context(nc.Block())
        k = len(pairs)

        @block.vector
        def _(dve):
            dve.wait_ge(sem, value)
            for i, (src, _dst, _level) in enumerate(pairs):
                dve.tensor_reduce(g.tern_sum[:, i:i + 1], src, AX_X, ALU.add, apply_absolute_value=True
                                  ).then_inc(s.sums, 1)
            dve.wait_ge(s.total, 1)
            scale = 1.0 / (C * 512)
            for i, (_src, _dst, level) in enumerate(pairs):
                dve.tensor_scalar(level, g.bank[0][:, i:i + 1], scale, EPS, ALU.mult,
                                  ALU.add if mode == "added" else ALU.max).then_inc(s.mean, 1)
            dve.wait_ge(s.mean, k)
            for i, (_src, _dst, level) in enumerate(pairs):
                dve.reciprocal(g.tern_recip[:, i:i + 1], level).then_inc(s.recip, 1)
            dve.wait_ge(s.recip, k)
            for i, (src, _dst, _level) in enumerate(pairs):
                dve.tensor_scalar(src, src, g.tern_recip[:, i:i + 1], ROUND, ALU.mult, ALU.add).then_inc(s.scaled, 1)
            dve.wait_ge(s.scaled, k)
            for src, _dst, _level in pairs:
                dve.tensor_scalar(src, src, ROUND, 1.0, ALU.subtract, ALU.min).then_inc(s.rounded, 1)
            dve.wait_ge(s.rounded, k)
            for src, dst, _level in pairs:
                dve.tensor_scalar(dst, src, -1.0, None, ALU.max).then_inc(s.clipped, 1)

        @block.tensor
        def _(pe):
            pe.wait_ge(s.sums, k)
            pe.matmul(g.bank[0][:, 0:k], g.ones[:, :], g.tern_sum[:, 0:k], start=True, stop=True).then_inc(s.total, 1)


ROWS = ["L0_xattn_bv", "L0_xattn_bcv", "L0_xattn_bp", "L1_xattn_ln1_g", "L1_xattn_ln1_b", "L1_xattn_ln2_g",
        "L1_xattn_ln2_b", "L1_xattn_a1_li1_b", "L1_xattn_a1_li3_b", "L1_xattn_a2_li1_b", "L1_xattn_a2_li3_b",
        "L1_ffn_b2", "L2_ffn_ln1_g", "L2_ffn_ln1_b", "L2_ffn_b1", "L2_ffn_ln2_g", "L2_ffn_ln2_b", "L2_ffn_b2",
        "L3_xattn_bo"]


def build(nc, dram, cols, rows):
    with ExitStack() as ctx:
        def sb(name, shape, dt=F32):
            return ctx.enter_context(nc.sbuf_tensor(name, shape, dt))

        def sem(name):
            return ctx.enter_context(nc.semaphore(name))

        def two(name, shape, dt=F32):
            return [sb(f"{name}{p}", shape, dt) for p in range(2)]

        g = Store()
        g.X, g.A, g.XA = (sb(n, [P, B * NT, C]) for n in ("X", "A", "XA"))
        g.xn, g.xT, g.yT, g.resb = two("xn", [P, NT, C]), two("xT", [P, T]), two("yT", [P, T]), two("resb", [P, NT, C])
        g.qT, g.qh = two("qT", [P, 8 * T]), two("qh", [P, 8 * T], BF16)
        g.kT, g.kh = two("kT", [P, G * T]), two("kh", [P, G * T], BF16)
        g.V = two("V", [P, NT * H * (SLOT + 1)])
        g.kmask, g.kmaskh = g.kT, g.kh
        g.ctxb = two("ctxb", [CC, 2, TC])
        g.prob = [sb(f"prob{i}", [P, 512]) for i in range(3)]
        g.probsum, g.rec = [sb(f"probsum{i}", [P, T]) for i in range(3)], sb("rec", [P, T])
        g.probm = [sb(f"probm{i}", [P, NT, P]) for i in range(3)]
        g.silu = g.yT
        g.osb, g.oT = sb("osb", [P, NT * H * 64]), sb("oT", [P, 8 * T])
        g.negmax, g.negmax4 = sb("negmax", [P, NT, H]), sb("negmax4", [P, NT, 4, SLOT], BF16)
        g.negmaxT = two("negmaxT", [P, T], BF16)
        g.recip, g.recip16 = sb("recip", [P, NT, 8]), sb("recip16", [P, NT, H])
        g.stats = [sb(f"stats{k}", [P, NT, 6]) for k in range(3)]
        g.mv = [sb(f"mv{k}", [P, NT, 2]) for k in range(3)]
        g.veps = [sb(f"veps{k}", [P, NT]) for k in range(3)]
        g.rstd = [sb(f"rstd{k}", [P, NT]) for k in range(3)]
        g.mvh, g.rstdh = sb("mvh", [P, NT, 2]), sb("rstdh", [P, NT])
        g.ident, g.identh = sb("ident", [P, P]), sb("identh", [P, P], BF16)
        g.causal, g.ones = sb("causal", [P, P], BF16), sb("ones", [P, P])
        g.sel_head, g.sel_pair = sb("sel_head", [P, H, P], BF16), sb("sel_pair", [P, PAIRS, P], BF16)
        g.sel_part = [g.qT[0][:, :].bitcast(BF16)[:, i * PAIRS * P:(i + 1) * PAIRS * P]
                      .rearrange("p (j k) -> p j k", j=PAIRS) for i in range(3)]
        g.sel_expert = sb("sel_expert", [48, PAIRS, P], BF16)
        g.head_mask = {D: sb(f"head_mask{D}", [P, P // D]) for D in (8, 32, 64)}
        g.minus_half, g.minus_round = sb("minus_half", [P, NT]), sb("minus_round", [P, 1])
        g.gate = record(
            nmax=sb("g_nmax", [P, NT]), e=sb("g_e", [P, NT, 16]), sum=sb("g_sum", [P, NT]), rsum=sb("g_rsum", [P, NT]),
            probs=sb("g_probs", [P, NT, 24]), top=sb("g_top", [P, NT, 8]), keys=sb("g_keys", [P, NT, 8]),
            marked=sb("g_marked", [P, NT, 24]), w=sb("g_w", [P, NT, 16]), wsum=sb("g_wsum", [P, NT]),
            wguard=sb("g_wguard", [P, NT]), wrecip=sb("g_wrecip", [P, NT]), c=two("g_c", [P, NT, 16]),
            part=two("g_part", [P, NT, 3, 16], BF16), rest=sb("g_rest", [P, 1, NT, 16]))
        g.combT = g.XA[0:48, :, :].rearrange("p t c -> p (t c)").bitcast(BF16)[:, 0:B * T]
        n_ctx = B * TC // P
        g.ctx_tok, g.ctx_stats = sb("ctx_tok", [P, n_ctx, CC]), sb("ctx_stats", [P, n_ctx, 6])
        g.ctx_mv, g.ctx_veps = sb("ctx_mv", [P, n_ctx, 2]), sb("ctx_veps", [P, n_ctx])
        g.ctx_rstd, g.ctx_half = sb("ctx_rstd", [P, n_ctx]), sb("ctx_half", [P, n_ctx])
        g.ctxnT, ctxT = sb("ctxnT", [CC, B, TC]), sb("ctxT", [CC, B, TC])
        g.tern_sum, g.tern_recip = sb("tern_sum", [P, 2]), sb("tern_recip", [P, 2])
        g.bank = [ctx.enter_context(nc.psum_tensor(f"bank{i}", [P, 512], F32)) for i in range(8)]

        w = record(loads=[], sem_x=sem("x_loaded"), sem_small=sem("small_loaded"), sem_ctx=sem("ctx_loaded"),
                            small_count=2)
        row_tile = sb("row_tile", [P, dram.rows.shape[0]])
        col_tile = sb("col_tile", [P, dram.cols.shape[1]])
        w.loads.extend([(row_tile[:, :], dram.rows.partition_broadcast(P), w.sem_small), (col_tile[:, :], dram.cols, w.sem_small),
                    (ctxT[:, :, :], dram.ctxT, w.sem_ctx),
                    (g.ctx_tok[:, :, :], dram.ctx.rearrange("b k c -> (b k) c").rearrange("(n p) c -> p n c", p=P), w.sem_ctx)])

        def row(name):
            a, n = rows[name]
            return row_tile[:, a:a + n]

        def col(name, count=1):
            a, _ = cols[name]
            return col_tile[:, a:a + count]

        layer = [(sem(f"weights{i}_loaded"), [0]) for i in range(7)]
        later = {k: [] for k in range(3, 7)}

        flat = lambda x: x[:, :, :].rearrange("p t c -> p (t c)")
        first, second = sb("weights_first", [P, 5648]), sb("weights_second", [P, 3072])
        region = {0: first[:, :], 1: first[:, :], 2: second[:, :], 3: first[:, :], 4: second[:, :], 5: flat(g.A),
                  6: flat(g.XA)}
        starts = {0: 0, 2: 0, 3: 0, 4: 0, 5: 0, 6: 0}

        def weight(name, k, shape):
            src = dram.weights[name]
            start = 0 if k == 1 else k
            n = int(np.prod(shape[1:]))
            at = starts[start]
            starts[start] += n
            assert starts[start] <= region[k].shape[1], name
            view = region[k][0:shape[0], at:at + n]
            if len(shape) == 3:
                view = view.rearrange("p (k c) -> p k c", k=shape[1])
            (w.loads if k <= 2 else later[k]).append((view, src, layer[k][0]))
            layer[k][1][0] += 16
            return view

        def loaded(k, and_ctx=False):
            def wait_for(eng):
                eng.wait_ge(layer[k][0], layer[k][1][0])
                if and_ctx:
                    eng.wait_ge(w.sem_ctx, 32)
            return wait_for

        W = record(
            q0=weight("L0_q", 0, [P, G * P]), k0=weight("L0_k", 0, [P, G * P]), v0=weight("L0_v", 0, [P, P]),
            cq0=weight("L0_cq", 0, [P, P]), ck0=weight("L0_ck", 0, [CC, P]), cv0=weight("L0_cv", 0, [CC, P]),
            p0=weight("L0_p", 0, [P, 1, C]), ps0=weight("L0_ps", 0, [P, G, C]),
            gate0=weight("L0_gate", 1, [P, 16]), w10=weight("L0_w1", 1, [P, 1024]), w30=weight("L0_w3", 1, [P, 1024]),
            w20=weight("L0_w2", 1, [P, 8, C]), sw1=weight("L0_sw1", 1, [P, 64]), sw3=weight("L0_sw3", 1, [P, 64]),
            sw2=weight("L0_sw2", 1, [64, C]),
            q1=weight("L1_q1", 2, [P, 512]), k1=weight("L1_k1", 2, [P, 512]), v1=weight("L1_v1", 2, [P, 512]),
            o1=weight("L1_o1", 2, [P, 4, C]), f1=weight("L1_f1", 2, [P, 512]), e1=weight("L1_e1", 2, [P, 4, C]),
            q2=weight("L1_q2", 3, [P, 512]), k2=weight("L1_k2", 3, [CC, 512]), v2=weight("L1_v2", 3, [CC, 512]),
            o2=weight("L1_o2", 3, [P, 4, C]), f2=weight("L1_f2", 3, [P, 512]), e2=weight("L1_e2", 3, [P, 4, C]),
            t1=weight("L1_w1", 3, [P, 512]), t2=weight("L1_w2", 3, [P, 4, C]),
            l2q=weight("L2_q", 4, [P, P]), l2k=weight("L2_k", 4, [CC, P]), l2v=weight("L2_v", 4, [CC, P]),
            l2o=weight("L2_o", 4, [P, 1, C]), l2w1=weight("L2_w1", 4, [P, 512]), l2w2=weight("L2_w2", 4, [P, 4, C]),
            q3=weight("L3_q", 5, [P, 1024]), k3=weight("L3_k", 5, [CC, 1024]), v3=weight("L3_v", 5, [CC, 1024]),
            o3=weight("L3_o", 5, [P, 8, C]), gate3=weight("L3_gate", 6, [P, 8]), w3=weight("L3_w", 6, [P, 8 * C]))
        w1q, w2q = sb("w1q", [P, 512], BF16), sb("w2q", [P, 4, C], BF16)
        levels = sb("levels", [P, 4])
        for k in "ab":
            buf = record(peak=sb(f"peak_{k}", [P, NT]), peakc=sb(f"peakc_{k}", [P, NT]),
                                  recip=sb(f"qrecip_{k}", [P, NT]), scale=sb(f"qscale_{k}", [P, NT]),
                                  level=two(f"level_{k}", [P, NT]),
                                  wlevel=levels[:, 2:3] if k == "a" else levels[:, 3:4])
            if k == "a":
                g.quant_a = buf
            else:
                g.quant_b = buf

        plain = [(None, None, None)]
        att = dict(q_gain=None, q_shift=None, kv_gain=None, kv_shift=None, bq=None, bk=None, bv=None, bias=None,
                   wide_v=0, causal=False, norms=plain, loads=())
        prepare(nc, g, w, dram)
        self_attention(nc, g, "own0", record(**(att | dict(
            source=g.X, residual=g.X, target=g.A, D=8, scale=8 ** -0.5, causal=True, wq=W.q0, wk=W.k0, wv=W.v0, wo=W.ps0,
            bq=col("bq", 4), bk=col("bk", 4), bv=row("L0_xattn_bv"), bias=row("L0_xattn_bp"), loaded=loaded(0)))))
        cross_attention(nc, g, "ctx0", record(**(att | dict(
            source=g.X, residual=g.A, target=g.A, D=8, scale=8 ** -0.5, ctxT=ctxT, wq=W.cq0, wk=W.ck0, wv=W.cv0, wo=W.p0,
            bq=col("bcq"), bk=col("bck"), bv=row("L0_xattn_bcv"), head_mask=g.head_mask[8], loaded=loaded(0, True)))))
        moe0 = dict(source=g.A, norms=plain, experts=16, top=4, guard=0.0, loaded=loaded(1), loads=())
        route(nc, g, "route0", record(**moe0, gate_w=W.gate0))
        gated_experts(nc, g, "moe0", record(**moe0, residual=g.A, target=g.X, w1=W.w10, w3=W.w30, w2=W.w20,
                                                     sw1=W.sw1, sw3=W.sw3, sw2=W.sw2))
        a1, a2 = "L1_xattn_a1_", "L1_xattn_a2_"
        self_attention(nc, g, "own1", record(**(att | dict(
            source=g.X, residual=g.XA, target=g.A, D=32, scale=32 ** -0.5, wide_v=1,
            norms=[(None, None, None), (row("L1_xattn_ln1_g"), row("L1_xattn_ln1_b"), g.XA), (None, None, None)],
            wq=W.q1, wk=W.k1, wv=W.v1, wo=W.o1, q_gain=col(a1 + "lnx_g"), q_shift=col(a1 + "lnx_b"),
            kv_gain=col(a1 + "lny_g"), kv_shift=col(a1 + "lny_b"), bias=row(a1 + "li1_b"), loaded=loaded(2), loads=later[3]))))
        feed_forward(nc, g, "net1", record(
            source=g.A, norms=plain, residuals=[g.A, g.XA], target=g.A, relu=False, x_gain=col(a1 + "ln3_g"),
            x_shift=col(a1 + "ln3_b"), w1=W.f1, b1=col(a1 + "li2_b", 4), w2=W.e1, bias=row(a1 + "li3_b"), loaded=loaded(2), loads=()))
        normalise_context(nc, g, w, record(ctx_gain=col(a2 + "lny_g")[0:CC, :], ctx_shift=col(a2 + "lny_b")[0:CC, :]))
        cross_attention(nc, g, "ctx1", record(**(att | dict(
            source=g.A, residual=g.XA, target=g.A, D=32, scale=32 ** -0.5, ctxT=g.ctxnT,
            norms=[(row("L1_xattn_ln2_g"), row("L1_xattn_ln2_b"), g.XA), (None, None, None)],
            wq=W.q2, wk=W.k2, wv=W.v2, wo=W.o2, q_gain=col(a2 + "lnx_g"), q_shift=col(a2 + "lnx_b"),
            bias=row(a2 + "li1_b"), head_mask=g.head_mask[32], loaded=loaded(3), loads=later[4]))))
        feed_forward(nc, g, "net2", record(
            source=g.A, norms=plain, residuals=[g.A, g.XA, g.X], target=g.X, relu=False, x_gain=col(a2 + "ln3_g"),
            x_shift=col(a2 + "ln3_b"), w1=W.f2, b1=col(a2 + "li2_b", 4), w2=W.e2, bias=row(a2 + "li3_b"), loaded=loaded(3), loads=()))
        ternary_weights(nc, g, "tern1", w, layer[3][0], layer[3][1][0],
                        [(W.t1[:, :], W.t1[:, :], levels[:, 0:1]),
                         (W.t2[:, :, :].rearrange("p k c -> p (k c)"), W.t2[:, :, :].rearrange("p k c -> p (k c)"),
                          levels[:, 1:2])], "added")
        feed_forward(nc, g, "net3", record(
            source=g.X, norms=plain, residuals=[g.X], target=g.X, relu=True, x_gain=None, x_shift=None,
            w1=W.t1, b1=col("L1_ffn_b1", 4), w2=W.t2, bias=row("L1_ffn_b2"), loaded=loaded(3), loads=later[5] + later[6]))
        cross_attention(nc, g, "ctx2", record(**(att | dict(
            source=g.X, residual=g.X, target=g.X, D=8, scale=8 ** -0.5, ctxT=ctxT, wq=W.l2q, wk=W.l2k, wv=W.l2v,
            wo=W.l2o, head_mask=g.head_mask[8], loaded=loaded(4)))))
        ternary_weights(nc, g, "tern2", w, layer[4][0], layer[4][1][0],
                        [(W.l2w1[:, :], w1q[:, :], levels[:, 2:3]),
                         (W.l2w2[:, :, :].rearrange("p k c -> p (k c)"), w2q[:, :, :].rearrange("p k c -> p (k c)"),
                          levels[:, 3:4])], "clipped")
        quantised_feed_forward(nc, g, "net4", record(
            source=g.X, residual=g.X, target=g.X, norms=[(None, None, None), (row("L2_ffn_ln1_g"), row("L2_ffn_ln1_b"), None)],
            w1=w1q, b1=row("L2_ffn_b1"), gain2=row("L2_ffn_ln2_g"), shift2=row("L2_ffn_ln2_b"), w2=w2q,
            bias=row("L2_ffn_b2"), loads=()))
        cross_attention(nc, g, "ctx3", record(**(att | dict(
            source=g.X, residual=g.X, target=g.X, D=64, scale=64 ** -0.5, ctxT=ctxT, wq=W.q3, wk=W.k3, wv=W.v3,
            wo=W.o3, bias=row("L3_xattn_bo"), head_mask=g.head_mask[64], loaded=loaded(5)))))
        routed_experts(nc, g, "moe3", record(
            source=g.X, residual=g.X, target=g.X, norms=plain, experts=8, top=2, guard=1e-6, gate_w=W.gate3, w=W.w3,
            loaded=loaded(6)), dram.out)


def kernel(**inputs):
    import concourse.bacc as bacc
    from concourse.bass_utils import run_bass_kernel_spmd

    v = {k: np.asarray(a) for k, a in inputs.items()}

    def slots(a):
        out = np.zeros((*a.shape[:-1], G, HG, SLOT), a.dtype)
        out[..., 0:8] = a.reshape(*a.shape[:-1], G, HG, 8)
        return out.reshape(*a.shape[:-1], G * P)

    def heads(a):
        return a.transpose(1, 0, 2).reshape(a.shape[1], -1)

    def tiles(a):
        return a.reshape(-1, P, a.shape[-1]).transpose(1, 0, 2)

    a1, a2 = "L1_xattn_a1_", "L1_xattn_a2_"
    weights = {
        "L0_q": slots(v["L0_xattn_Wq"]), "L0_k": slots(v["L0_xattn_Wk"]), "L0_v": v["L0_xattn_Wv"],
        "L0_cq": v["L0_xattn_Wcq"], "L0_ck": v["L0_xattn_Wck"], "L0_cv": v["L0_xattn_Wcv"],
        "L0_p": tiles(v["L0_xattn_Wp"]), "L0_ps": tiles(slots(v["L0_xattn_Wp"].T).T), "L0_gate": v["L0_ffn_gate_w"].T,
        "L0_w1": v["L0_ffn_w1"].reshape(1024, C).T, "L0_w3": v["L0_ffn_w3"].reshape(1024, C).T,
        "L0_w2": tiles(v["L0_ffn_w2"].transpose(0, 2, 1).reshape(1024, C)),
        "L0_sw1": v["L0_ffn_sw1"].T, "L0_sw3": v["L0_ffn_sw3"].T, "L0_sw2": v["L0_ffn_sw2"].T,
        "L1_q1": heads(v[a1 + "wq"]), "L1_k1": heads(v[a1 + "wk"]), "L1_v1": heads(v[a1 + "wv"]),
        "L1_o1": tiles(v[a1 + "li1_w"]), "L1_f1": v[a1 + "li2_w"], "L1_e1": tiles(v[a1 + "li3_w"]),
        "L1_q2": heads(v[a2 + "wq"]), "L1_k2": heads(v[a2 + "wk"]), "L1_v2": heads(v[a2 + "wv"]),
        "L1_o2": tiles(v[a2 + "li1_w"]), "L1_f2": v[a2 + "li2_w"], "L1_e2": tiles(v[a2 + "li3_w"]),
        "L1_w1": v["L1_ffn_W1"].T, "L1_w2": tiles(v["L1_ffn_W2"].T),
        "L2_q": v["L2_xattn_Wq"].T, "L2_k": v["L2_xattn_Wkv"][0:P].T, "L2_v": v["L2_xattn_Wkv"][P:2 * P].T,
        "L2_o": tiles(v["L2_xattn_Wo"].T), "L2_w1": v["L2_ffn_w1"].T, "L2_w2": tiles(v["L2_ffn_w2"].T),
        "L3_q": v["L3_xattn_Wq"], "L3_k": v["L3_xattn_Wk"], "L3_v": v["L3_xattn_Wv"], "L3_o": tiles(v["L3_xattn_Wo"]),
        "L3_gate": v["L3_ffn_router_w"].T, "L3_w": v["L3_ffn_expert_weights"].transpose(1, 0, 2).reshape(P, 8 * C),
    }
    columns = {"bq": slots(v["L0_xattn_bq"]).reshape(G, P).T, "bk": slots(v["L0_xattn_bk"]).reshape(G, P).T,
               "bcq": v["L0_xattn_bcq"][:, None], "bck": v["L0_xattn_bck"][:, None],
               "L1_ffn_b1": v["L1_ffn_b1"].reshape(4, P).T}
    for a in (a1, a2):
        for n in ("lnx_g", "lnx_b", "lny_g", "lny_b", "ln3_g", "ln3_b"):
            x = v[a + n]
            columns[a + n] = np.concatenate([x, np.zeros(P - len(x), x.dtype)])[:, None]
        columns[a + "li2_b"] = v[a + "li2_b"].reshape(4, P).T
    cols, rows, at = {}, {}, 0
    for n, x in columns.items():
        cols[n] = (at, x.shape[1])
        at += x.shape[1]
    at = 0
    for n in ROWS:
        rows[n] = (at, v[n].shape[0])
        at += v[n].shape[0]

    nc = bacc.Bacc("TRN2", target_bir_lowering=False, num_devices=1)
    arrays = {}

    def feed(name, a):
        a = np.ascontiguousarray(a)
        arrays["in_" + name] = a
        return nc.dram_tensor("in_" + name, a.shape, mybir.dt.from_np(a.dtype), kind="ExternalInput").ap()

    dram = record(
        x=feed("x", v["x"]), ctx=feed("ctx", v["ctx_512"]), ctxT=feed("ctxT", v["ctx_512"].transpose(2, 0, 1)),
        cols=feed("cols", np.concatenate(list(columns.values()), axis=1)),
        rows=feed("rows", np.concatenate([v[n] for n in ROWS])),
        weights={n: feed(n, a) for n, a in weights.items()},
        out=nc.dram_tensor("out_x", (B, T, C), F32, kind="ExternalOutput").ap())
    build(nc, dram, cols, rows)
    r = run_bass_kernel_spmd(nc, [arrays], core_ids=[0])
    return r.results[0]["out_x"]
```

```python
from collections import namedtuple
from contextlib import ExitStack, contextmanager

import numpy as np

import concourse.bass as bass
from concourse import mybir

F32 = mybir.dt.float32
BF16 = mybir.dt.bfloat16
ALU = mybir.AluOpType
ACT = mybir.ActivationFunctionType
AX_X = mybir.AxisListType.X

P = 128
B, T, C = 16, 256, 128
NT = T // P
TC, CC = 64, 64
H = 16
SLOT = 32
HG = P // SLOT
G = H // HG
PAIRS = H // 2
EPS = 1e-5
MASKED = -1e30
ROUND = 1.5 * 2.0 ** 23


class Store:
    pass


def record(**fields):
    return namedtuple("record", fields)(**fields)


def per_batch(eng, prologue, body, epilogue=None):
    prologue()
    body(0, 0)
    with eng.Fori(0, (B - 4) // 2) as pair:
        body(2 * pair + 1, 1)
        body(2 * pair + 2, 0)
    for n in range(B - 3, B):
        body(n, n % 2)
    if epilogue:
        epilogue()


def has(n, ahead):
    return not isinstance(n, int) or 0 <= n + ahead < B


def wait(eng, sem, value):
    if not isinstance(value, int) or value > 0:
        eng.wait_ge(sem, value)


def wait_apart(eng, sem, value):
    eng.wait_ge(sem, value)
    eng.nop(nofuse=True)


def bank_uses(front, middle, tail):
    def before(step, m, k):
        if step == "tail":
            done = m + 1 if isinstance(m, int) and m == B - 1 else m + 2
            return (front + middle) * done + tail * m + k
        ahead = front if step == "middle" else 0
        if isinstance(m, int) and m == 0:
            return ahead + k
        return (front + middle) * m + tail * (m - 1) + ahead + k
    return before


def bank_order(events):
    front = sum(a == 1 for _, a in events)
    own = sum(a == 0 for _, a in events)

    def before(name, element):
        i, ahead = next((i, a) for i, (e, a) in enumerate(events) if e == name)
        body = element - ahead
        same = sum(has(body, a) for _, a in events[:i]) if not isinstance(body, int) or 0 <= body < B else \
            sum(a == ahead for _, a in events[:i])
        if isinstance(body, int) and body <= 0:
            return front * (body + 1) + same
        done = 2 * front + own + len(events) * (body - 1) + same
        return done - front if isinstance(body, int) and body == B else done
    return before


def tokens(array, n):
    return array[:, bass.ds(NT * n, NT), :] if not isinstance(n, int) else array[:, NT * n:NT * n + NT, :]


def tile_of(array, n, t):
    at = NT * n + t
    return array[:, bass.ds(at, 1), :] if not isinstance(at, int) else array[:, at:at + 1, :]


@contextmanager
def stage_semaphores(nc, prefix, names):
    sems = {s: nc.alloc_semaphore(f"{prefix}_{s}") for s in names.split()}
    yield record(**sems)
    nc.clear_and_free_semaphores(list(sems.values()))
    nc.all_engine_barrier()


def sem_space(nc, ctx, prefix, names):
    return ctx.enter_context(stage_semaphores(nc, prefix, names))



LN_SEMS = " ".join(f"{s}{k}" for k in range(3) for s in ("stats", "mean", "veps", "rstd", "norm", "gain", "shift"))


def ln_sems(s, k):
    return [(s.stats0, s.mean0, s.rstd0, s.norm0), (s.stats1, s.mean1, s.rstd1, s.norm1),
            (s.stats2, s.mean2, s.rstd2, s.norm2)][k]


def ln_pool(pool, s, buf, k, n):
    _, mean, rstd, _ = ln_sems(s, k)
    veps = (s.veps0, s.veps1, s.veps2)[k]
    wait_apart(pool, mean, NT * (n + 1))
    pool.tensor_scalar(buf.veps[k][:, :], buf.mv[k][:, :, 1], EPS, None, ALU.add).then_inc(veps, 1)
    pool.wait_ge(veps, n + 1)
    pool.tensor_tensor(out=buf.rstd[k][:, :], in0=buf.veps[k][:, :], in1=buf.minus_half[:, :],
                       op=ALU.pow).then_inc(rstd, 1)


def ln_chain(s, g, cfg, n, p):
    src = [tile_of(cfg.source, n, t)[:, 0, :] for t in range(NT)]
    out = []
    for k, (gain, shift, keep) in enumerate(cfg.norms):
        last = k == len(cfg.norms) - 1
        dst = ([g.xn[p][:, t, :] for t in range(NT)] if last or keep is None
               else [tile_of(keep, n, t)[:, 0, :] for t in range(NT)])
        out.append((src, dst, gain, shift))
        src = dst
    return out


def ln_steps(dve, s, g, cfg, n, p):
    steps = []
    for k, (src, dst, gain, shift) in enumerate(ln_chain(s, g, cfg, n, p)):
        stats, mean, rstd, norm = ln_sems(s, k)
        gs, ss = [(s.gain0, s.shift0), (s.gain1, s.shift1), (s.gain2, s.shift2)][k]

        def gather(k=k, src=src, stats=stats, mean=mean):
            for t in range(NT):
                dve.bn_stats(g.stats[k][:, t, :], src[t]).then_inc(stats, 1)
            wait_apart(dve, stats, NT * (n + 1))
            for t in range(NT):
                dve.bn_aggr(g.mv[k][:, t, :], g.stats[k][:, t, :]).then_inc(mean, 1)

        def apply(k=k, src=src, dst=dst, mean=mean, rstd=rstd, norm=norm):
            dve.wait_ge(mean, NT * (n + 1))
            dve.wait_ge(rstd, n + 1)
            for t in range(NT):
                dve.tensor_scalar(dst[t], src[t], g.mv[k][:, t, 0:1], g.rstd[k][:, t:t + 1],
                                  ALU.subtract, ALU.mult).then_inc(norm, 1)
            wait_apart(dve, norm, NT * (n + 1))

        def centre(k=k, src=src, dst=dst, gain=gain, mean=mean, gs=gs):
            dve.wait_ge(mean, NT * (n + 1))
            for t in range(NT):
                dve.scalar_tensor_tensor(out=dst[t], in0=src[t], scalar=g.mv[k][:, t, 0:1], in1=gain,
                                         op0=ALU.subtract, op1=ALU.mult).then_inc(gs, 1)

        def scale(k=k, dst=dst, shift=shift, rstd=rstd, gs=gs, ss=ss):
            dve.wait_ge(rstd, n + 1)
            dve.wait_ge(gs, NT * (n + 1))
            for t in range(NT):
                dve.scalar_tensor_tensor(out=dst[t], in0=dst[t], scalar=g.rstd[k][:, t:t + 1], in1=shift,
                                         op0=ALU.mult, op1=ALU.add).then_inc(ss, 1)
            wait_apart(dve, ss, NT * (n + 1))

        steps += [gather] + ([centre, scale] if gain is not None else [apply])
    return steps


def front_vector(dve, s, g, cfg, n, p):
    for step in ln_steps(dve, s, g, cfg, n, p):
        step()


def spread_over(steps, slots):
    return {slot: [step for i, step in enumerate(steps) if slots[i * len(slots) // len(steps)] == slot]
            for slot in slots}


def front_pool(pool, s, g, cfg, n):
    for k in range(len(cfg.norms)):
        ln_pool(pool, s, g, k, n)


def wait_normed(eng, s, cfg, n):
    k = len(cfg.norms) - 1
    if cfg.norms[k][0] is not None:
        eng.wait_ge((s.shift0, s.shift1, s.shift2)[k], NT * (n + 1))
    else:
        eng.wait_ge(ln_sems(s, k)[3], NT * (n + 1))



def self_attention(nc, g, name, cfg):
    D = cfg.D
    a_events = ["x", "q", "k"] + ["v"] * cfg.wide_v + ["shift"]
    fa = bank_order([(e, 1) for e in a_events])
    fb = bank_order([("q", 1), ("k", 1), ("v", 1), ("out", -1)])
    pieces = [(0, j, 0, 4, P) for j in range(HG)] if cfg.causal else []
    pieces += [(qt, j, i, 2, T) for qt in range(1 if cfg.causal else 0, 2) for j in range(HG) for i in (0, 2)]
    NPC = len(pieces)
    LAG = 2
    NB = 4
    AT = dict(x=0, q=1, k=2, v=4, out=10, final=11, shift=14)
    PIECES_AT = [4, 5, 6, 8, 9, 10, 12, 13]
    NORMS_AT = [0, 2, 3, 7, 11, 14, 15]
    NORMALISE_AT = {(HG * gr + HG + LAG + 1) % H: gr for gr in range(G)}
    piece_at = {h: [i for i in range(NPC) if PIECES_AT[i * len(PIECES_AT) // NPC] == h] for h in range(H)}
    SW = 384 if cfg.causal else 512
    K1 = 256
    K1Q = P if cfg.causal else 0
    with ExitStack() as ctx:
        s = sem_space(nc, ctx, name, LN_SEMS + " a_full a_free b_full b_free max_full max_free "
                      "negmax_ready scores_ready exp_done masked pv_done recip_done "
                      "heads_normed ones_ready bias_added summed")
        qT = [g.qT[p][:, :].rearrange("p (g i q) -> p g i q", g=G, i=2) for p in range(2)]
        kT = [g.kT[p][:, 0:G * T].rearrange("p (g q) -> p g q", g=G) for p in range(2)]
        qh = [g.qh[p][:, :].rearrange("p (g i q) -> p g i q", g=G, i=2) for p in range(2)]
        kh = [g.kh[p][:, 0:G * T].rearrange("p (g q) -> p g q", g=G) for p in range(2)]
        V = [g.V[p][:, 0:NT * H * SLOT].rearrange("p (t h d) -> p t h d", t=NT, h=H) for p in range(2)]
        yT = g.yT if cfg.kv_gain is not None else g.xT
        oT = [g.oT[:, p * G * T:(p + 1) * G * T].rearrange("p (n q) -> p n q", n=G) for p in range(2)]
        bias_masked = g.bias_masked
        FA, FB, MX, SC, O = g.bank[0], g.bank[1], g.bank[2:4], g.bank[4:6], g.bank[6:8]
        block = ctx.enter_context(nc.Block())
        load_later(block, cfg)

        def two_groups(bank):
            return bank[:, 0:512].rearrange("p (g q) -> p g q", g=2)

        @block.vector
        def _(dve):
            for p in range(2):
                last = dve.memset(V[p][:, :, :, :], 0.0)
            if cfg.bq is not None:
                for i in range(2):
                    last = dve.tensor_scalar(bias_masked[:, i, :], cfg.bq, g.slot_mask[:, i:i + 1], None, ALU.mult)
            last.then_inc(s.ones_ready, 1)
            dve.wait_ge(s.ones_ready, 1)

            def project(m, p, what):
                bias = cfg.bq if what == "q" else cfg.bk
                dve.wait_ge(s.b_full, fb(what, m) + 1)
                src = two_groups(FB)
                for out in (() if what == "q" else (kh[p], kT[p])):
                    if bias is None:
                        last = dve.tensor_copy(out[:, 0:2, :], src)
                    else:
                        last = dve.tensor_tensor(out=out[:, 0:2, :], in0=src,
                                                 in1=bias[:, 0:2].unsqueeze(2).to_broadcast([P, 2, T]), op=ALU.add)
                if what == "q":
                    for i in range(2):
                        mask = g.slot_mask[:, i:i + 1]
                        if bias is None:
                            last = dve.tensor_scalar(qT[p][:, 0:2, i, :], src, mask, None, ALU.mult)
                        else:
                            for gr in range(2):
                                last = dve.tensor_scalar(qT[p][:, gr, i, :], src[:, gr, :], bias[:, gr:gr + 1], mask,
                                                         ALU.add, ALU.mult)
                last.then_inc(s.b_free, 1)
                if what == "q":
                    dve.wait_ge(s.b_free, fb("q", m) + 1)
                    dve.tensor_copy(qh[p][:, 0:2, :, :], qT[p][:, 0:2, :, :])

            def values(m, p):
                dve.wait_ge(s.b_full, fb("v", m) + 1)
                for t in range(1 if cfg.wide_v else NT):
                    src = FB[:, t * H * D:(t + 1) * H * D].rearrange("p (h d) -> p h d", h=H)
                    if cfg.bv is None:
                        last = dve.tensor_copy(V[p][:, t, :, 0:D], src)
                    else:
                        last = dve.tensor_tensor(out=V[p][:, t, :, 0:D], in0=src,
                                                 in1=cfg.bv.rearrange("p (h d) -> p h d", h=H), op=ALU.add)
                last.then_inc(s.b_free, 1)

            def piece(m, i):
                qt, j, g0, nh, keys = pieces[i]
                dve.wait_ge(s.max_full, NPC * m + i + 1)
                dve.tensor_reduce(g.negmax[:, qt, :].rearrange("p (g j) -> p g j", g=G)[:, g0:g0 + nh, j],
                                  MX[i % 2][:, 0:512].rearrange("p (h k) -> p h k", h=nh),
                                  AX_X, ALU.max, negate=True).then_inc(s.max_free, 1)

            def spread(m):
                dve.wait_ge(s.max_free, NPC * (m + 1))
                dve.tensor_copy(g.negmax4[:, :, :, 0:H],
                                g.negmax[:, :, :].unsqueeze(2).to_broadcast([P, NT, 4, H])
                                ).then_inc(s.negmax_ready, 1)

            def normalise(n, gr, p):
                dve.wait_ge(s.pv_done, H * n + HG * (gr + 1))
                wait(dve, s.heads_normed, G * n + gr)
                dve.reciprocal(g.rec[:, :], O[gr % 2][:, T:2 * T]).then_inc(s.recip_done, 1)
                dve.wait_ge(s.recip_done, G * n + gr + 1)
                dve.tensor_tensor(out=oT[p][:, gr, :], in0=O[gr % 2][:, 0:T], in1=g.rec[:, :], op=ALU.mult
                                  ).then_inc(s.heads_normed, 1)

            def final(n, p):
                dve.wait_ge(s.b_full, fb("out", n) + 1)
                dve.wait_ge(s.bias_added, n + 1)
                dve.tensor_tensor(out=tokens(cfg.target, n), in0=FB[:, 0:T].rearrange("p (t c) -> p t c", t=NT),
                                  in1=g.resb[p][:, :, :], op=ALU.add).then_inc(s.b_free, 1)

            def prologue():
                front_vector(dve, s, g, cfg, 0, 0)
                front_vector(dve, s, g, cfg, 1, 1)
                project(0, 0, "q")
                project(0, 0, "k")
                values(0, 0)
                for i in range(NPC):
                    piece(0, i)
                spread(0)

            def body(n, p):
                ln = spread_over(ln_steps(dve, s, g, cfg, n + 2, p), NORMS_AT) if has(n, 2) else {}
                for h in range(H):
                    if h == AT["shift"] and has(n, 1):
                        spread(n + 1)
                    if has(n, 1):
                        if h == AT["q"]:
                            project(n + 1, 1 - p, "q")
                        if h == AT["k"]:
                            project(n + 1, 1 - p, "k")
                        if h == AT["v"]:
                            values(n + 1, 1 - p)
                        for i in piece_at[h]:
                            piece(n + 1, i)
                    if h == AT["final"] and has(n, -1):
                        final(n - 1, 1 - p)
                    gr = NORMALISE_AT.get(h)
                    if gr is not None and gr < G - 1:
                        normalise(n, gr, p)
                    elif gr is not None and has(n, -1):
                        normalise(n - 1, gr, 1 - p)
                    for step in ln.get(h, ()):
                        step()

            def epilogue():
                normalise(B - 1, G - 1, 1)
                final(B - 1, 1)

            per_batch(dve, prologue, body, epilogue)

        @block.gpsimd
        def _(pool):
            passes = []
            for gain, _shift, _keep in cfg.norms:
                passes.append(sum(2 if c[0] is None else 3 for c in cfg.norms[:len(passes)]))
            steps = sum(2 if c[0] is None else 3 for c in cfg.norms)
            norms_at = spread_over(list(range(steps)), NORMS_AT)
            norms_at = {h: [passes.index(i) for i in at if i in passes] for h, at in norms_at.items()}

            def mask(n, h):
                wait_apart(pool, s.exp_done, H * n + h + 1)
                if cfg.causal:
                    diag = g.prob[h % NB][:, 0:512].rearrange("p (b q) -> p b q", b=2)[:, :, 0:P]
                    pool.affine_select(out=diag, in_=diag, compare_op=ALU.is_ge, fill=0.0, base=0,
                                       pattern=[[0, 2], [1, P]], channel_multiplier=-1).then_inc(s.masked, 1)
                else:
                    for t in range(NT):
                        last = pool.affine_select(out=g.probm[h % NB][:, t, :],
                                                  in_=g.prob[h % NB][:, t * (K1 + P):t * (K1 + P) + P],
                                                  compare_op=ALU.is_gt, fill=0.0, base=0,
                                                  pattern=[[-1, P]], channel_multiplier=1)
                    last.then_inc(s.masked, 1)

            def key_sum(n, h):
                a, b = g.prob[h % NB], g.probsum[h % NB]
                if cfg.causal:
                    pool.wait_ge(s.masked, H * n + h + 1)
                    pool.tensor_tensor(out=b[:, P:T], in0=a[:, P:T], in1=a[:, K1:SW], op=ALU.add).then_inc(s.summed, 1)
                else:
                    pool.tensor_tensor(out=b[:, :], in0=a[:, 0:T], in1=a[:, K1:SW], op=ALU.add).then_inc(s.summed, 1)

            def body(n, p):
                for h in range(H):
                    mask(n, h)
                    key_sum(n, h)
                    if h == 1:
                        pool.tensor_tensor(out=g.resb[p][:, :, :], in0=tokens(cfg.residual, n),
                                           in1=cfg.bias.unsqueeze(1).to_broadcast([P, NT, C]),
                                           op=ALU.add).then_inc(s.bias_added, 1)
                    if has(n, 2):
                        for k in norms_at.get(h, ()):
                            ln_pool(pool, s, g, k, n + 2)

            def prologue():
                front_pool(pool, s, g, cfg, 0)
                front_pool(pool, s, g, cfg, 1)

            per_batch(pool, prologue, body)

        @block.scalar
        def _(act):
            def transposed(m, p):
                act.wait_ge(s.a_full, fa("x", m) + 1)
                if cfg.q_gain is None:
                    act.activation(g.xT[p][:, :], FA[:, 0:T], ACT.Copy).then_inc(s.a_free, 1)
                else:
                    act.activation(g.yT[p][:, :], FA[:, 0:T], ACT.Identity, scale=cfg.kv_gain, bias=cfg.kv_shift)
                    act.activation(g.xT[p][:, :], FA[:, 0:T], ACT.Identity, scale=cfg.q_gain,
                                   bias=cfg.q_shift).then_inc(s.a_free, 1)

            def project(m, p, what):
                bias = cfg.bq if what == "q" else cfg.bk
                act.wait_ge(s.a_full, fa(what, m) + 1)
                for out in (() if what == "q" else (kh[p], kT[p])):
                    if bias is None:
                        last = act.activation(out[:, 2:4, :], two_groups(FA), ACT.Copy)
                    else:
                        act.activation(out[:, 2, :], FA[:, 0:T], ACT.Identity, bias=bias[:, 2:3])
                        last = act.activation(out[:, 3, :], FA[:, T:2 * T], ACT.Identity, bias=bias[:, 3:4])
                if what == "q":
                    for i in range(2):
                        mask = g.slot_mask[:, i:i + 1]
                        if bias is None:
                            last = act.activation(qT[p][:, 2:4, i, :], two_groups(FA), ACT.Identity, scale=mask)
                        else:
                            for gr in (2, 3):
                                last = act.activation(qT[p][:, gr, i, :], FA[:, (gr - 2) * T:(gr - 1) * T], ACT.Identity,
                                                      scale=mask, bias=bias_masked[:, i, gr:gr + 1])
                last.then_inc(s.a_free, 1)
                if what == "q":
                    act.wait_ge(s.a_free, fa("q", m) + 1)
                    act.activation(qh[p][:, 2:4, :, :], qT[p][:, 2:4, :, :], ACT.Copy)

            def values(m, p):
                act.wait_ge(s.a_full, fa("v", m) + 1)
                act.activation(V[p][:, 1, :, 0:D], FA[:, 0:512].rearrange("p (h d) -> p h d", h=H),
                               ACT.Copy).then_inc(s.a_free, 1)

            def shift(m, p):
                act.wait_ge(s.a_full, fa("shift", m) + 1)
                act.activation(g.negmaxT[p][:, :], FA[:, 0:P].bitcast(BF16), ACT.Copy).then_inc(s.a_free, 1)

            def exponent(n, h):
                act.wait_ge(s.scores_ready, H * n + h + 1)
                wait(act, s.pv_done, H * n + h - (NB - 1))
                act.activation(g.prob[h % NB][:, 0:SW], SC[h % 2][:, 0:SW], ACT.Exp,
                               scale=cfg.scale).then_inc(s.exp_done, 1)

            def prologue():
                act.wait_ge(s.ones_ready, 1)
                transposed(0, 0)
                project(0, 0, "q")
                project(0, 0, "k")
                if cfg.wide_v:
                    values(0, 0)
                shift(0, 0)

            def body(n, p):
                for h in range(H):
                    exponent(n, h)
                    if has(n, 1):
                        if h == AT["x"]:
                            transposed(n + 1, 1 - p)
                        if h == AT["q"]:
                            project(n + 1, 1 - p, "q")
                        if h == AT["k"]:
                            project(n + 1, 1 - p, "k")
                        if h == AT["v"] and cfg.wide_v:
                            values(n + 1, 1 - p)
                        if h == AT["shift"]:
                            shift(n + 1, 1 - p)

            per_batch(act, prologue, body)

        @block.tensor
        def _(pe):
            cfg.loaded(pe)
            pe.wait_ge(s.ones_ready, 1)

            def transposed(m, p):
                wait_normed(pe, s, cfg, m)
                wait(pe, s.a_free, fa("x", m))
                for t in range(NT):
                    last = pe.transpose(FA[:, t * P:(t + 1) * P], g.xn[p][:, t, :], g.ident[:, :])
                last.then_inc(s.a_full, 1)

            def project(m, p, what, bank):
                w, x = (cfg.wq, g.xT[p]) if what == "q" else (cfg.wk, yT[p])
                if what == "q" and bank == "b":
                    pe.wait_ge(s.a_free, fa("x", m) + 1)
                if bank == "b":
                    wait(pe, s.b_free, fb(what, m))
                else:
                    wait(pe, s.a_free, fa(what, m))
                dst, full, g0 = (FB, s.b_full, 0) if bank == "b" else (FA, s.a_full, 2)
                for k in range(2):
                    last = pe.matmul(dst[:, k * T:(k + 1) * T], w[:, (g0 + k) * P:(g0 + k + 1) * P], x[:, :],
                                     start=True, stop=True)
                last.then_inc(full, 1)

            def values(m, p):
                wait(pe, s.b_free, fb("v", m))
                if cfg.wide_v:
                    pe.matmul(FB[:, 0:512], yT[p][:, 0:P], cfg.wv[:, :], start=True, stop=True).then_inc(s.b_full, 1)
                    wait(pe, s.a_free, fa("v", m))
                    pe.matmul(FA[:, 0:512], yT[p][:, P:2 * P], cfg.wv[:, :], start=True, stop=True
                              ).then_inc(s.a_full, 1)
                else:
                    for t in range(NT):
                        last = pe.matmul(FB[:, t * P:(t + 1) * P], yT[p][:, t * P:(t + 1) * P], cfg.wv[:, :],
                                         start=True, stop=True)
                    last.then_inc(s.b_full, 1)

            def piece(m, i, p):
                qt, j, g0, nh, keys = pieces[i]
                if i == 0:
                    pe.wait_ge(s.b_free, fb("k", m) + 1)
                    pe.wait_ge(s.a_free, fa("k", m) + 1)
                wait(pe, s.max_free, NPC * m + i - 1)
                bank = MX[i % 2]
                if cfg.causal:
                    out = bank[:, 0:512].rearrange("p (h k) -> p h k", h=nh)[:, :, keys - P:keys]
                    pe.matmul(out, g.identh[:, :], g.causal[:, :].unsqueeze(1).to_broadcast([P, nh, P]),
                              start=True, stop=False, skip_group_check=True)
                rows = slice(2 * SLOT * (j // 2), 2 * SLOT * (j // 2 + 1))
                for k in range(nh):
                    last = pe.matmul(bank[:, k * keys:(k + 1) * keys], qh[p][rows, g0 + k, j % 2, qt * P:(qt + 1) * P],
                                     kh[p][rows, g0 + k, 0:keys], start=not cfg.causal, stop=True,
                                     skip_group_check=True)
                last.then_inc(s.max_full, 1)

            def shift(m):
                pe.wait_ge(s.negmax_ready, m + 1)
                wait(pe, s.a_free, fa("shift", m))
                for t in range(NT):
                    last = pe.transpose(FA[:, 0:P].bitcast(BF16)[:, t * P:(t + 1) * P],
                                        g.negmax4[:, t, :, :].rearrange("p r c -> p (r c)"), g.identh[:, :])
                last.then_inc(s.a_full, 1)

            def scores(n, h, p):
                if h == 0:
                    pe.wait_ge(s.a_free, fa("shift", n) + 1)
                    pe.wait_ge(s.b_free, fb("v", n) + 1)
                wait(pe, s.exp_done, H * n + h - 1)
                rows, odd, gr = slice(2 * SLOT * (h % HG // 2), 2 * SLOT * (h % HG // 2 + 1)), h % 2, h // HG
                bank = SC[h % 2]
                pe.matmul(bank[:, 0:T], g.sel_head[:, h, :], g.negmaxT[p][:, :],
                          start=True, stop=False, skip_group_check=True)
                pe.matmul(bank[:, K1:SW], g.sel_head[:, h, :], g.negmaxT[p][:, K1Q:T],
                          start=False, stop=False, skip_group_check=True)
                pe.matmul(bank[:, 0:T], kT[p][rows, gr, 0:P], qT[p][rows, gr, odd, :],
                          start=False, stop=False, skip_group_check=True)
                pe.matmul(bank[:, K1:SW], kT[p][rows, gr, P:T], qT[p][rows, gr, odd, K1Q:T],
                          start=False, stop=True, skip_group_check=True).then_inc(s.scores_ready, 1)

            def weigh(n, h, p):
                pe.wait_ge(s.masked, H * n + h + 1)
                pe.wait_ge(s.summed, H * n + h + 1)
                if h % HG == 0:
                    wait(pe, s.heads_normed, G * n + h // HG - 1)
                r, bank, a = SLOT * (h % HG), O[(h // HG) % 2], g.prob[h % NB]
                v0, v1, ones = V[p][:, 0, h, :], V[p][:, 1, h, :], g.ones[:, 0:SLOT]

                def product(columns, lhs, rhs, start=False, stop=False):
                    return pe.matmul(bank[r:r + SLOT, columns], lhs, rhs, start=start, stop=stop,
                                     skip_group_check=True)

                if cfg.causal:
                    product(slice(0, T), v0, a[:, 0:T], start=True)
                    product(slice(P, T), v1, a[:, K1:SW])
                    product(slice(T, T + P), ones, a[:, 0:P])
                    last = product(slice(T + P, 2 * T), ones, g.probsum[h % NB][:, P:T], stop=True)
                else:
                    product(slice(0, P), v0, g.probm[h % NB][:, 0, :], start=True)
                    product(slice(0, P), v1, a[:, K1:K1 + P])
                    product(slice(P, T), v1, g.probm[h % NB][:, 1, :])
                    last = product(slice(T, 2 * T), ones, g.probsum[h % NB][:, :], stop=True)
                last.then_inc(s.pv_done, 1)

            def out(n, p):
                pe.wait_ge(s.heads_normed, G * (n + 1))
                wait(pe, s.b_free, fb("out", n))
                for t in range(NT):
                    for k in range(G):
                        last = pe.matmul(FB[:, t * P:(t + 1) * P], oT[p][:, k, t * P:(t + 1) * P], cfg.wo[:, k, :],
                                         start=(k == 0), stop=(k == G - 1))
                last.then_inc(s.b_full, 1)

            def prologue():
                transposed(0, 0)
                for what in "qk":
                    project(0, 0, what, "b")
                    project(0, 0, what, "a")
                values(0, 0)
                for i in range(NPC):
                    piece(0, i, 0)
                shift(0)

            def body(n, p):
                for h in range(H):
                    scores(n, h, p)
                    if h == AT["out"] and has(n, -1):
                        out(n - 1, 1 - p)
                    if has(n, 1):
                        if h == AT["x"]:
                            transposed(n + 1, 1 - p)
                        for what in "qk":
                            if h == AT[what]:
                                project(n + 1, 1 - p, what, "b")
                                project(n + 1, 1 - p, what, "a")
                        if h == AT["v"]:
                            values(n + 1, 1 - p)
                        for i in piece_at[h]:
                            piece(n + 1, i, 1 - p)
                        if h == AT["shift"]:
                            shift(n + 1)
                    if h >= LAG:
                        weigh(n, h - LAG, p)
                    elif has(n, -1):
                        weigh(n - 1, h - LAG + H, 1 - p)

            def epilogue():
                for h in range(H - LAG, H):
                    weigh(B - 1, h, 1)
                out(B - 1, 1)

            per_batch(pe, prologue, body, epilogue)



def cross_attention(nc, g, name, cfg):
    D = cfg.D
    NO = H * D // P
    HT = H // NO
    QC = max(1, NO // 2)
    QW = min(NO, 2)
    VC = max(1, H * D // 512)
    VW = H * D // VC
    GROUPS = PAIRS // 2
    PU = max(k for k in (2, 4, 8) if 2 * k * (D + 1) <= 512)
    NU = PAIRS // PU
    T_AT = {4: [(2, 0), (3, 0), (0, -1), (0, -1)], 2: [(3, 0), (0, -1)], 1: [(1, -1)]}[NU]
    assert NU == QC
    turned = [[(f"turned{u}", "BA"[u % 2 == 0], ahead) for u, (step, ahead) in enumerate(T_AT) if step == i]
              for i in range(GROUPS)]
    queries = [(f"q{c}", "BA"[c % 2], 1) for c in range(QC)]
    values = [(f"v{c}", "BA"[c % 2], 1) for c in range(VC)]
    order = (turned[0] + [("k", "B", 1), ("x", "A", 1)] + turned[1] + queries + [("out", "B", -1)] + turned[2]
             + values + turned[3] + [("shift", "A", 1)])
    fa = bank_order([(name, ahead) for name, bank, ahead in order if bank == "A"])
    fb = bank_order([(name, ahead) for name, bank, ahead in order if bank == "B"])
    with ExitStack() as ctx:
        s = sem_space(nc, ctx, name, LN_SEMS + " a_full a_free b_full b_free low max_full max_free "
                      "negmax_ready scores_ready exp_done pv_done recip_done ctx_ready "
                      "heads_normed ones_ready bias_added")
        qT = [g.qT[p][:, 0:NO * T].rearrange("p (n q) -> p n q", n=NO) for p in range(2)]
        qh = [g.qh[p][:, 0:NO * T].rearrange("p (n q) -> p n q", n=NO) for p in range(2)]
        V = [g.V[p][:, 0:H * (D + 1)].rearrange("p (j i d) -> p j i d", j=PAIRS, i=2) for p in range(2)]
        osb = g.osb[:, 0:NT * H * D].rearrange("p (t f) -> p t f", t=NT)
        oT = g.oT[:, 0:NO * T].rearrange("p (n q) -> p n q", n=NO)
        FA, FB, MX, SC, O = g.bank[0], g.bank[1], g.bank[2:4], g.bank[4:6], g.bank[6:8]
        block = ctx.enter_context(nc.Block())
        load_later(block, cfg)

        def spread_v(eng, p, c, bank):
            j0, nj = c * PAIRS // VC, PAIRS // VC
            for i in range(2):
                rows = slice(i * TC, (i + 1) * TC)
                dst = V[p][rows, j0:j0 + nj, i, 0:D]
                src = bank[rows, 0:VW].rearrange("p (j i d) -> p j i d", j=nj, i=2)[:, :, i, :]
                if eng == "act":
                    last = nc.scalar.activation(dst, src, ACT.Copy)
                elif cfg.bv is None:
                    last = nc.vector.tensor_copy(dst, src)
                else:
                    last = nc.vector.tensor_tensor(
                        out=dst, in0=src, op=ALU.add,
                        in1=cfg.bv[rows, :].rearrange("p (j i d) -> p j i d", j=nj, i=2)[:, :, i, :])
            return last

        @block.vector
        def _(dve):
            for p in range(2):
                dve.memset(g.negmaxT[p][:, :], 0.0)
                dve.memset(V[p][:, :, :, :], 0.0).then_inc(s.ones_ready, 1)
            dve.wait_ge(s.ones_ready, 2)
            for p in range(2):
                dve.memset(V[p][0:TC, :, 0, D:D + 1], 1.0)
                dve.memset(V[p][TC:P, :, 1, D:D + 1], 1.0).then_inc(s.ones_ready, 1)
            dve.wait_ge(s.ones_ready, 4)

            def queries_to(m, p, c):
                dve.wait_ge(s.b_full, fb(f"q{c}", m) + 1)
                src = FB[:, 0:QW * T].rearrange("p (n q) -> p n q", n=QW)
                for out in (qh, qT):
                    dst = out[p][:, QW * c:QW * (c + 1), :]
                    if cfg.bq is None:
                        last = dve.tensor_copy(dst, src)
                    else:
                        last = dve.tensor_scalar(dst, src, cfg.bq, None, ALU.add)
                last.then_inc(s.b_free, 1)

            def keys(m, p):
                dve.wait_ge(s.b_full, fb("k", m) + 1)
                k = FB[:, 0:NO * TC].rearrange("p (n k) -> p n k", n=NO)
                if NO == 1:
                    dst = g.kmask[p][:, :].rearrange("p (h k) -> p h k", h=H)
                    kb = k[:, 0, :].unsqueeze(1).to_broadcast([P, H, TC])
                    hm = cfg.head_mask[:, :].unsqueeze(2).to_broadcast([P, H, TC])
                    if cfg.bk is None:
                        last = dve.tensor_tensor(out=dst, in0=kb, in1=hm, op=ALU.mult)
                    else:
                        last = dve.scalar_tensor_tensor(out=dst, in0=kb, scalar=cfg.bk, in1=hm,
                                                        op0=ALU.add, op1=ALU.mult)
                else:
                    for h in range(HT):
                        dst = g.kmask[p][:, :].rearrange("p (n h k) -> p n h k", n=NO, h=HT)[:, :, h, :]
                        last = dve.tensor_scalar(dst, k, cfg.head_mask[:, h:h + 1], None, ALU.mult)
                last.then_inc(s.b_free, 1)

            def values_to(m, p):
                dve.wait_ge(s.b_full, fb("v0", m) + 1)
                spread_v("dve", p, 0, FB).then_inc(s.b_free, 1)

            def piece(m, i):
                qt, half = divmod(i, 2)
                dve.wait_ge(s.max_full, 4 * m + i + 1)
                dve.tensor_reduce(g.negmax[:, qt, 8 * half:8 * half + 8],
                                  MX[i % 2][:, 0:512].rearrange("p (h k) -> p h k", h=8),
                                  AX_X, ALU.max, negate=True).then_inc(s.max_free, 1)

            def spread(m):
                dve.wait_ge(s.max_free, 4 * (m + 1))
                dve.tensor_copy(g.negmax4[:, :, 0, 0:H], g.negmax[:, :, :]).then_inc(s.negmax_ready, 1)

            def normalise(n, u):
                dve.wait_ge(s.pv_done, GROUPS * n + (u + 1) * PU // 2)
                for qt in range(NT):
                    o = O[qt][:, 0:2 * PU * (D + 1)].rearrange("p (h d) -> p h d", h=2 * PU)
                    dve.reciprocal(g.recip16[:, qt, 0:2 * PU], o[:, :, D]).then_inc(s.recip_done, 1)
                dve.wait_ge(s.recip_done, NT * (NU * n + u + 1))
                for qt in range(NT):
                    o = O[qt][:, 0:2 * PU * (D + 1)].rearrange("p (h d) -> p h d", h=2 * PU)
                    last = dve.tensor_tensor(
                        out=osb[:, qt, u * 2 * PU * D:(u + 1) * 2 * PU * D].rearrange("p (h d) -> p h d", h=2 * PU),
                        in0=o[:, :, 0:D], in1=g.recip16[:, qt, 0:2 * PU].unsqueeze(2).to_broadcast([P, 2 * PU, D]),
                        op=ALU.mult)
                last.then_inc(s.heads_normed, 1)

            def turned_to(n, u):
                dve.wait_ge(s.b_full, fb(f"turned{u}", n) + 1)
                dve.tensor_copy(oT[:, QW * u:QW * (u + 1), :], FB[:, 0:512].rearrange("p (n q) -> p n q", n=2)
                                ).then_inc(s.b_free, 1)

            def final(n, p):
                dve.wait_ge(s.b_full, fb("out", n) + 1)
                if cfg.bias is not None:
                    dve.wait_ge(s.bias_added, n + 1)
                res = tokens(cfg.residual, n) if cfg.bias is None else g.resb[p][:, :, :]
                dve.tensor_tensor(out=tokens(cfg.target, n), in0=FB[:, 0:T].rearrange("p (t c) -> p t c", t=NT),
                                  in1=res, op=ALU.add).then_inc(s.b_free, 1)

            def prologue():
                front_vector(dve, s, g, cfg, 0, 0)
                front_vector(dve, s, g, cfg, 1, 1)
                keys(0, 0)
                for c in range(0, QC, 2):
                    queries_to(0, 0, c)
                for i in range(4):
                    piece(0, i)
                spread(0)
                values_to(0, 0)

            def body(n, p):
                ln = spread_over(ln_steps(dve, s, g, cfg, n + 2, p), list(range(GROUPS))) if has(n, 2) else {}
                for e in range(GROUPS):
                    if e == 0:
                        if (NU - 1) % 2 and has(n, -1):
                            turned_to(n - 1, NU - 1)
                        if has(n, 1):
                            keys(n + 1, 1 - p)
                    if e == 1 and has(n, 1):
                        for c in range(0, QC, 2):
                            queries_to(n + 1, 1 - p, c)
                    if e == 2:
                        if NU == 4:
                            normalise(n, 0)
                        if has(n, 1):
                            piece(n + 1, 0)
                            piece(n + 1, 1)
                        if has(n, -1):
                            final(n - 1, 1 - p)
                        if has(n, 1):
                            piece(n + 1, 2)
                    if e == 3:
                        if NU > 1:
                            normalise(n, NU // 2 - 1)
                        if has(n, 1):
                            piece(n + 1, 3)
                            spread(n + 1)
                            values_to(n + 1, 1 - p)
                        if NU == 4:
                            normalise(n, 2)
                            turned_to(n, 1)
                    for step in ln.get(e, ()):
                        step()
                normalise(n, NU - 1)

            def epilogue():
                if (NU - 1) % 2:
                    turned_to(B - 1, NU - 1)
                final(B - 1, 1)

            per_batch(dve, prologue, body, epilogue)

        @block.gpsimd
        def _(pool):
            def context(m, p):
                pool.tensor_copy(g.ctxb[p][:, :, :], (cfg.ctxT[:, bass.ds(m, 1), :] if not isinstance(m, int)
                                                      else cfg.ctxT[:, m:m + 1, :]).to_broadcast([CC, 2, TC])
                                 ).then_inc(s.ctx_ready, 1)

            def prologue():
                for m in range(2):
                    front_pool(pool, s, g, cfg, m)
                    context(m, m)

            def body(n, p):
                if has(n, 2):
                    ln_pool(pool, s, g, 0, n + 2)
                wait_apart(pool, s.exp_done, GROUPS * n + 1)
                if has(n, 2):
                    context(n + 2, p)
                if cfg.bias is not None:
                    pool.tensor_tensor(out=g.resb[p][:, :, :], in0=tokens(cfg.residual, n),
                                       in1=cfg.bias.unsqueeze(1).to_broadcast([P, NT, C]),
                                       op=ALU.add).then_inc(s.bias_added, 1)
                for k in range(1, len(cfg.norms)):
                    if has(n, 2):
                        ln_pool(pool, s, g, k, n + 2)

            per_batch(pool, prologue, body)

        @block.scalar
        def _(act):
            act.wait_ge(s.ones_ready, 4)

            def transposed(m, p):
                act.wait_ge(s.a_full, fa("x", m) + 1)
                if cfg.q_gain is None:
                    act.activation(g.xT[p][:, :], FA[:, 0:T], ACT.Copy).then_inc(s.a_free, 1)
                else:
                    act.activation(g.xT[p][:, :], FA[:, 0:T], ACT.Identity, scale=cfg.q_gain,
                                   bias=cfg.q_shift).then_inc(s.a_free, 1)

            def queries_to(m, p, c):
                act.wait_ge(s.a_full, fa(f"q{c}", m) + 1)
                for out in (qh, qT):
                    last = act.activation(out[p][:, 2 * c:2 * c + 2, :], FA[:, 0:512].rearrange("p (n q) -> p n q", n=2),
                                          ACT.Copy)
                last.then_inc(s.a_free, 1)

            def low_keys(m, p):
                act.wait_ge(s.b_free, fb("k", m) + 1)
                act.activation(g.kmaskh[p][:, :], g.kmask[p][:, :], ACT.Copy).then_inc(s.low, 1)

            def values_to(m, p):
                act.wait_ge(s.a_full, fa("v1", m) + 1)
                spread_v("act", p, 1, FA).then_inc(s.a_free, 1)

            def shift(m, p):
                act.wait_ge(s.a_full, fa("shift", m) + 1)
                act.activation(g.negmaxT[p][0:H, :], FA[0:H, 0:P].bitcast(BF16), ACT.Copy).then_inc(s.a_free, 1)

            def turned_to(n, u):
                act.wait_ge(s.a_full, fa(f"turned{u}", n) + 1)
                act.activation(oT[:, QW * u:QW * (u + 1), :], FA[:, 0:QW * T].rearrange("p (n q) -> p n q", n=QW),
                               ACT.Copy).then_inc(s.a_free, 1)

            def turn(n, step):
                for u, (at, ahead) in enumerate(T_AT):
                    if at == step and u % 2 == 0 and has(n, ahead):
                        turned_to(n + ahead, u)

            def prologue():
                transposed(0, 0)
                low_keys(0, 0)
                for c in range(1, QC, 2):
                    queries_to(0, 0, c)
                if VC > 1:
                    values_to(0, 0)
                shift(0, 0)

            def body(n, p):
                turn(n, 0)
                for e in range(GROUPS):
                    act.wait_ge(s.scores_ready, GROUPS * n + e + 1)
                    if e >= 3:
                        act.wait_ge(s.pv_done, GROUPS * n + e - 2)
                    act.activation(g.prob[e % 3][:, :], SC[e % 2][:, :], ACT.Exp,
                                   scale=cfg.scale).then_inc(s.exp_done, 1)
                    if e == 0 and has(n, 1):
                        transposed(n + 1, 1 - p)
                    if e == 1:
                        if has(n, 1):
                            low_keys(n + 1, 1 - p)
                        turn(n, 1)
                        for c in range(1, QC, 2):
                            if has(n, 1):
                                queries_to(n + 1, 1 - p, c)
                    if e == 2:
                        turn(n, 2)
                    if e == 3:
                        if VC > 1 and has(n, 1):
                            values_to(n + 1, 1 - p)
                        turn(n, 3)
                        if has(n, 1):
                            shift(n + 1, 1 - p)

            per_batch(act, prologue, body, lambda: (turn(B, 0), turn(B, 1)))

        @block.tensor
        def _(pe):
            cfg.loaded(pe)
            pe.wait_ge(s.ones_ready, 4)

            BANK, FULL = dict(A=FA, B=FB), dict(A=s.a_full, B=s.b_full)

            def use(bank, name, m):
                if bank == "A":
                    wait(pe, s.a_free, fa(name, m))
                else:
                    wait(pe, s.b_free, fb(name, m))

            def transposed(m, p):
                wait_normed(pe, s, cfg, m)
                use("A", "x", m)
                for t in range(NT):
                    last = pe.transpose(FA[:, t * P:(t + 1) * P], g.xn[p][:, t, :], g.ident[:, :])
                last.then_inc(s.a_full, 1)

            def project_q(m, p, c):
                if c == 0:
                    pe.wait_ge(s.a_free, fa("x", m) + 1)
                bank = "BA"[c % 2]
                use(bank, f"q{c}", m)
                for i in range(QW):
                    tile = QW * c + i
                    last = pe.matmul(BANK[bank][:, i * T:(i + 1) * T], cfg.wq[:, tile * P:(tile + 1) * P],
                                     g.xT[p][:, :], start=True, stop=True)
                last.then_inc(FULL[bank], 1)

            def project_k(m, p):
                pe.wait_ge(s.ctx_ready, m + 1)
                use("B", "k", m)
                for i in range(NO):
                    last = pe.matmul(FB[:, i * TC:(i + 1) * TC], cfg.wk[:, i * P:(i + 1) * P], g.ctxb[p][:, 0, :],
                                     start=True, stop=True)
                last.then_inc(s.b_full, 1)

            def project_v(m, p, c):
                bank = "BA"[c % 2]
                use(bank, f"v{c}", m)
                pe.matmul(BANK[bank][:, 0:VW], g.ctxb[p][:, :, :].rearrange("p i k -> p (i k)"),
                          cfg.wv[:, c * VW:(c + 1) * VW], start=True, stop=True).then_inc(FULL[bank], 1)

            def piece(m, i, p):
                qt, half = divmod(i, 2)
                if i == 0:
                    pe.wait_ge(s.low, m + 1)
                    last_b = (QC - 1) // 2 * 2
                    pe.wait_ge(s.b_free, fb(f"q{last_b}", m) + 1)
                    if QC > 1:
                        pe.wait_ge(s.a_free, fa(f"q{QC - 1}", m) + 1)
                if i >= 2:
                    pe.wait_ge(s.max_free, 4 * m + i - 1)
                tiles = range(NO) if NO == 1 else range(half * NO // 2, (half + 1) * NO // 2)
                w = 512 if NO == 1 else HT * TC
                for k, n in enumerate(tiles):
                    last = pe.matmul(MX[i % 2][:, k * w:(k + 1) * w], qh[p][:, n, qt * P:(qt + 1) * P],
                                     g.kmaskh[p][:, half * 512 + k * w:half * 512 + (k + 1) * w],
                                     start=True, stop=True, skip_group_check=True)
                last.then_inc(s.max_full, 1)

            def shift(m):
                pe.wait_ge(s.negmax_ready, m + 1)
                use("A", "shift", m)
                for t in range(NT):
                    last = pe.transpose(FA[0:H, 0:P].bitcast(BF16)[:, t * P:(t + 1) * P],
                                        g.negmax4[:, t, 0, 0:H], g.identh[:, :])
                last.then_inc(s.a_full, 1)

            def scores(n, e, p):
                if e == 0:
                    pe.wait_ge(s.a_free, fa("shift", n) + 1)
                    pe.wait_ge(s.b_free, fb("v0", n) + 1)
                if e >= 2:
                    pe.wait_ge(s.exp_done, GROUPS * n + e - 1)
                for i in range(2):
                    j = 2 * e + i
                    out = SC[e % 2][:, i * T:(i + 1) * T]
                    pe.matmul(out, g.sel_pair[:, j, :], g.negmaxT[p][:, :], start=True, stop=False)
                    last = pe.matmul(out, g.kmask[p][:, j * P:(j + 1) * P], qT[p][:, j * NO // PAIRS, :],
                                     start=False, stop=True)
                last.then_inc(s.scores_ready, 1)

            def weigh(n, e, p):
                pe.wait_ge(s.exp_done, GROUPS * n + e + 1)
                u = e * 2 // PU
                if e * 2 % PU == 0:
                    wait(pe, s.heads_normed, NU * n + u)
                for i in range(2):
                    j = 2 * e + i
                    w = 2 * (D + 1)
                    for qt in range(NT):
                        last = pe.matmul(O[qt][:, (j % PU) * w:(j % PU + 1) * w],
                                         g.prob[e % 3][:, i * T + qt * P:i * T + (qt + 1) * P],
                                         V[p][:, j, :, :].rearrange("p i d -> p (i d)"), start=True, stop=True)
                last.then_inc(s.pv_done, 1)

            def turn(n, step, units=range(NU)):
                for u in units:
                    at, ahead = T_AT[u]
                    if at == step and has(n, ahead):
                        pe.wait_ge(s.heads_normed, NU * (n + ahead) + u + 1)
                        bank = "BA"[u % 2 == 0]
                        use(bank, f"turned{u}", n + ahead)
                        for i in range(QW):
                            for t in range(NT):
                                k = QW * u + i
                                last = pe.transpose(BANK[bank][:, i * T + t * P:i * T + (t + 1) * P],
                                                    osb[:, t, k * P:(k + 1) * P], g.ident[:, :])
                        last.then_inc(FULL[bank], 1)

            def out(n):
                last_a = (NU - 1) // 2 * 2
                pe.wait_ge(s.a_free, fa(f"turned{last_a}", n) + 1)
                use("B", "out", n)
                for t in range(NT):
                    for k in range(NO):
                        last = pe.matmul(FB[:, t * P:(t + 1) * P], oT[:, k, t * P:(t + 1) * P], cfg.wo[:, k, :],
                                         start=(k == 0), stop=(k == NO - 1))
                last.then_inc(s.b_full, 1)

            def prologue():
                project_k(0, 0)
                transposed(0, 0)
                for c in range(QC):
                    project_q(0, 0, c)
                for i in range(4):
                    piece(0, i, 0)
                for c in range(VC):
                    project_v(0, 0, c)
                shift(0)

            def body(n, p):
                nx = has(n, 1)
                turn(n, 0, range(0, NU, 2))
                scores(n, 0, p)
                turn(n, 0, range(1, NU, 2))
                if nx:
                    first, second = (transposed, project_k) if NO > 4 else (project_k, transposed)
                    first(n + 1, 1 - p)
                    second(n + 1, 1 - p)
                scores(n, 1, p)
                turn(n, 1)
                if nx:
                    for c in range(min(QC, 2)):
                        project_q(n + 1, 1 - p, c)
                weigh(n, 0, p)
                if nx:
                    for c in range(2, QC):
                        project_q(n + 1, 1 - p, c)
                scores(n, 2, p)
                if nx:
                    piece(n + 1, 0, 1 - p)
                    piece(n + 1, 1, 1 - p)
                if has(n, -1):
                    out(n - 1)
                weigh(n, 1, p)
                if nx:
                    piece(n + 1, 2, 1 - p)
                turn(n, 2)
                scores(n, 3, p)
                if nx:
                    piece(n + 1, 3, 1 - p)
                    project_v(n + 1, 1 - p, 0)
                weigh(n, 2, p)
                if nx and VC > 1:
                    project_v(n + 1, 1 - p, 1)
                turn(n, 3)
                if nx:
                    shift(n + 1)
                weigh(n, 3, p)

            def epilogue():
                turn(B, 0)
                turn(B, 1)
                out(B - 1)

            per_batch(pe, prologue, body, epilogue)



def feed_forward(nc, g, name, cfg):
    HT = 4
    extra = len(cfg.residuals) - 1
    with ExitStack() as ctx:
        s = sem_space(nc, ctx, name, LN_SEMS + " xt_full xt_ready hidden_full hidden_ready out_full "
                      "residual_a residual_b target_ready")
        hT = [g.qT[p][:, 0:HT * T].rearrange("p (n q) -> p n q", n=HT) for p in range(2)]
        XT = g.bank[0:2]
        HID = [g.bank[2:4], g.bank[4:6]]
        OUT = g.bank[6:8]
        block = ctx.enter_context(nc.Block())
        load_later(block, cfg)

        @block.vector
        def _(dve):
            def activate(m, p):
                for k in range(HT):
                    if k % 2 == 0:
                        dve.wait_ge(s.hidden_full, 2 * m + k // 2 + 1)
                    last = dve.tensor_scalar(hT[p][:, k, :], HID[p][k // 2][:, (k % 2) * T:(k % 2 + 1) * T],
                                             cfg.b1[:, k:k + 1], 0.0, ALU.add, ALU.max)
                last.then_inc(s.hidden_ready, 1)

            def final(n, p):
                dve.wait_ge(s.out_full, n + 1)
                if extra:
                    dve.wait_ge(s.residual_b, extra * (n + 1))
                else:
                    dve.wait_ge(s.residual_a, n + 1)
                dve.tensor_tensor(out=tokens(cfg.target, n), in0=OUT[p][:, 0:T].rearrange("p (t c) -> p t c", t=NT),
                                  in1=g.resb[p][:, :, :], op=ALU.add).then_inc(s.target_ready, 1)

            def prologue():
                front_vector(dve, s, g, cfg, 0, 0)
                front_vector(dve, s, g, cfg, 1, 1)
                if cfg.relu:
                    activate(0, 0)

            def body(n, p):
                gather, apply = ln_steps(dve, s, g, cfg, n + 2, p) if has(n, 2) else [lambda: None] * 2
                gather()
                if has(n, -1):
                    final(n - 1, 1 - p)
                else:
                    dve.wait_ge(s.xt_full, 1)
                apply()
                if cfg.relu and has(n, 1):
                    activate(n + 1, 1 - p)

            per_batch(dve, prologue, body, lambda: final(B - 1, 1))

        @block.gpsimd
        def _(pool):
            def body(n, p):
                if has(n, 2):
                    ln_pool(pool, s, g, 0, n + 2)
                elif isinstance(n, int):
                    pool.wait_ge(s.target_ready, n - 1)
                res = g.resb[p][:, :, :]
                pool.tensor_tensor(out=res, in0=tokens(cfg.residuals[0], n),
                                   in1=cfg.bias.unsqueeze(1).to_broadcast([P, NT, C]),
                                   op=ALU.add).then_inc(s.residual_a, 1)
                if extra:
                    pool.wait_ge(s.residual_a, n + 1)
                for i, r in enumerate(cfg.residuals[1:]):
                    pool.tensor_tensor(out=res, in0=res, in1=tokens(r, n), op=ALU.add).then_inc(s.residual_b, 1)
                    if i < extra - 1:
                        pool.wait_ge(s.residual_b, extra * n + i + 1)

            per_batch(pool, lambda: (front_pool(pool, s, g, cfg, 0), front_pool(pool, s, g, cfg, 1)), body)

        @block.scalar
        def _(act):
            def transposed(m, p):
                act.wait_ge(s.xt_full, m + 1)
                if cfg.x_gain is None:
                    act.activation(g.xT[p][:, :], XT[p][:, 0:T], ACT.Copy).then_inc(s.xt_ready, 1)
                else:
                    act.activation(g.xT[p][:, :], XT[p][:, 0:T], ACT.Identity, scale=cfg.x_gain,
                                   bias=cfg.x_shift).then_inc(s.xt_ready, 1)

            def activate(m, p):
                for k in range(HT):
                    if k % 2 == 0:
                        act.wait_ge(s.hidden_full, 2 * m + k // 2 + 1)
                    last = act.activation(hT[p][:, k, :], HID[p][k // 2][:, (k % 2) * T:(k % 2 + 1) * T],
                                          ACT.Gelu, bias=cfg.b1[:, k:k + 1])
                last.then_inc(s.hidden_ready, 1)

            def prologue():
                transposed(0, 0)
                if not cfg.relu:
                    activate(0, 0)
                transposed(1, 1)

            def body(n, p):
                if not cfg.relu and has(n, 1):
                    activate(n + 1, 1 - p)
                if has(n, 2):
                    transposed(n + 2, p)

            per_batch(act, prologue, body)

        @block.tensor
        def _(pe):
            cfg.loaded(pe)

            def transposed(m, p):
                wait_normed(pe, s, cfg, m)
                for t in range(NT):
                    last = pe.transpose(XT[p][:, t * P:(t + 1) * P], g.xn[p][:, t, :], g.ident[:, :])
                last.then_inc(s.xt_full, 1)

            def hidden(m, p):
                pe.wait_ge(s.xt_ready, m + 1)
                for k in range(HT):
                    mm = pe.matmul(HID[p][k // 2][:, (k % 2) * T:(k % 2 + 1) * T], cfg.w1[:, k * P:(k + 1) * P],
                                   g.xT[p][:, :], start=True, stop=True)
                    if k % 2:
                        mm.then_inc(s.hidden_full, 1)

            def output(n, p):
                pe.wait_ge(s.hidden_ready, n + 1)
                if isinstance(n, int) and n >= B - 2:
                    pe.wait_ge(s.target_ready, n - 1)
                for t in range(NT):
                    for k in range(HT):
                        last = pe.matmul(OUT[p][:, t * P:(t + 1) * P], hT[p][:, k, t * P:(t + 1) * P],
                                         cfg.w2[:, k, :], start=(k == 0), stop=(k == HT - 1))
                last.then_inc(s.out_full, 1)

            def prologue():
                transposed(0, 0)
                hidden(0, 0)
                transposed(1, 1)

            def body(n, p):
                if has(n, 1):
                    hidden(n + 1, 1 - p)
                output(n, p)
                if has(n, 2):
                    transposed(n + 2, p)

            per_batch(pe, prologue, body)



def route(nc, g, name, cfg):
    E, K, S = cfg.experts, cfg.top, 8 - cfg.top
    N = B * NT
    gb = g.gate
    with ExitStack() as ctx:
        s = sem_space(nc, ctx, name, LN_SEMS + " xt_full xt_ready logits_full logits_ready sentinels "
                      "exped maxed shifted summed rsum probs_ready topped keys_ready replaced weighed "
                      "wsum wguard wrecip combined pbias split_a split_b split_c split_d parts_full parts_ready")
        XT, LG, PT = g.bank[0:2], g.bank[2:4], g.bank[4:8]
        xt_of = lambda m: cfg.xT[:, bass.ds(T * m, T)] if not isinstance(m, int) else cfg.xT[:, T * m:T * m + T]
        block = ctx.enter_context(nc.Block())

        def wide(column):
            return column.unsqueeze(2).to_broadcast([P, N, E])

        @block.vector
        def _(dve):
            dve.memset(gb.probs[:, :, :], -1.0)
            dve.memset(gb.keys[:, :, :], -1.0).then_inc(s.sentinels, 1)

            def gather(m, p):
                for t in range(NT):
                    dve.bn_stats(g.stats[p][:, t, :], tile_of(cfg.source, m, t)[:, 0, :]).then_inc(s.stats0, 1)
                wait_apart(dve, s.stats0, NT * (m + 1))
                for t in range(NT):
                    dve.bn_aggr(g.mv[p][:, t, :], g.stats[p][:, t, :]).then_inc(s.mean0, 1)

            def apply(m, p):
                dve.wait_ge(s.rstd0, m + 1)
                if not isinstance(m, int) or m > 1:
                    dve.wait_ge(s.xt_full, m - 1)
                for t in range(NT):
                    dve.tensor_scalar(g.xn[p][:, t, :], tile_of(cfg.source, m, t)[:, 0, :], g.mv[p][:, t, 0:1],
                                      g.rstd[p][:, t:t + 1], ALU.subtract, ALU.mult).then_inc(s.norm0, 1)

            def prologue():
                gather(0, 0)
                gather(1, 1)
                apply(0, 0)

            def body(n, p):
                if has(n, 1):
                    apply(n + 1, 1 - p)
                if has(n, 2):
                    gather(n + 2, p)

            per_batch(dve, prologue, body)
            e, probs, w, c = gb.e[:, :, 0:E], gb.probs[:, :, 0:E], gb.w[:, :, 0:E], gb.c[:, :, 0:E]
            dve.wait_ge(s.logits_ready, B)
            dve.tensor_reduce(gb.nmax[:, :], e, AX_X, ALU.max, negate=True).then_inc(s.maxed, 1)
            dve.wait_ge(s.maxed, 1)
            dve.tensor_tensor(out=e, in0=e, in1=wide(gb.nmax[:, :]), op=ALU.add).then_inc(s.shifted, 1)
            dve.wait_ge(s.exped, 1)
            dve.tensor_reduce(gb.sum[:, :], e, AX_X, ALU.add).then_inc(s.summed, 1)
            dve.wait_ge(s.summed, 1)
            dve.reciprocal(gb.rsum[:, :], gb.sum[:, :]).then_inc(s.rsum, 1)
            dve.wait_ge(s.sentinels, 1)
            dve.wait_ge(s.rsum, 1)
            dve.tensor_tensor(out=probs, in0=e, in1=wide(gb.rsum[:, :]), op=ALU.mult).then_inc(s.probs_ready, 1)
            dve.wait_ge(s.probs_ready, 1)
            for t in range(N):
                dve.max(gb.top[:, t, :], gb.probs[:, t, 0:E]).then_inc(s.topped, 1)
            dve.wait_ge(s.topped, N)
            dve.tensor_copy(gb.keys[:, :, 0:K], gb.top[:, :, 0:K]).then_inc(s.keys_ready, 1)
            dve.wait_ge(s.keys_ready, 1)
            for t in range(N):
                dve.match_replace(gb.marked[:, t, 0:E + S], gb.keys[:, t, :], gb.probs[:, t, 0:E + S], -2.0
                                  ).then_inc(s.replaced, 1)
            dve.wait_ge(s.replaced, N)
            dve.scalar_tensor_tensor(out=w, in0=gb.marked[:, :, 0:E], scalar=0.0, in1=probs,
                                     op0=ALU.is_lt, op1=ALU.mult).then_inc(s.weighed, 1)
            dve.wait_ge(s.weighed, 1)
            dve.tensor_reduce(gb.wsum[:, :], w, AX_X, ALU.add).then_inc(s.wsum, 1)
            dve.wait_ge(s.wsum, 1)
            total = gb.wsum
            if cfg.guard:
                dve.tensor_scalar(gb.wguard[:, :], gb.wsum[:, :], cfg.guard, None, ALU.add).then_inc(s.wguard, 1)
                dve.wait_ge(s.wguard, 1)
                total = gb.wguard
            dve.reciprocal(gb.wrecip[:, :], total[:, :]).then_inc(s.wrecip, 1)
            dve.wait_ge(s.wrecip, 1)
            dve.tensor_tensor(out=c, in0=w, in1=wide(gb.wrecip[:, :]), op=ALU.mult).then_inc(s.combined, 1)
            dve.wait_ge(s.combined, 1)
            if not cfg.parts:
                dve.tensor_tensor(out=w, in0=c, in1=probs, op=ALU.mult).then_inc(s.pbias, 1)
                dve.wait_ge(s.pbias, 1)
                dve.tensor_reduce(gb.wsum[:, :], w, AX_X, ALU.add)
                return
            part, rest = gb.part, gb.rest
            dve.tensor_copy(part[:, :, 0, :], c).then_inc(s.split_a, 1)
            dve.wait_ge(s.split_a, 1)
            dve.tensor_tensor(out=rest[:, :, :], in0=c, in1=part[:, :, 0, :], op=ALU.subtract).then_inc(s.split_b, 1)
            dve.wait_ge(s.split_b, 1)
            dve.tensor_copy(part[:, :, 1, :], rest[:, :, :]).then_inc(s.split_c, 1)
            dve.wait_ge(s.split_c, 1)
            dve.tensor_tensor(out=part[:, :, 2, :], in0=rest[:, :, :], in1=part[:, :, 1, :], op=ALU.subtract
                              ).then_inc(s.split_d, 1)

        @block.gpsimd
        def _(pool):
            def rstd(m, p):
                wait_apart(pool, s.mean0, NT * (m + 1))
                pool.tensor_scalar(g.veps[p][:, :], g.mv[p][:, :, 1], EPS, None, ALU.add).then_inc(s.veps0, 1)
                pool.wait_ge(s.veps0, m + 1)
                pool.tensor_tensor(out=g.rstd[p][:, :], in0=g.veps[p][:, :], in1=g.minus_half[:, :],
                                   op=ALU.pow).then_inc(s.rstd0, 1)

            per_batch(pool, lambda: (rstd(0, 0), rstd(1, 1)), lambda n, p: has(n, 2) and rstd(n + 2, p))

        @block.scalar
        def _(act):
            def transposed(m, p):
                act.wait_ge(s.xt_full, m + 1)
                act.activation(xt_of(m), XT[p][:, 0:T], ACT.Copy)
                act.activation(g.xT[p][:, :], XT[p][:, 0:T], ACT.Copy).then_inc(s.xt_ready, 1)

            def body(n, p):
                if has(n, 1):
                    transposed(n + 1, 1 - p)
                act.wait_ge(s.logits_full, n + 1)
                act.activation(tokens(gb.e, n)[:, :, 0:E], LG[p][:, 0:NT * E].rearrange("p (t e) -> p t e", t=NT),
                               ACT.Copy).then_inc(s.logits_ready, 1)

            per_batch(act, lambda: transposed(0, 0), body)
            act.wait_ge(s.shifted, 1)
            act.activation(gb.e[:, :, 0:E], gb.e[:, :, 0:E], ACT.Exp).then_inc(s.exped, 1)
            if cfg.parts:
                for i in range(len(PT)):
                    act.wait_ge(s.parts_full, i + 1)
                    act.activation(g.combT[:, i * 1024:(i + 1) * 1024], PT[i][0:3 * E, :].bitcast(BF16), ACT.Copy
                                   ).then_inc(s.parts_ready, 1)

        @block.tensor
        def _(pe):
            cfg.loaded(pe)

            def transposed(m, p):
                pe.wait_ge(s.norm0, NT * (m + 1))
                for t in range(NT):
                    last = pe.transpose(XT[p][:, t * P:(t + 1) * P], g.xn[p][:, t, :], g.ident[:, :])
                last.then_inc(s.xt_full, 1)

            def body(n, p):
                if has(n, 1):
                    transposed(n + 1, 1 - p)
                pe.wait_ge(s.xt_ready, n + 1)
                for t in range(NT):
                    last = pe.matmul(LG[p][:, t * E:(t + 1) * E], g.xT[p][:, t * P:(t + 1) * P], cfg.gate_w[:, :],
                                     start=True, stop=True)
                last.then_inc(s.logits_full, 1)

            per_batch(pe, lambda: transposed(0, 0), body)
            if cfg.parts:
                pe.wait_ge(s.split_d, 1)
                for t in range(N):
                    mm = pe.transpose(PT[t // 8][0:3 * E, :].bitcast(BF16)[:, (t % 8) * P:(t % 8 + 1) * P],
                                      gb.part[:, t, :, :].rearrange("p k e -> p (k e)"), g.identh[:, :])
                    if t % 8 == 7:
                        mm.then_inc(s.parts_full, 1)


def gated_experts(nc, g, name, cfg):
    E, HID = 16, 64
    U = E // 2 + 1
    LAG = 2
    with ExitStack() as ctx:
        s = sem_space(nc, ctx, name, "hidden_full weights_full silu_done gated scaled used target_ready")
        HB, CB, Y = g.bank[0:3], g.bank[3:6], g.bank[6:8]
        block = ctx.enter_context(nc.Block())
        of = lambda array, n: array[:, bass.ds(T * n, T)] if not isinstance(n, int) else array[:, T * n:T * n + T]

        def rows(u):
            return P if u < U - 1 else HID

        @block.vector
        def _(dve):
            def unit(n, u):
                r = rows(u)
                dve.wait_ge(s.silu_done, U * n + u + 1)
                wait(dve, s.used, U * n + u - 2)
                a = g.prob[u % 3][0:r, 0:T]
                dve.tensor_tensor(out=a, in0=g.silu[u % 3][0:r, :], in1=HB[u % 3][0:r, T:2 * T], op=ALU.mult
                                  ).then_inc(s.gated, 1)
                if u < U - 1:
                    dve.wait_ge(s.weights_full, (U - 1) * n + u + 1)
                    dve.wait_ge(s.gated, U * n + u + 1)
                    dve.tensor_tensor(out=a, in0=a, in1=CB[u % 3][:, 0:T], op=ALU.mult).then_inc(s.scaled, 1)

            def final(n, p):
                dve.wait_ge(s.used, U * (n + 1))
                dve.tensor_tensor(out=tokens(cfg.target, n), in0=Y[p][:, 0:T].rearrange("p (t c) -> p t c", t=NT),
                                  in1=tokens(cfg.residual, n), op=ALU.add).then_inc(s.target_ready, 1)

            def body(n, p):
                for u in range(U):
                    unit(n, u)
                    if u == LAG + 1 and has(n, -1):
                        final(n - 1, 1 - p)

            per_batch(dve, lambda: None, body, lambda: final(B - 1, 1))

        @block.scalar
        def _(act):
            def body(n, p):
                for u in range(U):
                    act.wait_ge(s.hidden_full, U * n + u + 1)
                    act.activation(g.silu[u % 3][0:rows(u), :], HB[u % 3][0:rows(u), 0:T], ACT.Silu
                                   ).then_inc(s.silu_done, 1)

            per_batch(act, lambda: None, body)

        @block.tensor
        def _(pe):
            cfg.loaded(pe)

            def hidden(n, u):
                if not isinstance(n, int) or U * n + u > 2:
                    wait_apart(pe, s.gated, U * n + u - 2)
                r = rows(u)
                w1 = cfg.w1[:, u * P:(u + 1) * P] if u < U - 1 else cfg.sw1[:, :]
                w3 = cfg.w3[:, u * P:(u + 1) * P] if u < U - 1 else cfg.sw3[:, :]
                x = of(cfg.xT, n)
                pe.matmul(HB[u % 3][0:r, 0:T], w1, x, start=True, stop=True)
                pe.matmul(HB[u % 3][0:r, T:2 * T], w3, x, start=True, stop=True).then_inc(s.hidden_full, 1)
                if u < U - 1:
                    before = (U - 1) * n + u - (2 if u >= 3 else 1)
                    if not isinstance(n, int) or before > 0:
                        wait_apart(pe, s.scaled, before)
                    pe.matmul(CB[u % 3][:, 0:T], g.sel_expert[:, u, :], of(g.combT, n), start=True, stop=True
                              ).then_inc(s.weights_full, 1)

            def output(n, u, p):
                r = rows(u)
                if u < U - 1:
                    pe.wait_ge(s.scaled, (U - 1) * n + u + 1)
                else:
                    pe.wait_ge(s.gated, U * n + u + 1)
                w2 = cfg.w2[:, u, :] if u < U - 1 else cfg.sw2[:, :]
                for t in range(NT):
                    last = pe.matmul(Y[p][:, t * P:(t + 1) * P], g.prob[u % 3][0:r, t * P:(t + 1) * P], w2,
                                     start=(u == 0 and t == 0), stop=(u == U - 1), skip_group_check=True)
                last.then_inc(s.used, 1)

            def body(n, p):
                for u in range(U):
                    hidden(n, u)
                    if u >= LAG:
                        output(n, u - LAG, p)
                    elif has(n, -1):
                        output(n - 1, u - LAG + U, 1 - p)

            per_batch(pe, lambda: None, body, lambda: [output(B - 1, u, 1) for u in range(U - LAG, U)])



def quantise_steps(dve, q, buf, source, p, n):
    peak_done, guard_done, recip_done, level_done, rounded = q

    def peak():
        dve.tensor_reduce(buf.peak[:, :], source, AX_X, ALU.max, apply_absolute_value=True).then_inc(peak_done, 1)

    def guard():
        dve.wait_ge(peak_done, n + 1)
        dve.tensor_scalar(buf.peakc[:, :], buf.peak[:, :], 1e-5, None, ALU.max).then_inc(guard_done, 1)

    def reciprocal():
        dve.wait_ge(guard_done, n + 1)
        dve.reciprocal(buf.recip[:, :], buf.peakc[:, :]).then_inc(recip_done, 1)

    def level():
        dve.wait_ge(recip_done, n + 1)
        dve.tensor_scalar(buf.scale[:, :], buf.recip[:, :], 127.0, None, ALU.mult)
        dve.tensor_scalar(buf.level[p][:, :], buf.peakc[:, :], 1.0 / 127.0, buf.wlevel, ALU.mult, ALU.mult
                          ).then_inc(level_done, 1)

    def rounding():
        dve.wait_ge(level_done, n + 1)
        for t in range(NT):
            dve.tensor_scalar(source[:, t, :], source[:, t, :], buf.scale[:, t:t + 1], ROUND, ALU.mult, ALU.add
                              ).then_inc(rounded, 1)

    return peak, guard, reciprocal, level, rounding


def quantised_feed_forward(nc, g, name, cfg):
    HT, F = 4, 512
    Q = "peak guard recip level rounded"
    with ExitStack() as ctx:
        s = sem_space(nc, ctx, name, LN_SEMS + " low_a at_full at_ready hidden_full biased geled clipped_a clipped_b "
                      "stats_h mean_h veps_h rstd_h gain_h shift_h low_b bt_full bt_ready out_full "
                      "residual_added target_ready " + " ".join(f"{x}_{k}" for k in "ab" for x in Q.split()))
        qa = (s.peak_a, s.guard_a, s.recip_a, s.level_a, s.rounded_a)
        qb = (s.peak_b, s.guard_b, s.recip_b, s.level_b, s.rounded_b)
        hid = [g.qT[p][:, 0:NT * F].rearrange("p (t f) -> p t f", t=NT) for p in range(2)]
        intsT = [g.qh[p][:, 0:HT * T].rearrange("p (n q) -> p n q", n=HT) for p in range(2)]
        ints_b = g.kh[0][:, 0:NT * F].rearrange("p (t f) -> p t f", t=NT)
        ints_a = g.kh[1][:, 0:NT * C].rearrange("p (t f) -> p t f", t=NT)
        xTh = g.negmaxT[0]
        AT, HB, BT, OUT = g.bank[0], g.bank[1:5], g.bank[5], g.bank[6:8]
        limits = (ROUND + 127.0, ROUND - 128.0, ALU.min, ALU.max)
        block = ctx.enter_context(nc.Block())

        @block.vector
        def _(dve):
            def quantise_x(m, p):
                return quantise_steps(dve, qa, g.quant_a, g.xn[p][:, :, :], p, m)

            def clip_x(m, p):
                dve.wait_ge(s.rounded_a, NT * (m + 1))
                dve.tensor_scalar(g.xn[p][:, :, :], g.xn[p][:, :, :], *limits).then_inc(s.clipped_a, 1)

            def bias(m, p):
                for t in range(NT):
                    dve.wait_ge(s.hidden_full, NT * m + t + 1)
                    last = dve.scalar_tensor_tensor(out=hid[p][:, t, :], in0=HB[2 * p + t][:, :],
                                                    scalar=g.quant_a.level[p][:, t:t + 1], in1=cfg.b1,
                                                    op0=ALU.mult, op1=ALU.add)
                last.then_inc(s.biased, 1)

            def gather_hidden(n, p):
                wait_apart(dve, s.geled, n + 1)
                for t in range(NT):
                    dve.bn_stats(g.stats[2][:, t, :], hid[p][:, t, :]).then_inc(s.stats_h, 1)
                wait_apart(dve, s.stats_h, NT * (n + 1))
                for t in range(NT):
                    dve.bn_aggr(g.mvh[:, t, :], g.stats[2][:, t, :]).then_inc(s.mean_h, 1)

            def normalise_hidden(n, p):
                dve.wait_ge(s.mean_h, NT * (n + 1))
                for t in range(NT):
                    h = hid[p][:, t, :]
                    dve.scalar_tensor_tensor(out=h, in0=h, scalar=g.mvh[:, t, 0:1], in1=cfg.gain2,
                                             op0=ALU.subtract, op1=ALU.mult).then_inc(s.gain_h, 1)
                dve.wait_ge(s.rstd_h, n + 1)
                dve.wait_ge(s.gain_h, NT * (n + 1))
                for t in range(NT):
                    h = hid[p][:, t, :]
                    dve.scalar_tensor_tensor(out=h, in0=h, scalar=g.rstdh[:, t:t + 1], in1=cfg.shift2,
                                             op0=ALU.mult, op1=ALU.add).then_inc(s.shift_h, 1)

            def final(n, p):
                dve.wait_ge(s.out_full, n + 1)
                dve.wait_ge(s.residual_added, n + 1)
                for t in range(NT):
                    last = dve.scalar_tensor_tensor(out=tile_of(cfg.target, n, t)[:, 0, :], in0=OUT[p][:, t * P:(t + 1) * P],
                                                    scalar=g.quant_b.level[p][:, t:t + 1], in1=g.resb[p][:, t, :],
                                                    op0=ALU.mult, op1=ALU.add)
                last.then_inc(s.target_ready, 1)

            def prologue():
                for m in range(2):
                    front_vector(dve, s, g, cfg, m, m)
                    for step in quantise_x(m, m):
                        step()
                    clip_x(m, m)
                bias(0, 0)

            def body(n, p):
                steps = ln_steps(dve, s, g, cfg, n + 2, p) if has(n, 2) else [lambda: None] * 5
                gather_x, apply_x, gather_x2, centre_x, scale_x = steps
                gather_hidden(n, p)
                gather_x()
                normalise_hidden(n, p)
                apply_x()
                gather_x2()
                if has(n, -1):
                    final(n - 1, 1 - p)
                if has(n, 1):
                    bias(n + 1, 1 - p)
                peak_h, guard_h, reciprocal_h, level_h, round_h = quantise_steps(dve, qb, g.quant_b, hid[p], p, n)
                peak_x, guard_x, reciprocal_x, level_x, round_x = (quantise_x(n + 2, p) if has(n, 2)
                                                                   else [lambda: None] * 5)
                dve.wait_ge(s.shift_h, NT * (n + 1))
                for step in (peak_h, centre_x, guard_h, scale_x, reciprocal_h, peak_x, level_h, guard_x, round_h,
                             reciprocal_x, level_x, round_x):
                    step()
                if has(n, 2):
                    clip_x(n + 2, p)

            per_batch(dve, prologue, body, lambda: final(B - 1, 1))

        @block.gpsimd
        def _(pool):
            def body(n, p):
                wait_apart(pool, s.mean_h, NT * (n + 1))
                pool.tensor_scalar(g.veps[2][:, :], g.mvh[:, :, 1], EPS, None, ALU.add).then_inc(s.veps_h, 1)
                pool.wait_ge(s.veps_h, n + 1)
                pool.tensor_tensor(out=g.rstdh[:, :], in0=g.veps[2][:, :], in1=g.minus_half[:, :],
                                   op=ALU.pow).then_inc(s.rstd_h, 1)
                if has(n, 2):
                    front_pool(pool, s, g, cfg, n + 2)
                wait_apart(pool, s.rounded_b, NT * (n + 1))
                pool.tensor_scalar(hid[p], hid[p], *limits).then_inc(s.clipped_b, 1)
                pool.tensor_tensor(out=g.resb[p][:, :, :], in0=tokens(cfg.residual, n),
                                   in1=cfg.bias.unsqueeze(1).to_broadcast([P, NT, C]),
                                   op=ALU.add).then_inc(s.residual_added, 1)

            per_batch(pool, lambda: (front_pool(pool, s, g, cfg, 0), front_pool(pool, s, g, cfg, 1)), body)

        @block.scalar
        def _(act):
            def integers_x(m, p):
                act.wait_ge(s.clipped_a, m + 1)
                act.activation(ints_a, g.xn[p][:, :, :], ACT.Identity, bias=g.minus_round[:, :]).then_inc(s.low_a, 1)

            def transposed_x(m):
                act.wait_ge(s.at_full, m + 1)
                act.activation(xTh[:, :], AT[:, 0:P].bitcast(BF16), ACT.Copy).then_inc(s.at_ready, 1)

            def gelu(m, p):
                act.wait_ge(s.biased, m + 1)
                act.activation(hid[p], hid[p], ACT.Gelu).then_inc(s.geled, 1)

            def prologue():
                for m in range(2):
                    integers_x(m, m)
                    transposed_x(m)
                gelu(0, 0)

            def body(n, p):
                if has(n, 1):
                    gelu(n + 1, 1 - p)
                act.wait_ge(s.clipped_b, n + 1)
                act.activation(ints_b, hid[p], ACT.Identity, bias=g.minus_round[:, :]).then_inc(s.low_b, 1)
                if has(n, 2):
                    integers_x(n + 2, p)
                act.wait_ge(s.bt_full, n + 1)
                act.activation(intsT[p][:, :, :], BT[:, :].bitcast(BF16).rearrange("p (n q) -> p n q", n=HT),
                               ACT.Copy).then_inc(s.bt_ready, 1)
                if has(n, 2):
                    transposed_x(n + 2)

            per_batch(act, prologue, body)

        @block.tensor
        def _(pe):
            def transposed_x(m):
                pe.wait_ge(s.low_a, m + 1)
                for t in range(NT):
                    last = pe.transpose(AT[:, 0:P].bitcast(BF16)[:, t * P:(t + 1) * P], ints_a[:, t, :], g.identh[:, :])
                last.then_inc(s.at_full, 1)

            def hidden(m, p):
                pe.wait_ge(s.at_ready, m + 1)
                for t in range(NT):
                    pe.matmul(HB[2 * p + t][:, :], xTh[:, t * P:(t + 1) * P], cfg.w1[:, :], start=True, stop=True
                              ).then_inc(s.hidden_full, 1)

            def prologue():
                for m in range(2):
                    transposed_x(m)
                    hidden(m, m)

            def body(n, p):
                pe.wait_ge(s.low_b, n + 1)
                for k in range(HT):
                    for t in range(NT):
                        last = pe.transpose(BT[:, :].bitcast(BF16)[:, k * T + t * P:k * T + (t + 1) * P],
                                            ints_b[:, t, k * P:(k + 1) * P], g.identh[:, :])
                last.then_inc(s.bt_full, 1)
                if has(n, 2):
                    transposed_x(n + 2)
                pe.wait_ge(s.bt_ready, n + 1)
                for t in range(NT):
                    for k in range(HT):
                        last = pe.matmul(OUT[p][:, t * P:(t + 1) * P], intsT[p][:, k, t * P:(t + 1) * P],
                                         cfg.w2[:, k, :], start=(k == 0), stop=(k == HT - 1))
                last.then_inc(s.out_full, 1)
                if has(n, 2):
                    hidden(n + 2, p)

            per_batch(pe, prologue, body)



def routed_experts(nc, g, name, cfg, out):
    E = cfg.experts
    gb = g.gate
    with ExitStack() as ctx:
        s = sem_space(nc, ctx, name, "x_ready weights_ready experts_full summed_in stored started")
        EX = [g.bank[0:4], g.bank[4:8]]
        out_v = out.rearrange("b (t p) c -> p (b t) c", p=P)
        block = ctx.enter_context(nc.Block())

        @block.sync
        def _(sp):
            def body(n, p):
                sp.wait_ge(s.summed_in, NT * E * (n + 1))
                dst = out_v[:, bass.ds(NT * n, NT), :] if not isinstance(n, int) else out_v[:, NT * n:NT * n + NT, :]
                sp.dma_start(dst, tokens(cfg.target, n)).then_inc(s.stored, 16)

            per_batch(sp, lambda: None, body)
            sp.wait_ge(s.stored, 16 * B)

        @block.vector
        def _(dve):
            def body(n, p):
                dve.wait_ge(s.weights_ready, n + 1)
                last = dve.tensor_tensor(out=g.resb[p][:, :, :], in0=tokens(cfg.residual, n),
                                         in1=gb.pn[p][:, :].unsqueeze(2).to_broadcast([P, NT, C]), op=ALU.add)
                last.then_inc(s.started, 1)
                dve.wait_ge(s.started, n + 1)
                for e in range(E):
                    for t in range(NT):
                        if e % 4 == 0:
                            dve.wait_ge(s.experts_full, 4 * n + 2 * (e // 4) + t + 1)
                        if e:
                            dve.wait_ge(s.summed_in, NT * (E * n + e - 1) + t + 1)
                        acc = g.resb[p][:, t, :]
                        dst = acc if e < E - 1 else tile_of(cfg.target, n, t)[:, 0, :]
                        dve.scalar_tensor_tensor(out=dst, in0=EX[p][2 * (e // 4) + t][:, (e % 4) * P:(e % 4 + 1) * P],
                                                 scalar=gb.cn[p][:, t, e:e + 1], in1=acc, op0=ALU.mult, op1=ALU.add
                                                 ).then_inc(s.summed_in, 1)

            per_batch(dve, lambda: None, body)

        @block.scalar
        def _(act):
            def fetch(m, p):
                if not isinstance(m, int) or m > 1:
                    act.wait_ge(s.summed_in, NT * E * (m - 1))
                act.activation(g.xT[p][:, :], cfg.xT[:, bass.ds(T * m, T)] if not isinstance(m, int)
                               else cfg.xT[:, T * m:T * m + T], ACT.Copy).then_inc(s.x_ready, 1)
                act.activation(gb.cn[p][:, :, :], tokens(gb.c, m)[:, :, 0:E], ACT.Copy)
                act.activation(gb.pn[p][:, :], gb.wsum[:, bass.ds(NT * m, NT)] if not isinstance(m, int)
                               else gb.wsum[:, NT * m:NT * m + NT], ACT.Copy).then_inc(s.weights_ready, 1)

            per_batch(act, lambda: fetch(0, 0), lambda n, p: has(n, 1) and fetch(n + 1, 1 - p))

        @block.tensor
        def _(pe):
            cfg.loaded(pe)

            def body(n, p):
                pe.wait_ge(s.x_ready, n + 1)
                for k in range(2):
                    for t in range(NT):
                        pe.matmul(EX[p][2 * k + t][:, :], g.xT[p][:, t * P:(t + 1) * P],
                                  cfg.w[:, 4 * k * P:4 * (k + 1) * P], start=True, stop=True
                                  ).then_inc(s.experts_full, 1)

            per_batch(pe, lambda: None, body)



def prepare(nc, g, w, dram):
    with ExitStack() as ctx:
        s = sem_space(nc, ctx, "prepare", "zeroed built")
        block = ctx.enter_context(nc.Block())

        @block.sync
        def _(sp):
            sp.dma_start(g.X[:, :, :], dram.x.rearrange("b (t p) c -> p (b t) c", p=P)).then_inc(w.sem_x, 16)
            for dst, src, sem in w.loads:
                sp.dma_start(dst, src).then_inc(sem, 16)
            sp.wait_ge(w.sem_x, 16)
            sp.wait_ge(w.sem_small, 16 * w.small_count)

        @block.gpsimd
        def _(pool):
            pool.memset(g.ident[:, :], 0.0)
            pool.memset(g.identh[:, :], 0.0)
            pool.memset(g.causal[:, :], 0.0)
            pool.memset(g.ones[:, :], 1.0)
            pool.memset(g.sel_head[:, :, :], 1.0)
            pool.memset(g.sel_pair[:, :, :], 1.0)
            for part in g.sel_part:
                pool.memset(part[:, :, :], 1.0)
            pool.memset(g.minus_half[:, :], -0.5)
            pool.memset(g.minus_round[:, :], -ROUND)
            pool.memset(g.negmax4[:, :, :, :], 0.0)
            for hm in g.head_mask.values():
                last = pool.memset(hm[:, :], 1.0)
            last.then_inc(s.zeroed, 1)
            pool.wait_ge(s.zeroed, 1)

            count = [0]

            def keep(view, cmp, fill, base, pattern, mult):
                pool.affine_select(out=view, in_=view, compare_op=cmp, fill=fill, base=base, pattern=pattern,
                                   channel_multiplier=mult).then_inc(s.built, 1)
                count[0] += 1
                pool.wait_ge(s.built, count[0])

            for ident in (g.ident, g.identh):
                keep(ident[:, :], ALU.not_equal, 1.0, 0, [[-1, P]], 1)
            keep(g.causal[:, :], ALU.is_ge, MASKED, 0, [[-1, P]], 1)
            keep(g.sel_head[:, :, :].rearrange("p (g j) k -> p g j k", g=G), ALU.is_equal, 0.0, 0,
                 [[-HG, G], [-(SLOT + 1), HG], [0, P]], 1)
            keep(g.sel_pair[:, :, :].rearrange("p j (i k) -> p j i k", i=2), ALU.is_equal, 0.0, 0,
                 [[-2, PAIRS], [-1, 2], [0, TC]], 1)
            for part in range(3):
                view = g.sel_part[part][:, :, :].rearrange("p j (i k) -> p j i k", i=2)
                keep(view, ALU.is_equal, 0.0, -16 * part, [[-2, PAIRS], [-1, 2], [0, 64]], 1)
            for D, hm in g.head_mask.items():
                keep(hm[:, :], ALU.is_ge, 0.0, 0, [[-D, P // D]], 1)
                keep(hm[:, :], ALU.is_ge, 0.0, D - 1, [[D, P // D]], -1)
            pool.tensor_tensor(out=g.slot_mask[:, :], in0=g.head_mask[SLOT][:, 0:2], in1=g.head_mask[SLOT][:, 2:4],
                               op=ALU.add)
            pool.tensor_tensor(out=g.sel_part[0][:, :, :], in0=g.sel_part[0][:, :, :], in1=g.sel_part[1][:, :, :],
                               op=ALU.add).then_inc(s.built, 1)
            pool.wait_ge(s.built, count[0] + 1)
            pool.tensor_tensor(out=g.sel_expert[:, :, :], in0=g.sel_part[0][0:48, :, :], in1=g.sel_part[2][0:48, :, :],
                               op=ALU.add).then_inc(s.built, 1)


def load_later(block, cfg):
    if cfg.loads:
        @block.sync
        def _(sp):
            for dst, src, sem in cfg.loads:
                sp.dma_start(dst, src).then_inc(sem, 16)


def normalise_context(nc, g, w, v):
    n = B * TC // P
    with ExitStack() as ctx:
        s = sem_space(nc, ctx, "context", "stats mean veps rstd norm full done")
        raw, st, mv, ve, rs = g.ctx_tok, g.ctx_stats, g.ctx_mv, g.ctx_veps, g.ctx_rstd
        block = ctx.enter_context(nc.Block())

        @block.vector
        def _(dve):
            dve.wait_ge(w.sem_ctx, 32)
            for t in range(n):
                dve.bn_stats(st[:, t, :], raw[:, t, :]).then_inc(s.stats, 1)
            dve.wait_ge(s.stats, n)
            for t in range(n):
                dve.bn_aggr(mv[:, t, :], st[:, t, :]).then_inc(s.mean, 1)
            dve.wait_ge(s.rstd, 1)
            for t in range(n):
                dve.tensor_scalar(raw[:, t, :], raw[:, t, :], mv[:, t, 0:1], rs[:, t:t + 1], ALU.subtract, ALU.mult
                                  ).then_inc(s.norm, 1)

        @block.gpsimd
        def _(pool):
            pool.wait_ge(s.mean, n)
            pool.tensor_scalar(ve[:, :], mv[:, :, 1], EPS, None, ALU.add).then_inc(s.veps, 1)
            pool.wait_ge(s.veps, 1)
            pool.memset(g.ctx_half[:, :], -0.5).then_inc(s.veps, 1)
            pool.wait_ge(s.veps, 2)
            pool.tensor_tensor(out=rs[:, :], in0=ve[:, :], in1=g.ctx_half[:, :], op=ALU.pow).then_inc(s.rstd, 1)

        @block.tensor
        def _(pe):
            pe.wait_ge(s.norm, n)
            for t in range(n):
                mm = pe.transpose(g.bank[t // 4][0:CC, (t % 4) * P:(t % 4 + 1) * P], raw[:, t, :], g.ident[:, :])
                if t % 4 == 3:
                    mm.then_inc(s.full, 1)

        @block.scalar
        def _(act):
            for k in range(n // 4):
                act.wait_ge(s.full, k + 1)
                act.activation(g.ctxnT[:, k * 4 * NT:(k + 1) * 4 * NT, :],
                               g.bank[k][0:CC, :].rearrange("p (b k) -> p b k", k=TC),
                               ACT.Identity, scale=v.ctx_gain, bias=v.ctx_shift).then_inc(s.done, 1)


def ternary_weights(nc, g, name, w, sem, value, pairs, mode):
    with ExitStack() as ctx:
        s = sem_space(nc, ctx, name, "sums total mean recip scaled rounded clipped")
        block = ctx.enter_context(nc.Block())
        k = len(pairs)

        @block.vector
        def _(dve):
            dve.wait_ge(sem, value)
            for i, (src, _dst, _level) in enumerate(pairs):
                dve.tensor_reduce(g.tern_sum[:, i:i + 1], src, AX_X, ALU.add, apply_absolute_value=True
                                  ).then_inc(s.sums, 1)
            dve.wait_ge(s.total, 1)
            scale = 1.0 / (C * 512)
            for i, (_src, _dst, level) in enumerate(pairs):
                dve.tensor_scalar(level, g.bank[0][:, i:i + 1], scale, EPS, ALU.mult,
                                  ALU.add if mode == "added" else ALU.max).then_inc(s.mean, 1)
            dve.wait_ge(s.mean, k)
            for i, (_src, _dst, level) in enumerate(pairs):
                dve.reciprocal(g.tern_recip[:, i:i + 1], level).then_inc(s.recip, 1)
            dve.wait_ge(s.recip, k)
            for i, (src, _dst, _level) in enumerate(pairs):
                dve.tensor_scalar(src, src, g.tern_recip[:, i:i + 1], ROUND, ALU.mult, ALU.add).then_inc(s.scaled, 1)
            dve.wait_ge(s.scaled, k)
            for src, _dst, _level in pairs:
                dve.tensor_scalar(src, src, ROUND, 1.0, ALU.subtract, ALU.min).then_inc(s.rounded, 1)
            dve.wait_ge(s.rounded, k)
            for src, dst, _level in pairs:
                dve.tensor_scalar(dst, src, -1.0, None, ALU.max).then_inc(s.clipped, 1)

        @block.tensor
        def _(pe):
            pe.wait_ge(s.sums, k)
            pe.matmul(g.bank[0][:, 0:k], g.ones[:, :], g.tern_sum[:, 0:k], start=True, stop=True).then_inc(s.total, 1)


ROWS = ["L0_xattn_bv", "L0_xattn_bcv", "L0_xattn_bp", "L1_xattn_ln1_g", "L1_xattn_ln1_b", "L1_xattn_ln2_g",
        "L1_xattn_ln2_b", "L1_xattn_a1_li1_b", "L1_xattn_a1_li3_b", "L1_xattn_a2_li1_b", "L1_xattn_a2_li3_b",
        "L1_ffn_b2", "L2_ffn_ln1_g", "L2_ffn_ln1_b", "L2_ffn_b1", "L2_ffn_ln2_g", "L2_ffn_ln2_b", "L2_ffn_b2",
        "L3_xattn_bo"]


def build(nc, dram, cols, rows):
    with ExitStack() as ctx:
        def sb(name, shape, dt=F32):
            return ctx.enter_context(nc.sbuf_tensor(name, shape, dt))

        def sem(name):
            return ctx.enter_context(nc.semaphore(name))

        def two(name, shape, dt=F32):
            return [sb(f"{name}{p}", shape, dt) for p in range(2)]

        g = Store()
        g.X, g.A, g.XA = (sb(n, [P, B * NT, C]) for n in ("X", "A", "XA"))
        g.xn, g.xT, g.yT, g.resb = two("xn", [P, NT, C]), two("xT", [P, T]), two("yT", [P, T]), two("resb", [P, NT, C])
        g.qT, g.qh = two("qT", [P, 8 * T]), two("qh", [P, 8 * T], BF16)
        g.kT, g.kh = two("kT", [P, G * T]), two("kh", [P, G * T], BF16)
        g.V = two("V", [P, NT * H * (SLOT + 1)])
        g.kmask, g.kmaskh = g.kT, g.kh
        g.ctxb = two("ctxb", [CC, 2, TC])
        g.osb = sb("osb", [P, NT * H * 64])
        g.prob = [sb(f"prob{i}", [P, 512]) for i in range(3)] + [g.osb[:, 0:512]]
        g.probsum, g.rec = [sb(f"probsum{i}", [P, T]) for i in range(3)] + [g.osb[:, 512:512 + T]], sb("rec", [P, T])
        g.probm = [sb(f"probm{i}", [P, NT, P]) for i in range(3)]
        g.probm.append(g.osb[:, 1024:1024 + T].rearrange("p (t q) -> p t q", t=NT))
        g.silu = [g.yT[0], g.yT[1], g.xT[0]]
        g.oT = sb("oT", [P, 8 * T])
        g.negmax, g.negmax4 = sb("negmax", [P, NT, H]), sb("negmax4", [P, NT, 4, SLOT], BF16)
        g.negmaxT = two("negmaxT", [P, T], BF16)
        g.recip16 = sb("recip16", [P, NT, H])
        g.stats = [sb(f"stats{k}", [P, NT, 6]) for k in range(3)]
        g.mv = [sb(f"mv{k}", [P, NT, 2]) for k in range(3)]
        g.veps = [sb(f"veps{k}", [P, NT]) for k in range(3)]
        g.rstd = [sb(f"rstd{k}", [P, NT]) for k in range(3)]
        g.mvh, g.rstdh = sb("mvh", [P, NT, 2]), sb("rstdh", [P, NT])
        g.ident, g.identh = sb("ident", [P, P]), sb("identh", [P, P], BF16)
        g.causal, g.ones = sb("causal", [P, P], BF16), sb("ones", [P, P])
        g.sel_head, g.sel_pair = sb("sel_head", [P, H, P], BF16), sb("sel_pair", [P, PAIRS, P], BF16)
        g.sel_part = [g.qT[0][:, :].bitcast(BF16)[:, i * PAIRS * P:(i + 1) * PAIRS * P]
                      .rearrange("p (j k) -> p j k", j=PAIRS) for i in range(3)]
        g.sel_expert = sb("sel_expert", [48, PAIRS, P], BF16)
        g.head_mask = {D: sb(f"head_mask{D}", [P, P // D]) for D in (8, 32, 64)}
        g.slot_mask, g.bias_masked = sb("slot_mask", [P, 2]), sb("bias_masked", [P, 2, G])
        g.minus_half, g.minus_round = sb("minus_half", [P, NT]), sb("minus_round", [P, 1])
        N = B * NT
        whole = lambda x, a, e: x[:, a * N:(a + e) * N].rearrange("p (t e) -> p t e", e=e)
        g.gate = record(
            e=whole(g.osb, 0, 16), w=whole(g.osb, 16, 16), rest=whole(g.osb, 32, 16), c=whole(g.osb, 48, 16),
            probs=whole(g.oT, 0, 24), marked=whole(g.oT, 24, 24), keys=whole(g.oT, 48, 8), top=whole(g.oT, 56, 8),
            part=whole(g.qh[0], 0, 48).rearrange("p t (k e) -> p t k e", k=3), nmax=sb("g_nmax", [P, N]),
            sum=sb("g_sum", [P, N]), rsum=sb("g_rsum", [P, N]), wsum=sb("g_wsum", [P, N]), wguard=sb("g_wguard", [P, N]),
            wrecip=sb("g_wrecip", [P, N]), cn=two("g_cn", [P, NT, 8]), pn=two("g_pn", [P, NT]))
        g.combT = g.qT[0][0:48, :].bitcast(BF16)
        n_ctx = B * TC // P
        g.ctx_tok, g.ctx_stats = sb("ctx_tok", [P, n_ctx, CC]), sb("ctx_stats", [P, n_ctx, 6])
        g.ctx_mv, g.ctx_veps = sb("ctx_mv", [P, n_ctx, 2]), sb("ctx_veps", [P, n_ctx])
        g.ctx_rstd, g.ctx_half = sb("ctx_rstd", [P, n_ctx]), sb("ctx_half", [P, n_ctx])
        g.ctxnT, ctxT = sb("ctxnT", [CC, B, TC]), sb("ctxT", [CC, B, TC])
        g.tern_sum, g.tern_recip = sb("tern_sum", [P, 2]), sb("tern_recip", [P, 2])
        g.bank = [ctx.enter_context(nc.psum_tensor(f"bank{i}", [P, 512], F32)) for i in range(8)]

        w = record(loads=[], sem_x=sem("x_loaded"), sem_small=sem("small_loaded"), sem_ctx=sem("ctx_loaded"),
                            small_count=2)
        row_tile = sb("row_tile", [P, dram.rows.shape[0]])
        col_tile = sb("col_tile", [P, dram.cols.shape[1]])
        w.loads.extend([(row_tile[:, :], dram.rows.partition_broadcast(P), w.sem_small), (col_tile[:, :], dram.cols, w.sem_small),
                    (ctxT[:, :, :], dram.ctxT, w.sem_ctx),
                    (g.ctx_tok[:, :, :], dram.ctx.rearrange("b k c -> (b k) c").rearrange("(n p) c -> p n c", p=P), w.sem_ctx)])

        def row(name):
            a, n = rows[name]
            return row_tile[:, a:a + n]

        def col(name, count=1):
            a, _ = cols[name]
            return col_tile[:, a:a + count]

        layer = [(sem(f"weights{i}_loaded"), [0]) for i in range(7)]
        later = {k: [] for k in range(3, 7)}

        flat = lambda x: x[:, :, :].rearrange("p t c -> p (t c)")
        first, second = sb("weights_first", [P, 5648]), sb("weights_second", [P, 3072])
        region = {0: first[:, :], 1: first[:, :], 2: second[:, :], 3: first[:, :], 4: second[:, :], 5: flat(g.A),
                  6: flat(g.XA)}
        starts = {0: 0, 2: 0, 3: 0, 4: 0, 5: 0, 6: 0}

        def weight(name, k, shape):
            src = dram.weights[name]
            start = 0 if k == 1 else k
            n = int(np.prod(shape[1:]))
            at = starts[start]
            starts[start] += n
            assert starts[start] <= region[k].shape[1], name
            view = region[k][0:shape[0], at:at + n]
            if len(shape) == 3:
                view = view.rearrange("p (k c) -> p k c", k=shape[1])
            (w.loads if k <= 2 else later[k]).append((view, src, layer[k][0]))
            layer[k][1][0] += 16
            return view

        def loaded(k, and_ctx=False):
            def wait_for(eng):
                eng.wait_ge(layer[k][0], layer[k][1][0])
                if and_ctx:
                    eng.wait_ge(w.sem_ctx, 32)
            return wait_for

        W = record(
            q0=weight("L0_q", 0, [P, G * P]), k0=weight("L0_k", 0, [P, G * P]), v0=weight("L0_v", 0, [P, P]),
            cq0=weight("L0_cq", 0, [P, P]), ck0=weight("L0_ck", 0, [CC, P]), cv0=weight("L0_cv", 0, [CC, P]),
            p0=weight("L0_p", 0, [P, 1, C]), ps0=weight("L0_ps", 0, [P, G, C]),
            gate0=weight("L0_gate", 1, [P, 16]), w10=weight("L0_w1", 1, [P, 1024]), w30=weight("L0_w3", 1, [P, 1024]),
            w20=weight("L0_w2", 1, [P, 8, C]), sw1=weight("L0_sw1", 1, [P, 64]), sw3=weight("L0_sw3", 1, [P, 64]),
            sw2=weight("L0_sw2", 1, [64, C]),
            q1=weight("L1_q1", 2, [P, 512]), k1=weight("L1_k1", 2, [P, 512]), v1=weight("L1_v1", 2, [P, 512]),
            o1=weight("L1_o1", 2, [P, 4, C]), f1=weight("L1_f1", 2, [P, 512]), e1=weight("L1_e1", 2, [P, 4, C]),
            q2=weight("L1_q2", 3, [P, 512]), k2=weight("L1_k2", 3, [CC, 512]), v2=weight("L1_v2", 3, [CC, 512]),
            o2=weight("L1_o2", 3, [P, 4, C]), f2=weight("L1_f2", 3, [P, 512]), e2=weight("L1_e2", 3, [P, 4, C]),
            t1=weight("L1_w1", 3, [P, 512]), t2=weight("L1_w2", 3, [P, 4, C]),
            l2q=weight("L2_q", 4, [P, P]), l2k=weight("L2_k", 4, [CC, P]), l2v=weight("L2_v", 4, [CC, P]),
            l2o=weight("L2_o", 4, [P, 1, C]), l2w1=weight("L2_w1", 4, [P, 512]), l2w2=weight("L2_w2", 4, [P, 4, C]),
            q3=weight("L3_q", 5, [P, 1024]), k3=weight("L3_k", 5, [CC, 1024]), v3=weight("L3_v", 5, [CC, 1024]),
            o3=weight("L3_o", 5, [P, 8, C]), gate3=weight("L3_gate", 6, [P, 8]), w3=weight("L3_w", 6, [P, 8 * C]))
        w1q, w2q = sb("w1q", [P, 512], BF16), sb("w2q", [P, 4, C], BF16)
        levels = sb("levels", [P, 4])
        for k in "ab":
            buf = record(peak=sb(f"peak_{k}", [P, NT]), peakc=sb(f"peakc_{k}", [P, NT]),
                                  recip=sb(f"qrecip_{k}", [P, NT]), scale=sb(f"qscale_{k}", [P, NT]),
                                  level=two(f"level_{k}", [P, NT]),
                                  wlevel=levels[:, 2:3] if k == "a" else levels[:, 3:4])
            if k == "a":
                g.quant_a = buf
            else:
                g.quant_b = buf

        plain = [(None, None, None)]
        att = dict(q_gain=None, q_shift=None, kv_gain=None, kv_shift=None, bq=None, bk=None, bv=None, bias=None,
                   wide_v=0, causal=False, norms=plain, loads=())
        prepare(nc, g, w, dram)
        self_attention(nc, g, "own0", record(**(att | dict(
            source=g.X, residual=g.X, target=g.A, D=8, scale=8 ** -0.5, causal=True, wq=W.q0, wk=W.k0, wv=W.v0, wo=W.ps0,
            bq=col("bq", 4), bk=col("bk", 4), bv=row("L0_xattn_bv"), bias=row("L0_xattn_bp"), loaded=loaded(0)))))
        cross_attention(nc, g, "ctx0", record(**(att | dict(
            source=g.X, residual=g.A, target=g.A, D=8, scale=8 ** -0.5, ctxT=ctxT, wq=W.cq0, wk=W.ck0, wv=W.cv0, wo=W.p0,
            bq=col("bcq"), bk=col("bck"), bv=row("L0_xattn_bcv"), head_mask=g.head_mask[8], loaded=loaded(0, True)))))
        moe0 = dict(experts=16, xT=flat(g.XA), loaded=loaded(1))
        route(nc, g, "route0", record(**moe0, source=g.A, top=4, guard=0.0, gate_w=W.gate0, parts=True))
        gated_experts(nc, g, "moe0", record(**moe0, residual=g.A, target=g.X, w1=W.w10, w3=W.w30, w2=W.w20,
                                            sw1=W.sw1, sw3=W.sw3, sw2=W.sw2))
        a1, a2 = "L1_xattn_a1_", "L1_xattn_a2_"
        self_attention(nc, g, "own1", record(**(att | dict(
            source=g.X, residual=g.XA, target=g.A, D=32, scale=32 ** -0.5, wide_v=1,
            norms=[(None, None, None), (row("L1_xattn_ln1_g"), row("L1_xattn_ln1_b"), g.XA), (None, None, None)],
            wq=W.q1, wk=W.k1, wv=W.v1, wo=W.o1, q_gain=col(a1 + "lnx_g"), q_shift=col(a1 + "lnx_b"),
            kv_gain=col(a1 + "lny_g"), kv_shift=col(a1 + "lny_b"), bias=row(a1 + "li1_b"), loaded=loaded(2), loads=later[3]))))
        feed_forward(nc, g, "net1", record(
            source=g.A, norms=plain, residuals=[g.A, g.XA], target=g.A, relu=False, x_gain=col(a1 + "ln3_g"),
            x_shift=col(a1 + "ln3_b"), w1=W.f1, b1=col(a1 + "li2_b", 4), w2=W.e1, bias=row(a1 + "li3_b"), loaded=loaded(2), loads=()))
        normalise_context(nc, g, w, record(ctx_gain=col(a2 + "lny_g")[0:CC, :], ctx_shift=col(a2 + "lny_b")[0:CC, :]))
        cross_attention(nc, g, "ctx1", record(**(att | dict(
            source=g.A, residual=g.XA, target=g.A, D=32, scale=32 ** -0.5, ctxT=g.ctxnT,
            norms=[(row("L1_xattn_ln2_g"), row("L1_xattn_ln2_b"), g.XA), (None, None, None)],
            wq=W.q2, wk=W.k2, wv=W.v2, wo=W.o2, q_gain=col(a2 + "lnx_g"), q_shift=col(a2 + "lnx_b"),
            bias=row(a2 + "li1_b"), head_mask=g.head_mask[32], loaded=loaded(3), loads=later[4]))))
        feed_forward(nc, g, "net2", record(
            source=g.A, norms=plain, residuals=[g.A, g.XA, g.X], target=g.X, relu=False, x_gain=col(a2 + "ln3_g"),
            x_shift=col(a2 + "ln3_b"), w1=W.f2, b1=col(a2 + "li2_b", 4), w2=W.e2, bias=row(a2 + "li3_b"), loaded=loaded(3), loads=()))
        ternary_weights(nc, g, "tern1", w, layer[3][0], layer[3][1][0],
                        [(W.t1[:, :], W.t1[:, :], levels[:, 0:1]),
                         (W.t2[:, :, :].rearrange("p k c -> p (k c)"), W.t2[:, :, :].rearrange("p k c -> p (k c)"),
                          levels[:, 1:2])], "added")
        feed_forward(nc, g, "net3", record(
            source=g.X, norms=plain, residuals=[g.X], target=g.X, relu=True, x_gain=None, x_shift=None,
            w1=W.t1, b1=col("L1_ffn_b1", 4), w2=W.t2, bias=row("L1_ffn_b2"), loaded=loaded(3), loads=later[5] + later[6]))
        cross_attention(nc, g, "ctx2", record(**(att | dict(
            source=g.X, residual=g.X, target=g.X, D=8, scale=8 ** -0.5, ctxT=ctxT, wq=W.l2q, wk=W.l2k, wv=W.l2v,
            wo=W.l2o, head_mask=g.head_mask[8], loaded=loaded(4)))))
        ternary_weights(nc, g, "tern2", w, layer[4][0], layer[4][1][0],
                        [(W.l2w1[:, :], w1q[:, :], levels[:, 2:3]),
                         (W.l2w2[:, :, :].rearrange("p k c -> p (k c)"), w2q[:, :, :].rearrange("p k c -> p (k c)"),
                          levels[:, 3:4])], "clipped")
        quantised_feed_forward(nc, g, "net4", record(
            source=g.X, residual=g.X, target=g.X, norms=[(None, None, None), (row("L2_ffn_ln1_g"), row("L2_ffn_ln1_b"), None)],
            w1=w1q, b1=row("L2_ffn_b1"), gain2=row("L2_ffn_ln2_g"), shift2=row("L2_ffn_ln2_b"), w2=w2q,
            bias=row("L2_ffn_b2"), loads=()))
        cross_attention(nc, g, "ctx3", record(**(att | dict(
            source=g.X, residual=g.X, target=g.X, D=64, scale=64 ** -0.5, ctxT=ctxT, wq=W.q3, wk=W.k3, wv=W.v3,
            wo=W.o3, bias=row("L3_xattn_bo"), head_mask=g.head_mask[64], loaded=loaded(5)))))
        moe3 = dict(experts=8, xT=flat(g.A), loaded=loaded(6))
        route(nc, g, "route3", record(**moe3, source=g.X, top=2, guard=1e-6, gate_w=W.gate3, parts=False))
        routed_experts(nc, g, "moe3", record(**moe3, residual=g.X, target=g.X, w=W.w3), dram.out)


def kernel(**inputs):
    import concourse.bacc as bacc
    from concourse.bass_utils import run_bass_kernel_spmd

    v = {k: np.asarray(a) for k, a in inputs.items()}

    def slots(a):
        out = np.zeros((*a.shape[:-1], G, HG, SLOT), a.dtype)
        out[..., 0:8] = a.reshape(*a.shape[:-1], G, HG, 8)
        return out.reshape(*a.shape[:-1], G * P)

    def heads(a):
        return a.transpose(1, 0, 2).reshape(a.shape[1], -1)

    def tiles(a):
        return a.reshape(-1, P, a.shape[-1]).transpose(1, 0, 2)

    a1, a2 = "L1_xattn_a1_", "L1_xattn_a2_"
    weights = {
        "L0_q": slots(v["L0_xattn_Wq"]), "L0_k": slots(v["L0_xattn_Wk"]), "L0_v": v["L0_xattn_Wv"],
        "L0_cq": v["L0_xattn_Wcq"], "L0_ck": v["L0_xattn_Wck"], "L0_cv": v["L0_xattn_Wcv"],
        "L0_p": tiles(v["L0_xattn_Wp"]), "L0_ps": tiles(slots(v["L0_xattn_Wp"].T).T), "L0_gate": v["L0_ffn_gate_w"].T,
        "L0_w1": v["L0_ffn_w1"].reshape(1024, C).T, "L0_w3": v["L0_ffn_w3"].reshape(1024, C).T,
        "L0_w2": tiles(v["L0_ffn_w2"].transpose(0, 2, 1).reshape(1024, C)),
        "L0_sw1": v["L0_ffn_sw1"].T, "L0_sw3": v["L0_ffn_sw3"].T, "L0_sw2": v["L0_ffn_sw2"].T,
        "L1_q1": heads(v[a1 + "wq"]), "L1_k1": heads(v[a1 + "wk"]), "L1_v1": heads(v[a1 + "wv"]),
        "L1_o1": tiles(v[a1 + "li1_w"]), "L1_f1": v[a1 + "li2_w"], "L1_e1": tiles(v[a1 + "li3_w"]),
        "L1_q2": heads(v[a2 + "wq"]), "L1_k2": heads(v[a2 + "wk"]), "L1_v2": heads(v[a2 + "wv"]),
        "L1_o2": tiles(v[a2 + "li1_w"]), "L1_f2": v[a2 + "li2_w"], "L1_e2": tiles(v[a2 + "li3_w"]),
        "L1_w1": v["L1_ffn_W1"].T, "L1_w2": tiles(v["L1_ffn_W2"].T),
        "L2_q": v["L2_xattn_Wq"].T, "L2_k": v["L2_xattn_Wkv"][0:P].T, "L2_v": v["L2_xattn_Wkv"][P:2 * P].T,
        "L2_o": tiles(v["L2_xattn_Wo"].T), "L2_w1": v["L2_ffn_w1"].T, "L2_w2": tiles(v["L2_ffn_w2"].T),
        "L3_q": v["L3_xattn_Wq"], "L3_k": v["L3_xattn_Wk"], "L3_v": v["L3_xattn_Wv"], "L3_o": tiles(v["L3_xattn_Wo"]),
        "L3_gate": v["L3_ffn_router_w"].T, "L3_w": v["L3_ffn_expert_weights"].transpose(1, 0, 2).reshape(P, 8 * C),
    }
    columns = {"bq": slots(v["L0_xattn_bq"]).reshape(G, P).T, "bk": slots(v["L0_xattn_bk"]).reshape(G, P).T,
               "bcq": v["L0_xattn_bcq"][:, None], "bck": v["L0_xattn_bck"][:, None],
               "L1_ffn_b1": v["L1_ffn_b1"].reshape(4, P).T}
    for a in (a1, a2):
        for n in ("lnx_g", "lnx_b", "lny_g", "lny_b", "ln3_g", "ln3_b"):
            x = v[a + n]
            columns[a + n] = np.concatenate([x, np.zeros(P - len(x), x.dtype)])[:, None]
        columns[a + "li2_b"] = v[a + "li2_b"].reshape(4, P).T
    cols, rows, at = {}, {}, 0
    for n, x in columns.items():
        cols[n] = (at, x.shape[1])
        at += x.shape[1]
    at = 0
    for n in ROWS:
        rows[n] = (at, v[n].shape[0])
        at += v[n].shape[0]

    nc = bacc.Bacc("TRN2", target_bir_lowering=False, num_devices=1)
    arrays = {}

    def feed(name, a):
        a = np.ascontiguousarray(a)
        arrays["in_" + name] = a
        return nc.dram_tensor("in_" + name, a.shape, mybir.dt.from_np(a.dtype), kind="ExternalInput").ap()

    dram = record(
        x=feed("x", v["x"]), ctx=feed("ctx", v["ctx_512"]), ctxT=feed("ctxT", v["ctx_512"].transpose(2, 0, 1)),
        cols=feed("cols", np.concatenate(list(columns.values()), axis=1)),
        rows=feed("rows", np.concatenate([v[n] for n in ROWS])),
        weights={n: feed(n, a) for n, a in weights.items()},
        out=nc.dram_tensor("out_x", (B, T, C), F32, kind="ExternalOutput").ap())
    build(nc, dram, cols, rows)
    r = run_bass_kernel_spmd(nc, [arrays], core_ids=[0])
    return r.results[0]["out_x"]
```
